# Optimizing a Trainium2 kernel written in Bass

```python
import numpy as np
import jax
import jax.numpy as jnp

def _softmax(x, axis=-1):
    return jax.nn.softmax(x, axis=axis)

def _gelu(x):
    return jax.nn.gelu(x, approximate=True)

def _silu(x):
    return jax.nn.silu(x)

def _sigmoid(x):
    return jax.nn.sigmoid(x)

def _layernorm(x, axis=-1, eps=1e-05):
    m = jnp.mean(x, axis=axis, keepdims=True)
    v = jnp.var(x, axis=axis, keepdims=True)
    return (x - m) / jnp.sqrt(v + eps)

def _scatter_add(tgt, idx, src, axis=0):
    return tgt.at[idx].add(src)

def _segment_sum(src, seg, n):
    return jax.ops.segment_sum(src, seg, n)
kernel_name = 'mk_vit_tower_cls_d2_tok_img768_r4_f3ec01'

def setup_inputs(seed: int=0):
    np.random.seed(seed)
    _w = jnp.asarray

    def _rec_inputs():
        import jax
        import jax.numpy as jnp
        _rk = jax.random.key(seed)
        x = -0.00016672 + 0.999947 * jax.random.normal(jax.random.fold_in(_rk, 1), (16, 3, 96, 96), jnp.float32)
        cls_tok = 0.02 * jax.random.normal(jax.random.fold_in(_rk, 5), (1, 1, 192), jnp.float32)
        return (x, cls_tok)
    x, cls_tok = _rec_inputs()

    def _L0_tok_setup():
        import jax, jax.numpy as jnp
        import numpy as np
        PH = PW = 16
        C, H, W = (3, 96, 96)
        EMBED = 192
        PATCH_DIM = C * PH * PW
        key = jax.random.key(seed)
        k1, k2, k3 = jax.random.split(key, 3)
        x = jax.random.normal(k1, (64, C, H, W), dtype=jnp.float32)
        bound = 1.0 / np.sqrt(PATCH_DIM)
        W_proj = jax.random.uniform(k2, (EMBED, PATCH_DIM), minval=-bound, maxval=bound, dtype=jnp.float32)
        b_proj = jax.random.uniform(k3, (EMBED,), minval=-bound, maxval=bound, dtype=jnp.float32)
        return {'x': x, 'W_proj': W_proj, 'b_projb'[:6]: b_proj}
    _L0_tok_all = _L0_tok_setup()
    _L0_tok_in = {k: v for k, v in _L0_tok_all.items() if k in ('W_proj', 'b_proj')}
    del _L0_tok_all

    def _L0_attn_setup():
        import jax, jax.numpy as jnp
        import numpy as np
        B, N, C = (2, 1024, 192)
        H = 12
        HD = C // H
        THETA = 10000.0

        def _rope_tables(n, hd, dtype):
            inv = 1.0 / THETA ** (jnp.arange(0, hd, 2, dtype=jnp.float32) / hd)
            freqs = jnp.arange(n, dtype=jnp.float32)[:, None] * inv[None, :]
            cos = jnp.concatenate([jnp.cos(freqs), jnp.cos(freqs)], axis=-1).astype(dtype)
            sin = jnp.concatenate([jnp.sin(freqs), jnp.sin(freqs)], axis=-1).astype(dtype)
            return (cos, sin)

        def _rotate_half(x):
            x1, x2 = (x[..., :x.shape[-1] // 2], x[..., x.shape[-1] // 2:])
            return jnp.concatenate([-x2, x1], axis=-1)
        key = jax.random.key(seed)
        k1, k2, k3 = jax.random.split(key, 3)
        x = jax.random.normal(k1, (B, N, C), dtype=jnp.float32)
        w_qkv = jax.random.normal(k2, (3 * C, C), dtype=jnp.float32) * C ** (-0.5)
        b_qkv = jnp.zeros((3 * C,), dtype=jnp.float32)
        w_proj = jax.random.normal(k3, (C, C), dtype=jnp.float32) * C ** (-0.5)
        b_proj = jnp.zeros((C,), dtype=jnp.float32)
        return {'x': x, 'w_qkv': w_qkv, 'b_qkv': b_qkv, 'w_proj': w_proj, 'b_proj': b_proj}
    _L0_attn_all = _L0_attn_setup()
    _L0_attn_in = {k: v for k, v in _L0_attn_all.items() if k in ('w_qkv', 'b_qkv', 'w_proj', 'b_proj')}
    del _L0_attn_all

    def _L0_ffn_setup():
        import jax, jax.numpy as jnp
        import numpy as np
        B, N, C, H, E = (8, 256, 192, 768, 4)
        key = jax.random.key(seed)
        ks = jax.random.split(key, 8)
        s_in = 1.0 / np.sqrt(C)
        s_h = 1.0 / np.sqrt(H)
        return {'x': jax.random.normal(ks[0], (B, N, C), dtype=jnp.float32), 'gate_w': jax.random.normal(ks[1], (C, E), dtype=jnp.float32) * 0.01, 'gate_b': jnp.zeros((E,), dtype=jnp.float32), 'gate_center': jnp.zeros((E,), dtype=jnp.float32), 'w1': jax.random.uniform(ks[2], (E, C, H), jnp.float32, -s_in, s_in), 'b1': jax.random.uniform(ks[3], (E, H), jnp.float32, -s_in, s_in), 'w2': jax.random.uniform(ks[4], (E, H, C), jnp.float32, -s_h, s_h), 'b2': jax.random.uniform(ks[5], (E, C), jnp.float32, -s_h, s_h)}
    _L0_ffn_all = _L0_ffn_setup()
    _L0_ffn_in = {k: v for k, v in _L0_ffn_all.items() if k in ('gate_w', 'gate_b', 'gate_center', 'w1', 'b1', 'w2', 'b2')}
    del _L0_ffn_all

    def _L1_attn_setup():
        import jax, jax.numpy as jnp
        import numpy as np
        HALF_WIN = 6

        def _local_attn(x, w_qkv, w_proj, b_proj, num_heads=12):
            B, N, C = x.shape
            H = num_heads
            D = C // H
            W = 2 * HALF_WIN + 1
            qkv = (x @ w_qkv).reshape(B, N, 3, H, D)
            q, k, v = (qkv[:, :, 0], qkv[:, :, 1], qkv[:, :, 2])
            offs = jnp.arange(-HALF_WIN, HALF_WIN + 1)
            idx = jnp.arange(N)[:, None] + offs[None, :]
            valid = (idx >= 0) & (idx < N)
            idxc = jnp.clip(idx, 0, N - 1)
            k_win = k[:, idxc]
            v_win = v[:, idxc]
            scale = D ** (-0.5)
            scores = jnp.einsum('bnhd,bnwhd->bnhw', q, k_win) * scale
            neg = jnp.asarray(jnp.finfo(scores.dtype).min, scores.dtype)
            scores = jnp.where(valid[None, :, None, :], scores, neg)
            p = jax.nn.softmax(scores, axis=-1)
            out = jnp.einsum('bnhw,bnwhd->bnhd', p, v_win)
            out = out.reshape(B, N, C)
            return out @ w_proj + b_proj
        key = jax.random.key(seed)
        k1, k2, k3 = jax.random.split(key, 3)
        B, N, C = (2, 1024, 192)
        x = jax.random.normal(k1, (B, N, C), dtype=jnp.float32)
        s = 1.0 / np.sqrt(C)
        w_qkv = jax.random.uniform(k2, (C, 3 * C), jnp.float32, -s, s)
        w_proj = jax.random.uniform(k3, (C, C), jnp.float32, -s, s)
        b_proj = jnp.zeros((C,), jnp.float32)
        return {'x': x, 'w_qkv': w_qkv, 'w_proj': w_proj, 'b_proj': b_proj}
    _L1_attn_all = _L1_attn_setup()
    _L1_attn_in = {k: v for k, v in _L1_attn_all.items() if k in ('w_qkv', 'w_proj', 'b_proj')}
    del _L1_attn_all

    def _L1_ffn_setup():
        import jax, jax.numpy as jnp
        import numpy as np
        B, S, H = (2, 256, 192)
        E, K, I = (16, 4, 192)
        ALPHA, LIMIT, EPS = (1.702, 7.0, 1e-05)

        def _swiglu(h):
            x_glu, x_lin = jnp.split(h, 2, axis=-1)
            x_glu = jnp.minimum(x_glu, LIMIT)
            x_lin = jnp.clip(x_lin, -LIMIT, LIMIT)
            return x_glu * jax.nn.sigmoid(ALPHA * x_glu) * (x_lin + 1.0)
        key = jax.random.key(seed)
        ks = jax.random.split(key, 7)
        x = jax.random.normal(ks[0], (B, S, H), dtype=jnp.float32)
        scale = jnp.ones((H,), jnp.float32)
        gate_w = jax.random.normal(ks[1], (E, H), jnp.float32) * 0.02
        gate_b = jnp.zeros((E,), jnp.float32)
        w1 = jax.random.normal(ks[2], (E, H, 2 * I), jnp.float32) * 0.02
        b1 = jax.random.normal(ks[3], (E, 2 * I), jnp.float32) * 0.02
        w2 = jax.random.normal(ks[4], (E, I, H), jnp.float32) * 0.02
        b2 = jax.random.normal(ks[5], (E, H), jnp.float32) * 0.02
        return {'x': x, 'scale': scale, 'gate_w': gate_w, 'gate_b': gate_b, 'w1': w1, 'b1': b1, 'w2': w2, 'b2': b2}
    _L1_ffn_all = _L1_ffn_setup()
    _L1_ffn_in = {k: v for k, v in _L1_ffn_all.items() if k in ('scale', 'gate_w', 'gate_b', 'w1', 'b1', 'w2', 'b2')}
    del _L1_ffn_all
    return {'x': x, 'cls_tok': cls_tok, 'L0_tok_W_proj': _L0_tok_in['W_proj'], 'L0_tok_b_proj': _L0_tok_in['b_proj'], 'L0_attn_w_qkv': _L0_attn_in['w_qkv'], 'L0_attn_b_qkv': _L0_attn_in['b_qkv'], 'L0_attn_w_proj': _L0_attn_in['w_proj'], 'L0_attn_b_proj': _L0_attn_in['b_proj'], 'L0_ffn_gate_w': _L0_ffn_in['gate_w'], 'L0_ffn_gate_b': _L0_ffn_in['gate_b'], 'L0_ffn_gate_center': _L0_ffn_in['gate_center'], 'L0_ffn_w1': _L0_ffn_in['w1'], 'L0_ffn_b1': _L0_ffn_in['b1'], 'L0_ffn_w2': _L0_ffn_in['w2'], 'L0_ffn_b2': _L0_ffn_in['b2'], 'L1_attn_w_qkv': _L1_attn_in['w_qkv'], 'L1_attn_w_proj': _L1_attn_in['w_proj'], 'L1_attn_b_proj': _L1_attn_in['b_proj'], 'L1_ffn_scale': _L1_ffn_in['scale'], 'L1_ffn_gate_w': _L1_ffn_in['gate_w'], 'L1_ffn_gate_b': _L1_ffn_in['gate_b'], 'L1_ffn_w1': _L1_ffn_in['w1'], 'L1_ffn_b1': _L1_ffn_in['b1'], 'L1_ffn_w2': _L1_ffn_in['w2'], 'L1_ffn_b2': _L1_ffn_in['b2']}

def reference(x, cls_tok, L0_tok_W_proj, L0_tok_b_proj, L0_attn_w_qkv, L0_attn_b_qkv, L0_attn_w_proj, L0_attn_b_proj, L0_ffn_gate_w, L0_ffn_gate_b, L0_ffn_gate_center, L0_ffn_w1, L0_ffn_b1, L0_ffn_w2, L0_ffn_b2, L1_attn_w_qkv, L1_attn_w_proj, L1_attn_b_proj, L1_ffn_scale, L1_ffn_gate_w, L1_ffn_gate_b, L1_ffn_w1, L1_ffn_b1, L1_ffn_w2, L1_ffn_b2):
    import jax
    import jax.numpy as jnp

    def _L0_tok_ref(x, W_proj, b_proj):
        import jax, jax.numpy as jnp
        import numpy as np
        PH = PW = 16
        C, H, W = (3, 96, 96)
        EMBED = 192
        PATCH_DIM = C * PH * PW
        B = x.shape[0]
        Hn, Wn = (H // PH, W // PW)
        patches = x.reshape(B, C, Hn, PH, Wn, PW).transpose(0, 2, 4, 1, 3, 5)
        patches = patches.reshape(B, Hn * Wn, PATCH_DIM)
        return jnp.einsum('bnd,ed->bne', patches, W_proj) + b_proj

    def _L0_attn_ref(x, w_qkv, b_qkv, w_proj, b_proj):
        import jax, jax.numpy as jnp
        import numpy as np
        B, N, C = (2, 1024, 192)
        H = 12
        HD = C // H
        THETA = 10000.0

        def _rope_tables(n, hd, dtype):
            inv = 1.0 / THETA ** (jnp.arange(0, hd, 2, dtype=jnp.float32) / hd)
            freqs = jnp.arange(n, dtype=jnp.float32)[:, None] * inv[None, :]
            cos = jnp.concatenate([jnp.cos(freqs), jnp.cos(freqs)], axis=-1).astype(dtype)
            sin = jnp.concatenate([jnp.sin(freqs), jnp.sin(freqs)], axis=-1).astype(dtype)
            return (cos, sin)

        def _rotate_half(x):
            x1, x2 = (x[..., :x.shape[-1] // 2], x[..., x.shape[-1] // 2:])
            return jnp.concatenate([-x2, x1], axis=-1)
        b, n, c = x.shape
        scale = HD ** (-0.5)
        qkv = jnp.einsum('bnc,dc->bnd', x, w_qkv) + b_qkv
        qkv = qkv.reshape(b, n, 3, H, HD).transpose(2, 0, 3, 1, 4)
        q, k, v = (qkv[0], qkv[1], qkv[2])
        cos, sin = _rope_tables(n, HD, x.dtype)
        q = q * cos + _rotate_half(q) * sin
        k = k * cos + _rotate_half(k) * sin
        attn = jnp.einsum('bhqd,bhkd->bhqk', q, k) * scale
        attn = jax.nn.softmax(attn, axis=-1)
        out = jnp.einsum('bhqk,bhkd->bhqd', attn, v)
        out = out.transpose(0, 2, 1, 3).reshape(b, n, c)
        return jnp.einsum('bnc,dc->bnd', out, w_proj) + b_proj

    def _L0_ffn_ref(x, gate_w, gate_b, gate_center, w1, b1, w2, b2):
        import jax, jax.numpy as jnp
        import numpy as np
        B, N, C, H, E = (8, 256, 192, 768, 4)
        b, n, c = x.shape
        scores = jnp.einsum('bnc,ce->bne', x, gate_w) + gate_b
        p_experts = jax.nn.softmax(scores - gate_center, axis=-1)
        expert = jnp.argmax(p_experts, axis=-1).reshape(-1)
        xt = x.reshape(-1, c)
        h = jax.nn.gelu(jnp.einsum('tc,ech->eth', xt, w1) + b1[:, None, :], approximate=False)
        out_all = jnp.einsum('eth,ehc->etc', h, w2) + b2[:, None, :]
        out = jnp.take_along_axis(out_all, expert[None, :, None], axis=0)[0]
        return out.reshape(b, n, c)

    def _L1_attn_ref(x, w_qkv, w_proj, b_proj):
        import jax, jax.numpy as jnp
        import numpy as np
        HALF_WIN = 6

        def _local_attn(x, w_qkv, w_proj, b_proj, num_heads=12):
            B, N, C = x.shape
            H = num_heads
            D = C // H
            W = 2 * HALF_WIN + 1
            qkv = (x @ w_qkv).reshape(B, N, 3, H, D)
            q, k, v = (qkv[:, :, 0], qkv[:, :, 1], qkv[:, :, 2])
            offs = jnp.arange(-HALF_WIN, HALF_WIN + 1)
            idx = jnp.arange(N)[:, None] + offs[None, :]
            valid = (idx >= 0) & (idx < N)
            idxc = jnp.clip(idx, 0, N - 1)
            k_win = k[:, idxc]
            v_win = v[:, idxc]
            scale = D ** (-0.5)
            scores = jnp.einsum('bnhd,bnwhd->bnhw', q, k_win) * scale
            neg = jnp.asarray(jnp.finfo(scores.dtype).min, scores.dtype)
            scores = jnp.where(valid[None, :, None, :], scores, neg)
            p = jax.nn.softmax(scores, axis=-1)
            out = jnp.einsum('bnhw,bnwhd->bnhd', p, v_win)
            out = out.reshape(B, N, C)
            return out @ w_proj + b_proj
        return _local_attn(x, w_qkv, w_proj, b_proj)

    def _L1_ffn_ref(x, scale, gate_w, gate_b, w1, b1, w2, b2):
        import jax, jax.numpy as jnp
        import numpy as np
        B, S, H = (2, 256, 192)
        E, K, I = (16, 4, 192)
        ALPHA, LIMIT, EPS = (1.702, 7.0, 1e-05)

        def _swiglu(h):
            x_glu, x_lin = jnp.split(h, 2, axis=-1)
            x_glu = jnp.minimum(x_glu, LIMIT)
            x_lin = jnp.clip(x_lin, -LIMIT, LIMIT)
            return x_glu * jax.nn.sigmoid(ALPHA * x_glu) * (x_lin + 1.0)
        Bx, Sx, Hx = x.shape
        xf = x.astype(jnp.float32)
        t = xf * jax.lax.rsqrt(jnp.mean(xf * xf, axis=-1, keepdims=True) + EPS) * scale
        t = t.reshape(-1, Hx)
        T = t.shape[0]
        g = t @ gate_w.T + gate_b
        vals, idx = jax.lax.top_k(g, K)
        w = jax.nn.softmax(vals, axis=-1) / K
        full_w = jnp.zeros((T, E), jnp.float32).at[jnp.arange(T)[:, None], idx].set(w)
        h = jnp.einsum('th,ehf->tef', t, w1) + b1
        h = _swiglu(h)
        y = jnp.einsum('tei,eih->teh', h, w2) + b2
        out = jnp.einsum('teh,te->th', y, full_w) * K
        return x + out.astype(x.dtype).reshape(Bx, Sx, Hx)
    h = _L0_tok_ref(x, L0_tok_W_proj, L0_tok_b_proj)
    h = jnp.concatenate([jnp.broadcast_to(cls_tok, (h.shape[0], 1, h.shape[2])), h], axis=1)
    h = h + _L0_attn_ref(_layernorm(h, axis=-1), L0_attn_w_qkv, L0_attn_b_qkv, L0_attn_w_proj, L0_attn_b_proj)
    h = h + _L0_ffn_ref(_layernorm(h, axis=-1), L0_ffn_gate_w, L0_ffn_gate_b, L0_ffn_gate_center, L0_ffn_w1, L0_ffn_b1, L0_ffn_w2, L0_ffn_b2)
    h = h + _L1_attn_ref(_layernorm(h, axis=-1), L1_attn_w_qkv, L1_attn_w_proj, L1_attn_b_proj)
    h = h + _L1_ffn_ref(_layernorm(h, axis=-1), L1_ffn_scale, L1_ffn_gate_w, L1_ffn_gate_b, L1_ffn_w1, L1_ffn_b1, L1_ffn_w2, L1_ffn_b2)
    return h

_drawn_inputs = setup_inputs


def setup_inputs(seed=0):
    import zlib

    import numpy as np

    out = dict(_drawn_inputs(seed))
    spreads = {'L0_attn_b_qkv': (0.0, 0.1),
     'L0_attn_b_proj': (0.0, 0.1),
     'L0_ffn_gate_b': (0.0, 0.1),
     'L0_ffn_gate_center': (0.0, 0.1),
     'L1_attn_b_proj': (0.0, 0.1),
     'L1_ffn_scale': (1.0, 0.6),
     'L1_ffn_gate_b': (0.0, 0.8)}
    factors = {'L1_ffn_gate_w': 4.331,
     'L1_ffn_w1': 4.106,
     'L1_ffn_b1': 8.0,
     'L1_ffn_w2': 3.981,
     'L1_ffn_b2': 8.0}
    for name, (base, spread) in spreads.items():
        noise = np.random.default_rng([zlib.crc32(name.encode()), seed]).standard_normal(out[name].shape)
        drawn = base * np.exp(spread * noise) if base else spread * noise
        out[name] = jnp.asarray(drawn.astype(out[name].dtype))
    for name, factor in factors.items():
        out[name] = (out[name] * factor).astype(out[name].dtype)
    return out
```

```python
from contextlib import ExitStack

import concourse.bass as bass
from concourse import mybir

F32 = mybir.dt.float32
F32R = mybir.dt.float32r
ALU = mybir.AluOpType
ACT = mybir.ActivationFunctionType
AX_X = mybir.AxisListType.X

P = 128
IMAGES = 16
PATCH = 16
SIDE = 6
CHANNELS = 3
EMBED = 192
REST = EMBED - P
SEQ = SIDE * SIDE + 1
TOKENS = IMAGES * SEQ
HALF = TOKENS // 2
HALF_IMAGES = IMAGES // 2
TILES = (TOKENS + P - 1) // P
LAST = TOKENS - (TILES - 1) * P
PATCH_CHUNKS = CHANNELS * PATCH * PATCH // P
HEADS = 12
HEAD = EMBED // HEADS
HEADS_A = P // HEAD
HEADS_B = HEADS - HEADS_A
TRIO = 3
TRIOS = HEADS // TRIO
VCOLS = TRIO * HEAD + TRIO
STACK = TRIO * SEQ
SCALE = float(HEAD) ** -0.5
HIDDEN0 = 768
EXPERTS0 = 4
CHUNKS0 = HIDDEN0 // P
EXPERTS1 = 16
TOP = 4
PAIRS = EXPERTS1 // 2
UNITS = 3
LIMIT = 7.0
EPS = 1e-5
WINDOW = 6
FAR = -1e30
EMPTY = -3e38
TAKEN = 3e38
GROUPS = [[0, 1, 2], [3, 4, 5], [6, 7], [8, 9, 10], [11, 12, 13], [14, 15]]

EARLY = dict(ident=P, cos=HALF, sin=HALF, head=HEADS_A, trio=TRIO * HEAD, bqk=6, bv=2, bproj=EMBED)
LATE = dict(b1=EXPERTS0 * CHUNKS0, pair_b1=PAIRS * 2 * UNITS, gate_b=EXPERTS0, center=EXPERTS0,
            gate1_b=EXPERTS1, bproj1=EMBED, scale=EMBED, b2=EXPERTS0 * EMBED)
MULT = dict(gate=2 * EXPERTS0, gate1=2 * EXPERTS1, b2=EMBED, far=HEADS * SEQ, same=STACK, pad=1)
MULT_SPLIT = 2 * EXPERTS0 + 2 * EXPERTS1 + EMBED


def places(widths):
    at, out = 0, {}
    for name, width in widths.items():
        out[name] = (at, at + width)
        at += width
    return out, at


EARLY_AT, EARLY_N = places(EARLY)
LATE_AT, LATE_N = places(LATE)
MULT_AT, MULT_N = places(MULT)

QK0 = ["k", "k_turned", "q", "q_turned", "rest", "rest_turned"]
QK1 = ["k", "q", "rest"]
ATT0_CHUNK = len(QK0) * P + EMBED
ATT1_CHUNK = len(QK1) * P + EMBED
ATT0_N = 2 * ATT0_CHUNK + 2 * EMBED
ATT1_N = 2 * ATT1_CHUNK + 2 * EMBED
FFN0_N = 2 * HIDDEN0 + CHUNKS0 * EMBED
UP1_N = 2 * 2 * UNITS * P + 2
DOWN1_N = UNITS * EMBED
FFN1_N = UP1_N + DOWN1_N


def vit_tower(nc, x, w_embed, start, early, late, mult, att0, att1, ffn0, ffn1, out):
    ctx = ExitStack()
    with ctx:
        base = -(-nc.sbuf_base // 64) * 64
        top = [base]
        peak = [base]

        def here(name, shape, dtype, at):
            size = 4
            for s in shape[1:]:
                size *= s
            peak[0] = max(peak[0], at + size)
            return nc.alloc_sbuf_tensor_at(name, shape, dtype, offset=at), at + -(-size // 32) * 32

        def keep(name, shape, dtype=F32):
            t, top[0] = here(name, shape, dtype, top[0])
            return t

        def region(size):
            at = top[0]
            top[0] += -(-size // 32) * 32
            return at

        def placed(at, *tensors):
            out_ = []
            for name, shape, dtype in tensors:
                t, at = here(name, shape, dtype, at)
                out_.append(t)
            return out_

        def sem(name):
            return ctx.enter_context(nc.semaphore(name))

        h = keep("h", [P, TILES, EMBED])
        n = keep("n", [P, TILES, EMBED])
        x_hi = keep("x_hi", [P, TOKENS], F32R)
        x_lo = keep("x_lo", [P, TOKENS], F32R)
        x_rest = keep("x_rest", [P, TOKENS], F32R)
        ce = keep("ce", [P, EARLY_N])
        cl = keep("cl", [P, LATE_N])
        cm_hi = keep("cm_hi", [P, MULT_N], F32R)
        cm_lo = keep("cm_lo", [P, MULT_SPLIT], F32R)
        cm_raw = keep("cm_raw", [P, MULT_N])
        stats = keep("stats", [P, TILES, 6])
        moments = keep("moments", [P, TILES, 2])
        spread = keep("spread", [P, TILES])
        square = keep("square", [P, TILES])
        rstd = keep("rstd", [P, TILES])
        minus_half = keep("minus_half", [P, TILES])
        one = keep("one", [P, 1])
        top8 = keep("top8", [P, TILES, 8])
        s0 = keep("s0", [P, TILES, 12])
        s0_left = keep("s0_left", [P, TILES, 12])
        pick0 = keep("pick0", [P, TILES, 8])
        chosen = keep("chosen", [P, TILES, EXPERTS0])
        s1 = keep("s1", [P, TILES, EXPERTS1 + TOP])
        s1_left = keep("s1_left", [P, TILES, EXPERTS1 + TOP])
        pick1 = keep("pick1", [P, TILES, 8])
        gate = keep("gate", [P, TILES, EXPERTS1])
        among = keep("among", [P, TILES, EXPERTS1])
        gate_sum = keep("gate_sum", [P, TILES])
        gate_t = keep("gate_t", [64, TOKENS], F32R)
        lin_b1 = keep("lin_b1", [P, PAIRS * 2 * UNITS])

        r_split = region(2 * 2 * FFN0_N * 4)
        r_att_w = region(2 * ATT0_N * 4)
        r_att_raw = region(ATT0_N * 4)
        r_raw = region(2 * FFN0_N * 4)
        qz_a = keep("qz_a", [P, IMAGES, STACK])
        qz_b = keep("qz_b", [REST, IMAGES, STACK])
        vb = keep("vb", [STACK, IMAGES, TRIOS, VCOLS])
        r_work = top[0]

        w_raw, px_raw = placed(r_raw, ("w_raw", [P, PATCH_CHUNKS, EMBED], F32),
                               ("px_raw", [P, PATCH_CHUNKS, TOKENS], F32))
        w_split, px_hi, px_lo = placed(r_split, ("w_split", [P, 2, PATCH_CHUNKS, EMBED], F32R),
                                       ("px_hi", [P, PATCH_CHUNKS, TOKENS], F32R),
                                       ("px_lo", [P, PATCH_CHUNKS, TOKENS], F32R))
        (start_rows,) = placed(r_work, ("start_rows", [P, TILES, EMBED], F32))
        (a0_raw,) = placed(r_att_raw, ("a0_raw", [P, ATT0_N], F32))
        (a1_raw,) = placed(r_att_raw, ("a1_raw", [P, ATT1_N], F32))
        (y,) = placed(r_att_raw, ("y", [P, TILES, EMBED], F32))
        (a0,) = placed(r_att_w, ("a0", [P, 2, ATT0_N], F32R))
        (a1,) = placed(r_att_w, ("a1", [P, 2, ATT1_N], F32R))
        (f0_raw,) = placed(r_raw, ("f0_raw", [P, 2, FFN0_N], F32))
        (f1_raw,) = placed(r_raw, ("f1_raw", [P, 2, FFN1_N], F32))
        (f0,) = placed(r_split, ("f0", [P, 2, 2, FFN0_N], F32R))
        up1, down1 = placed(r_split, ("up1", [P, 2, 2, UP1_N], F32R), ("down1", [P, 2, 2, DOWN1_N], F32R))

        kb_at = r_work + IMAGES * EMBED * 4 + 2 * TOKENS * 4
        turn1, turn2 = placed(r_work, ("turn1", [P, TOKENS], F32), ("turn2", [P, TOKENS], F32))
        o_sb, k_a, k_b, kb_a, kb_b, probs, probs_t, o_div, o_max = placed(
            r_work, ("o_sb", [SEQ, IMAGES, EMBED], F32), ("k_a", [P, TOKENS], F32), ("k_b", [REST, TOKENS], F32),
            ("kb_a", [P, IMAGES, HEADS_A, SEQ], F32), ("kb_b", [REST, IMAGES, HEADS_B, SEQ], F32),
            ("probs", [STACK, 2, HEADS, SEQ], F32), ("probs_t", [STACK, 2, TRIOS, STACK], F32),
            ("o_div", [SEQ, 3, TRIOS, TRIO], F32),
            ("o_max", [STACK, 2, HEADS], F32))
        x3_hi, x3_rest, x3_lo = placed(kb_at, ("x3_hi", [P, IMAGES, STACK], F32R),
                                       ("x3_rest", [P, IMAGES, STACK], F32R), ("x3_lo", [P, IMAGES, STACK], F32R))
        hid0, hid0_hi, hid0_lo = placed(r_work, ("hid0", [P, 2, TOKENS], F32),
                                        ("hid0_hi", [P, 4, TOKENS], F32R), ("hid0_lo", [P, 4, TOKENS], F32R))
        glu, act1, lin, prod, hid1, hid1_hi, hid1_lo = placed(
            r_work, ("glu", [P, 2, TOKENS], F32), ("act1", [P, 2, TOKENS], F32),
            ("lin", [P, 2, TOKENS], F32), ("prod", [P, TOKENS], F32), ("hid1", [P, 2, TOKENS], F32),
            ("hid1_hi", [P, 2 * UNITS, TOKENS], F32R), ("hid1_lo", [P, 2 * UNITS, TOKENS], F32R))
        (gate_bc,) = placed(r_att_w, ("gate_bc", [P, 4, TOKENS], F32))
        assert peak[0] <= nc.sbuf_usable_end, peak[0] - nc.sbuf_usable_end

        ps = ctx.enter_context(nc.psum_tensor("ps", [P, 8, 512], F32))

        def cut(tensor, at, name):
            return tensor[:, at[name][0]:at[name][1]]

        ident = cut(ce, EARLY_AT, "ident")

        def rows_of(t):
            return P if t < TILES - 1 else LAST

        def halves(ap):
            return ap.rearrange("p (a c) -> p a c", a=2)

        def token_out(t):
            return ps[0:rows_of(t), t // 2, (t % 2) * EMBED:(t % 2 + 1) * EMBED]

        full_out = ps[:, 0:2, 0:2 * EMBED]
        last_out = ps[0:LAST, 2, 0:EMBED]

        def full_tiles(tensor):
            return tensor[:, 0:4, :].rearrange("p (a b) c -> p a (b c)", a=2)

        def features(lo, size):
            s = slice(lo, lo + size)
            return [(x_hi[:, s], 0, 0), (x_hi[:, s], 0, 1), (x_rest[:, s], 1, 0),
                    (x_rest[:, s], 1, 1), (x_lo[:, s], 0, 0)]

        def thrice(ap):
            return ap.rearrange("p (b k) -> p b k", k=SEQ).unsqueeze(2).broadcast_to([P, IMAGES, TRIO, SEQ])

        wraw_in, early_in, late_in, mult_in, att0_in, att1_in = (
            sem(s) for s in ("wraw_in", "early_in", "late_in", "mult_in", "att0_in", "att1_in"))
        px_in = [sem(f"px_in{c}") for c in range(PATCH_CHUNKS)]
        f0_in = [sem(f"f0_in{i}") for i in range(2)]
        f1_in = [sem(f"f1_in{i}") for i in range(2)]
        start_in, out_done = sem("start_in"), sem("out_done")
        px_hi_ready, px_lo_ready, embed_done = sem("px_hi_ready"), sem("px_lo_ready"), sem("embed_done")
        blank_ready, h_blank = sem("blank_ready"), sem("h_blank")
        mult_hi_ready, mult_lo_ready = sem("mult_hi_ready"), sem("mult_lo_ready")
        att_hi_ready, att_lo_ready, att1_hi_ready = sem("att_hi_ready"), sem("att_lo_ready"), sem("att1_hi_ready")
        ones_ready = sem("ones_ready")
        h_ready, h_biased = sem("h_ready"), sem("h_biased")
        stats_ready, moments_ready, spread_ready, rstd_ready, n_ready = (
            sem(s) for s in ("stats_ready", "moments_ready", "spread_ready", "rstd_ready", "n_ready"))
        y_ready, square_ready = sem("y_ready"), sem("square_ready")
        turned, x_hi_ready, x_lo_ready = sem("turned"), sem("x_hi_ready"), sem("x_lo_ready")
        A = []
        for layer in range(2):
            A.append({s: sem(f"{s}{layer}") for s in (
                "qk_done", "qk_read", "x3_act", "x3_pool", "x3_dve", "k_ready", "q_ready", "keys_act", "keys_dve", "keys_pool",
                "v_done", "v_ready", "s_done", "max_ready", "s_read", "p_ready", "pt_done", "pt_ready",
                "o_done", "div_ready", "o_ready", "ot_done", "ot_hi", "ot_lo", "proj_done")})
        gate0_done, s0_raw, s0_ready, top0_ready, pick0_ready, left0_ready, chosen_ready = (
            sem(s) for s in ("gate0_done", "s0_raw", "s0_ready", "top0_ready", "pick0_ready", "left0_ready", "chosen_ready"))
        f0_hi_ready, f0_lo_ready, up0_done, hid0_ready, hid0_hi_ready, hid0_lo_ready, down0_done, y0_added, b2_added = (
            sem(s) for s in ("f0_hi_ready", "f0_lo_ready", "up0_done", "hid0_ready", "hid0_hi_ready",
                             "hid0_lo_ready", "down0_done", "y0_added", "b2_added"))
        gate1_done, s1_ready, top1_ready, pick1_ready, left1_ready, among_ready, gap_ready, exp_ready, weigh_ready, gsum_ready, grec_ready, gate_ready = (
            sem(s) for s in ("gate1_done", "s1_ready", "top1_ready", "pick1_ready", "left1_ready", "among_ready",
                             "gap_ready", "exp_ready", "weigh_ready", "gsum_ready", "grec_ready", "gate_ready"))
        gt_done, gt_hi, gt_lo, lin_b1_ready = sem("gt_done"), sem("gt_hi"), sem("gt_lo"), sem("lin_b1_ready")
        up1_hi, up1_lo, down1_hi, down1_lo = sem("up1_hi"), sem("up1_lo"), sem("down1_hi"), sem("down1_lo")
        glu_done, lin_done, bc_done, bc_ready, glu_ready, lin_read, lin_ready, act1_ready, prod_ready, hid1_ready, hid1_hi_ready, hid1_lo_ready, down1_done = (
            sem(s) for s in ("glu_done", "lin_done", "bc_done", "bc_ready", "glu_ready", "lin_read", "lin_ready", "act1_ready",
                             "prod_ready", "hid1_ready", "hid1_hi_ready", "hid1_lo_ready", "down1_done"))
        result_ready = sem("result_ready")

        block = ctx.enter_context(nc.Block())

        @block.sync
        def _(sp):
            sp.dma_start(w_raw[:], w_embed).then_inc(wraw_in, 16)
            for c in range(PATCH_CHUNKS):
                sp.dma_start(px_raw[:, c, :], x[c]).then_inc(px_in[c], 16)
            sp.dma_start(ce[:], early).then_inc(early_in, 16)
            sp.dma_start(start_rows[:], start).then_inc(start_in, 16)
            sp.dma_start(a0_raw[:], att0).then_inc(att0_in, 16)
            sp.dma_start(cm_raw[:], mult).then_inc(mult_in, 16)
            sp.dma_start(cl[:], late).then_inc(late_in, 16)
            for e in range(EXPERTS0):
                if e == 0:
                    sp.wait_ge(px_lo_ready, PATCH_CHUNKS + 1)
                if e >= 2:
                    sp.wait_ge(f0_lo_ready, e - 1)
                sp.dma_start(f0_raw[:, e % 2, :], ffn0[e]).then_inc(f0_in[e % 2], 16)
                if e == 1:
                    sp.wait_ge(att_lo_ready, 1)
                    sp.dma_start(a1_raw[:], att1).then_inc(att1_in, 16)
            sp.wait_ge(f0_lo_ready, EXPERTS0)
            for q in range(2):
                sp.dma_start(f1_raw[:, q, :], ffn1[q]).then_inc(f1_in[q], 16)
            with sp.Fori(1, PAIRS // 2) as i:
                for q in range(2):
                    sp.wait_ge(down1_lo, i * 2 + (q - 1))
                    sp.dma_start(f1_raw[:, q, :], ffn1[bass.ds(i * 2 + q, 1)].rearrange("a p c -> (a p) c")
                                 ).then_inc(f1_in[q], 16)
            sp.wait_ge(result_ready, 1)
            sp.dma_start(out[0:4 * P, :].rearrange("(t p) c -> p t c", p=P), n[:, 0:4, :]).then_inc(out_done, 16)
            sp.wait_ge(result_ready, 2)
            sp.dma_start(out[4 * P:TOKENS, :], n[0:LAST, 4, :]).then_inc(out_done, 16)
            sp.wait_ge(out_done, 32)

        @block.gpsimd
        def _(pool):
            def power(stage):
                pool.wait_ge(spread_ready, stage + 1)
                pool.tensor_tensor(rstd[:], spread[:], minus_half[:], ALU.pow).then_inc(rstd_ready, 1)

            def bias_rows(stage, bias):
                pool.wait_ge(n_ready, TILES * (stage + 1))
                pool.tensor_tensor(h[:], h[:], bias.unsqueeze(1).broadcast_to([P, TILES, EMBED]),
                                   ALU.add).then_inc(h_biased, 1)

            def three_rest(layer):
                pool.wait_ge(x_lo_ready, 8 * layer + 4)
                pool.tensor_copy(x3_rest[:].rearrange("p b (r k) -> p b r k", r=TRIO), thrice(x_rest[:])
                                 ).then_inc(A[layer]["x3_pool"], 1)

            def keys_rest(layer):
                s = A[layer]
                pool.wait_ge(s["k_ready"], 2)
                pool.wait_ge(s["v_done"], HALF_IMAGES)
                for b in range(0, IMAGES, HALF_IMAGES):
                    kk = k_b[:, b * SEQ:(b + HALF_IMAGES) * SEQ].rearrange("p (b k) -> p b k", k=SEQ)
                    pool.tensor_tensor(
                        kb_b[:, b:b + HALF_IMAGES, :, :],
                        kk.unsqueeze(2).broadcast_to([REST, HALF_IMAGES, HEADS_B, SEQ]),
                        cut(ce, EARLY_AT, "head")[0:REST, 0:HEADS_B].unsqueeze(1).unsqueeze(3)
                        .broadcast_to([REST, HALF_IMAGES, HEADS_B, SEQ]),
                        ALU.mult).then_inc(s["keys_pool"], 1)

            def split(raw, hi, lo, hi_sem, hi_count, lo_sem):
                pool.tensor_tensor(hi, raw, one[:, 0:1].broadcast_to(list(raw.shape)), ALU.mult).then_inc(hi_sem, 1)
                pool.wait_ge(hi_sem, hi_count)
                pool.tensor_tensor(lo, raw, hi.bitcast(F32), ALU.subtract).then_inc(lo_sem, 1)

            pool.memset(minus_half[:], -0.5).then_inc(blank_ready, 1)
            pool.memset(one[:], 1.0).then_inc(blank_ready, 1)
            for t in (qz_a, qz_b):
                pool.memset(t[:], 0.0).then_inc(blank_ready, 1)
            for t in (s0, s1, pick0, pick1):
                pool.memset(t[:], EMPTY).then_inc(blank_ready, 1)
            pool.memset(gate_t[:].bitcast(F32), 0.0).then_inc(blank_ready, 1)
            pool.wait_ge(early_in, 16)
            trio = cut(ce, EARLY_AT, "trio")[0:STACK].rearrange("p (j d) -> p j d", d=HEAD)[:, :, 0:1]
            pool.tensor_copy(vb[:, :, :, TRIO * HEAD:].rearrange("p b g j -> p (b g) j"),
                             trio.rearrange("p j d -> p d j").broadcast_to([STACK, IMAGES * TRIOS, TRIO])
                             ).then_inc(ones_ready, 1)
            pool.wait_ge(blank_ready, 9)
            pool.wait_ge(att_hi_ready, 1)
            pool.tensor_tensor(a0[:, 1, :], a0_raw[:], a0[:, 0, :].bitcast(F32), ALU.subtract).then_inc(att_lo_ready, 1)
            power(0)
            three_rest(0)
            bias_rows(0, cut(ce, EARLY_AT, "bproj"))
            keys_rest(0)
            pool.wait_ge(mult_hi_ready, 1)
            pool.tensor_tensor(cm_lo[:], cm_raw[:, 0:MULT_SPLIT], cm_hi[:, 0:MULT_SPLIT].bitcast(F32),
                               ALU.subtract).then_inc(mult_lo_ready, 1)
            for e in range(EXPERTS0):
                pool.wait_ge(f0_in[e % 2], 16 * (e // 2 + 1))
                if e == 0:
                    pool.wait_ge(embed_done, 1)
                if e >= 2:
                    pool.wait_ge(down0_done, CHUNKS0 * (e - 1))
                split(f0_raw[:, e % 2, :], f0[:, e % 2, 0, :], f0[:, e % 2, 1, :], f0_hi_ready, e + 1, f0_lo_ready)
                if e == 1:
                    power(1)
            pool.wait_ge(att1_in, 16)
            pool.wait_ge(A[0]["proj_done"], 2)
            split(a1_raw[:], a1[:, 0, :], a1[:, 1, :], att1_hi_ready, 1, att_lo_ready)
            power(2)
            three_rest(1)
            bias_rows(2, cut(cl, LATE_AT, "bproj1"))
            keys_rest(1)
            pool.wait_ge(down0_done, EXPERTS0 * CHUNKS0)

            def split_pair(q, i):
                first = isinstance(i, int)
                pool.wait_ge(f1_in[q], 16 if first else i * 16 + 16)
                if not first:
                    pool.wait_ge(lin_done, i * (2 * UNITS) + UNITS * (q - 1))
                split(f1_raw[:, q, 0:UP1_N], up1[:, q, 0, :], up1[:, q, 1, :], up1_hi,
                      q + 1 if first else i * 2 + (q + 1), up1_lo)
                if not first:
                    pool.wait_ge(down1_done, i * (2 * UNITS) + UNITS * (q - 1))
                split(f1_raw[:, q, UP1_N:], down1[:, q, 0, :], down1[:, q, 1, :], down1_hi,
                      q + 1 if first else i * 2 + (q + 1), down1_lo)

            split_pair(0, 0)
            split_pair(1, 0)
            power(3)
            power(4)
            pool.wait_ge(y_ready, TILES)
            pool.tensor_tensor(h[:], h[:], y[:], ALU.add).then_inc(h_biased, 1)
            with pool.Fori(1, PAIRS // 2) as i:
                split_pair(0, i)
                split_pair(1, i)

        @block.tensor
        def _(pe):
            def mm(o, lhs, rhs, start, stop):
                return pe.matmul(o, lhs, rhs, start=start, stop=stop, skip_group_check=True)

            def turn_rows(stage):
                if stage == 0:
                    pe.wait_ge(early_in, 16)
                for lo, hi, bank in ((0, 3, 3), (3, TILES, 4)):
                    pe.wait_ge(n_ready, TILES * stage + hi)
                    for t in range(lo, hi):
                        m, at = rows_of(t), (t - lo) * P
                        last = pe.transpose(ps[:, bank, at:at + m], n[0:m, t, 0:P], ident[0:m, 0:m])
                    last.then_inc(turned, 1)
                    for t in range(lo, hi):
                        m, at = rows_of(t), (t - lo) * P
                        last = pe.transpose(ps[0:REST, bank + 2, at:at + m], n[0:m, t, P:EMBED], ident[0:m, 0:m])
                    last.then_inc(turned, 1)

            def rows_product(w, chunk_at, signal):
                for t in range(TILES):
                    passes = features(t * P, rows_of(t))
                    for k, (stat, c, part) in enumerate(passes):
                        at = chunk_at[c]
                        last = mm(token_out(t), stat, w[:, part, at:at + EMBED], k == 0, k == len(passes) - 1)
                    if t >= TILES - 2:
                        last.then_inc(signal, 1)

            def attention(layer, w, chunk, units):
                s = A[layer]
                stage = 2 * layer
                pe.wait_ge(att_lo_ready, layer + 1)
                pe.wait_ge(x_lo_ready, 4 * (stage + 1))

                def queries_keys(u):
                    if u >= 2:
                        pe.wait_ge(s["k_ready"] if layer else s["qk_read"], u - 1)
                    for hf in range(2):
                        for k, (mov, c, part) in enumerate(features(hf * HALF, HALF)):
                            at = c * chunk + u * P
                            last = mm(ps[:, 3 + 2 * (u % 2) + hf, 0:HALF], w[:, part, at:at + P], mov, k == 0, k == 4)
                    last.then_inc(s["qk_done"], 1)

                def image_values(i):
                    if i >= 2:
                        pe.wait_ge(s["v_ready"], i - 1)
                    for j in range(2):
                        b = 2 * i + j
                        for k, (stat, c, part) in enumerate(((x3_hi, 0, 0), (x3_hi, 0, 1), (x3_rest, 1, 0),
                                                             (x3_rest, 1, 1), (x3_lo, 0, 0))):
                            at = c * chunk + units * P
                            last = mm(ps[0:STACK, 7 * (1 - i % 2), j * EMBED:(j + 1) * EMBED],
                                      stat[:, b, :], w[:, part, at:at + EMBED], k == 0, k == 4)
                    last.then_inc(s["v_done"], 1)

                queries_keys(0)
                queries_keys(1)
                for side in ("x3_act", "x3_pool", "x3_dve"):
                    pe.wait_ge(s[side], 1)
                for i in range(HALF_IMAGES):
                    image_values(i)
                for u in range(2, units):
                    queries_keys(u)

                def scores(g):
                    group = GROUPS[g]
                    m = SEQ * len(group)
                    bank = 3 + g % 2
                    if g == 0:
                        pe.wait_ge(s["q_ready"], 8)
                        pe.wait_ge(s["keys_act"], KEYS_ACT[layer])
                        if KEYS_ACT[layer] < HEADS_A:
                            pe.wait_ge(s["keys_dve"], 2)
                        pe.wait_ge(s["keys_pool"], 2)
                    if g >= 2:
                        pe.wait_ge(s["s_read"], g - 1)
                    if layer:
                        far, same = cut(cm_hi, MULT_AT, "far"), cut(cm_hi, MULT_AT, "same")
                        mm(ps[0:m, bank, 0:HEADS * SEQ], same[0:SEQ, 0:m], far[0:SEQ, :], True, False)
                    for j, b in enumerate(group):
                        last = j == len(group) - 1
                        mm(ps[0:m, bank, 0:HEADS_A * SEQ], qz_a[:, b, 0:m],
                           kb_a[:, b, :, :].rearrange("p h k -> p (h k)"), not layer and j == 0, last)
                        done = mm(ps[0:m, bank, HEADS_A * SEQ:HEADS * SEQ], qz_b[:, b, 0:m],
                                  kb_b[:, b, :, :].rearrange("p h k -> p (h k)"), False, last)
                    done.then_inc(s["s_done"], 1)

                def turn_probs(g):
                    m = SEQ * len(GROUPS[g])
                    pe.wait_ge(s["p_ready"], g + 1)
                    if g >= 2:
                        pe.wait_ge(s["pt_ready"], g - 1)
                    for r in range(TRIOS):
                        last = pe.transpose(ps[0:STACK, 5 + g % 2, r * STACK:r * STACK + m],
                                            probs[0:m, g % 2, r * TRIO:(r + 1) * TRIO, :].rearrange("p h k -> p (h k)"),
                                            ident[0:m, 0:m])
                    last.then_inc(s["pt_done"], 1)

                def values(g):
                    if g == 0:
                        pe.wait_ge(s["v_ready"], HALF_IMAGES)
                        pe.wait_ge(ones_ready, 1)
                    pe.wait_ge(s["pt_ready"], g + 1)
                    if g >= 2:
                        pe.wait_ge(s["o_ready"], g - 1)
                    for j, b in enumerate(GROUPS[g]):
                        bank, at = OUT_BANKS[g % 2][j // 2], (j % 2) * TRIOS * VCOLS
                        for r in range(TRIOS):
                            last = mm(ps[0:SEQ, bank, at + r * VCOLS:at + (r + 1) * VCOLS],
                                      probs_t[:, g % 2, r, j * SEQ:(j + 1) * SEQ], vb[:, b, r, :], True, True)
                    last.then_inc(s["o_done"], 1)

                for g in range(len(GROUPS) + 2):
                    if g < len(GROUPS):
                        scores(g)
                    if 1 <= g <= len(GROUPS):
                        turn_probs(g - 1)
                    if g >= 2:
                        values(g - 2)
                pe.wait_ge(s["o_ready"], len(GROUPS))
                for hf in range(2):
                    for rest in range(2):
                        for i in range(HALF_IMAGES):
                            b = hf * HALF_IMAGES + i
                            part = o_sb[:, b, P:EMBED] if rest else o_sb[:, b, 0:P]
                            m = REST if rest else P
                            last = pe.transpose(ps[0:m, 3 + 2 * rest + hf, i * SEQ:(i + 1) * SEQ], part, ident[0:SEQ, 0:SEQ])
                        last.then_inc(s["ot_done"], 1)
                pe.wait_ge(s["ot_lo"], 4)
                rows_product(w, (2 * chunk, 2 * chunk + EMBED), s["proj_done"])

            def gates(stage, name, experts, signal):
                pe.wait_ge(x_lo_ready, 4 * (stage + 1))
                pe.wait_ge(mult_lo_ready, 1)
                for t in range(TILES):
                    for k, (stat, c, part) in enumerate(features(t * P, rows_of(t))):
                        at = MULT_AT[name][0] + c * experts
                        w = (cm_hi, cm_lo)[part]
                        last = mm(ps[0:rows_of(t), 7, t * experts:(t + 1) * experts], stat, w[:, at:at + experts], k == 0, k == 4)
                last.then_inc(signal, 1)

            def down(hi, lo, w_hi, w_lo, first, stop):
                for k, (stat, w) in enumerate(((hi, w_hi), (hi, w_lo), (lo, w_hi))):
                    for t in range(TILES):
                        last = mm(token_out(t), stat[:, t * P:t * P + rows_of(t)], w,
                                  first and k == 0 and t % 2 == 0, stop and k == 2)
                return last

            for c in range(PATCH_CHUNKS):
                pe.wait_ge(px_lo_ready, c + 2)
                last = down(px_hi[:, c, :], px_lo[:, c, :], w_split[:, 0, c, :], w_split[:, 1, c, :], c == 0, c == PATCH_CHUNKS - 1)
            last.then_inc(embed_done, 1)

            turn_rows(0)
            attention(0, a0, ATT0_CHUNK, len(QK0))
            turn_rows(1)
            gates(1, "gate", EXPERTS0, gate0_done)

            def up0(u):
                e, c = divmod(u, CHUNKS0)
                if c == 0:
                    pe.wait_ge(f0_lo_ready, e + 1)
                if u >= 2:
                    pe.wait_ge(hid0_ready, u - 1)
                for hf in range(2):
                    for k, (mov, ch, part) in enumerate(features(hf * HALF, HALF)):
                        at = ch * HIDDEN0 + c * P
                        last = mm(ps[:, 3 + 2 * (u % 2) + hf, 0:HALF], f0[:, e % 2, part, at:at + P], mov, k == 0, k == 4)
                last.then_inc(up0_done, 1)

            def down0(u):
                e, c = divmod(u, CHUNKS0)
                pe.wait_ge(hid0_lo_ready, u + 1)
                if c == 0 and e:
                    pe.wait_ge(y0_added, TILES * e)
                at = 2 * HIDDEN0 + c * EMBED
                down(hid0_hi[:, u % 4, :], hid0_lo[:, u % 4, :], f0[:, e % 2, 0, at:at + EMBED],
                     f0[:, e % 2, 1, at:at + EMBED], c == 0, c == CHUNKS0 - 1).then_inc(down0_done, 1)

            units0 = EXPERTS0 * CHUNKS0
            for u in range(units0 + 2):
                if u < units0:
                    up0(u)
                if u >= 2:
                    down0(u - 2)

            turn_rows(2)
            attention(1, a1, ATT1_CHUNK, len(QK1))
            turn_rows(3)
            gates(3, "gate1", EXPERTS1, gate1_done)
            def turn_gates():
                pe.wait_ge(gate_ready, 1)
                for t in range(TILES):
                    m = rows_of(t)
                    last = pe.transpose(ps[0:EXPERTS1, t // 4, (t % 4) * P:(t % 4) * P + m], gate[0:m, t, :], ident[0:m, 0:m])
                last.then_inc(gt_done, 1)

            def open_sums():
                for part, w in enumerate((cm_hi, cm_lo)):
                    b2 = w[0:GATE_ROWS, MULT_AT["b2"][0]:MULT_AT["b2"][1]]
                    for t in range(TILES):
                        mm(token_out(t), gate_t[0:GATE_ROWS, t * P:t * P + rows_of(t)], b2, part == 0 and t % 2 == 0, False)

            def broadcast_gate(q, expert, hf, pair):
                count = pair * 4 + (2 * expert + hf)
                if not isinstance(count, int) or count:
                    pe.wait_ge(bc_ready, count)
                at = UP1_N - 2 + expert
                pick = up1[0:GATE_ROWS, q, 0, at:at + 1].broadcast_to([GATE_ROWS, P])
                mm(ps[:, 7, 0:HALF], pick, gate_t[0:GATE_ROWS, hf * HALF:(hf + 1) * HALF], True, True).then_inc(bc_done, 1)

            def up1_unit(q, col, bank, signal):
                for hf in range(2):
                    for k, (mov, ch, part) in enumerate(features(hf * HALF, HALF)):
                        at = ch * 2 * UNITS * P + col * P
                        last = mm(ps[:, bank + hf, 0:HALF], up1[:, q, part, at:at + P], mov, k == 0, k == 4)
                last.then_inc(signal, 1)

            def down1_unit(slot, count, stop):
                pe.wait_ge(hid1_lo_ready, count)
                q, u = divmod(slot, UNITS)
                at = u * EMBED
                down(hid1_hi[:, slot, :], hid1_lo[:, slot, :], down1[:, q, 0, at:at + EMBED],
                     down1[:, q, 1, at:at + EMBED], False, stop).then_inc(down1_done, 1)

            def two_pairs(i):
                first = isinstance(i, int)
                for slot in range(2 * UNITS):
                    q, u = divmod(slot, UNITS)
                    unit = i * (2 * UNITS) + slot
                    pair = i * 2 + q
                    if u == 0:
                        pe.wait_ge(up1_lo, pair + 1)
                    if not (first and slot == 0):
                        pe.wait_ge(glu_ready, unit)
                    up1_unit(q, u, 3, glu_done)
                    if first and slot == 1:
                        pe.wait_ge(gt_lo, 2)
                        broadcast_gate(q, 0, 0, pair)
                    elif first and slot == 2:
                        broadcast_gate(q, 1, 1, pair)
                    elif not (first and slot == 0) and u < 2:
                        broadcast_gate(q, u, 0, pair)
                    if not (first and slot == 0):
                        pe.wait_ge(lin_read, unit)
                    up1_unit(q, UNITS + u, 5, lin_done)
                    if first and slot == 0:
                        turn_gates()
                    elif first and slot == 1:
                        broadcast_gate(q, 0, 1, pair)
                        open_sums()
                        broadcast_gate(q, 1, 0, pair)
                    elif u < 2:
                        broadcast_gate(q, u, 1, pair)
                    if not (first and slot < UNITS):
                        if u == 0:
                            pe.wait_ge(down1_lo, pair)
                        down1_unit((slot + UNITS) % (2 * UNITS), unit - (UNITS - 1), False)

            two_pairs(0)
            with pe.Fori(1, PAIRS // 2) as i:
                two_pairs(i)
            pe.wait_ge(down1_lo, PAIRS)
            for u in range(UNITS):
                down1_unit(UNITS + u, UNITS * (PAIRS - 1) + u + 1, u == UNITS - 1)

        @block.scalar
        def _(act):
            def copy(o, i):
                return act.activation(o, i, ACT.Copy)

            def feature_hi(stage):
                for k, (bank, lo, hi) in enumerate(TURNED):
                    act.wait_ge(turned, 4 * stage + k + 1)
                    m, dst = (REST, x_rest) if k % 2 else (P, x_hi)
                    copy(dst[0:m, lo:hi], ps[0:m, bank, 0:hi - lo]).then_inc(x_hi_ready, 1)

            def attention(layer):
                s = A[layer]
                act.wait_ge(x_lo_ready, 8 * layer + 4)
                copy(x3_hi[:].rearrange("p b (r k) -> p b r k", r=TRIO), thrice(x_hi[:])).then_inc(s["x3_act"], 1)
                act.wait_ge(s["k_ready"], 1)
                act.wait_ge(s["v_done"], HALF_IMAGES)
                for hd in range(KEYS_ACT[layer]):
                    act.activation(kb_a[:, :, hd, :], k_a[:].rearrange("p (b k) -> p b k", k=SEQ), ACT.Copy,
                                   scale=ce[:, EARLY_AT["head"][0] + hd:EARLY_AT["head"][0] + hd + 1]).then_inc(s["keys_act"], 1)

                def soften(g):
                    m = SEQ * len(GROUPS[g])
                    act.wait_ge(s["s_read"], g + 1)
                    act.activation(probs[0:m, g % 2], probs[0:m, g % 2], ACT.Exp, scale=SCALE).then_inc(s["p_ready"], 1)

                def keep_turned(g):
                    m = SEQ * len(GROUPS[g])
                    act.wait_ge(s["pt_done"], g + 1)
                    if g >= 2:
                        act.wait_ge(s["o_done"], g - 1)
                    copy(probs_t[:, g % 2, :, 0:m],
                         ps[0:STACK, 5 + g % 2, 0:TRIOS * STACK].rearrange("p (r c) -> p r c", c=STACK)[:, :, 0:m]
                         ).then_inc(s["pt_ready"], 1)

                for g in range(len(GROUPS) + 1):
                    if g < len(GROUPS):
                        soften(g)
                    if g:
                        keep_turned(g - 1)
                for k in range(4):
                    hf, rest = divmod(k, 2)
                    act.wait_ge(s["ot_done"], k + 1)
                    m = REST if rest else P
                    dst = (x_rest if rest else x_hi)[0:m, hf * HALF:(hf + 1) * HALF]
                    src = ps[0:m, 3 + 2 * rest + hf, 0:HALF]
                    if layer:
                        copy(dst, src).then_inc(s["ot_hi"], 1)
                    else:
                        at = EARLY_AT["bv"][0] + rest
                        act.activation(dst, src, ACT.Identity, bias=ce[0:m, at:at + 1]).then_inc(s["ot_hi"], 1)

            act.wait_ge(wraw_in, 16)
            copy(w_split[:, 0], w_raw[:]).then_inc(px_hi_ready, 1)
            for c in range(PATCH_CHUNKS):
                act.wait_ge(px_in[c], 16)
                copy(px_hi[:, c, :], px_raw[:, c, :]).then_inc(px_hi_ready, 1)
            act.wait_ge(early_in, 16)
            act.wait_ge(att0_in, 16)
            copy(a0[:, 0, :], a0_raw[:]).then_inc(att_hi_ready, 1)
            act.wait_ge(mult_in, 16)
            copy(cm_hi[:], cm_raw[:]).then_inc(mult_hi_ready, 1)

            feature_hi(0)
            attention(0)
            feature_hi(1)
            act.wait_ge(late_in, 16)
            for u in range(EXPERTS0 * CHUNKS0):
                act.wait_ge(up0_done, u + 1)
                if u >= 2:
                    act.wait_ge(hid0_lo_ready, u - 1)
                act.activation(halves(hid0[:, u % 2, :]), ps[:, 3 + 2 * (u % 2):5 + 2 * (u % 2), 0:HALF], ACT.Gelu,
                               bias=cl[:, LATE_AT["b1"][0] + u:LATE_AT["b1"][0] + u + 1]).then_inc(hid0_ready, 1)
            feature_hi(2)
            attention(1)
            feature_hi(3)
            act.wait_ge(gap_ready, 1)
            act.activation(gate[:], gate[:], ACT.Exp).then_inc(exp_ready, 1)

            def turned_gates():
                act.wait_ge(blank_ready, 9)
                act.wait_ge(gt_done, 1)
                copy(gate_t[0:EXPERTS1, 0:4 * P], ps[0:EXPERTS1, 0, 0:4 * P]).then_inc(gt_hi, 1)
                copy(gate_t[0:EXPERTS1, 4 * P:], ps[0:EXPERTS1, 1, 0:LAST]).then_inc(gt_hi, 1)

            def two_pairs(i):
                first = isinstance(i, int)
                for slot in range(2 * UNITS):
                    q, u = divmod(slot, UNITS)
                    unit = i * (2 * UNITS) + slot
                    pair = i * 2 + q

                    def keep_gate(expert, hf):
                        act.wait_ge(bc_done, pair * 4 + (2 * expert + hf + 1))
                        cols, mix = slice(hf * HALF, (hf + 1) * HALF), slice(expert * REST, (expert + 1) * REST)
                        if hf == 0 and not (first and q == 0):
                            act.wait_ge(hid1_ready, pair * UNITS - (2 - expert))
                        copy(gate_bc[:, expert, cols], ps[:, 7, 0:HALF])
                        copy(gate_bc[mix, 2 + q, cols], ps[mix, 7, 0:HALF]).then_inc(bc_ready, 1)

                    late = first and q == 0
                    if u < 2 and not late:
                        keep_gate(u, 0)
                    act.wait_ge(glu_ready, unit + 1)
                    if not (first and slot < 2):
                        act.wait_ge(prod_ready, unit - 1)
                    act.activation(act1[:, slot % 2, :], glu[:, slot % 2, :], ACT.Gelu_apprx_sigmoid).then_inc(act1_ready, 1)
                    if late and slot == 1:
                        keep_gate(0, 0)
                    if late and slot == 2:
                        keep_gate(1, 1)
                    act.wait_ge(lin_done, unit + 1)
                    at = UNITS + q * 2 * UNITS + u
                    column = lin_b1[:, at:at + 1] if first else lin_b1[:, bass.ds(i * (4 * UNITS) + at, 1)]
                    act.activation(halves(lin[:, slot % 2, :]), ps[:, 5:7, 0:HALF], ACT.Identity, bias=column).then_inc(lin_read, 1)
                    if late and slot == 0:
                        turned_gates()
                    if late and slot == 1:
                        keep_gate(0, 1)
                        keep_gate(1, 0)
                    if u < 2 and not late:
                        keep_gate(u, 1)
                    if not (first and slot == 0):
                        hidden_hi((slot - 1) % (2 * UNITS), unit, first and slot <= 2 * UNITS)

            def hidden_hi(slot, count, free):
                act.wait_ge(hid1_ready, count)
                if not free:
                    act.wait_ge(down1_done, count - 2 * UNITS)
                copy(hid1_hi[:, slot, :], hid1[:, slot % 2, :]).then_inc(hid1_hi_ready, 1)

            act.wait_ge(lin_b1_ready, 1)
            two_pairs(0)
            with act.Fori(1, PAIRS // 2) as i:
                two_pairs(i)
            hidden_hi(2 * UNITS - 1, UNITS * PAIRS, False)

        @block.vector
        def _(dve):
            sub, add, mult = ALU.subtract, ALU.add, ALU.mult

            def tt(o, a, b, op):
                return dve.tensor_tensor(o, a, b, op)

            def norm(stage):
                dve.wait_ge(h_ready, 2 * (stage + 1))
                for t in range(TILES):
                    dve.bn_stats(stats[:, t, :], h[:, t, :]).then_inc(stats_ready, 1)
                for t in range(TILES):
                    dve.wait_ge(stats_ready, TILES * stage + t + 1)
                    dve.bn_aggr(moments[:, t, :], stats[:, t, :]).then_inc(moments_ready, 1)
                dve.wait_ge(moments_ready, TILES * (stage + 1))
                var = moments[:, :, 1]
                dve.tensor_scalar(spread[:], var, EPS, None, add).then_inc(spread_ready, 1)
                dve.wait_ge(rstd_ready, stage + 1)
                for t in range(TILES):
                    row = dve.tensor_scalar((y if stage == 3 else n)[:, t, :], h[:, t, :], moments[:, t, 0:1], rstd[:, t:t + 1], sub, mult)
                    row.then_inc(y_ready if stage == 3 else n_ready, 1)
                if stage < 3:
                    return
                tt(square[:], var, rstd[:], mult).then_inc(square_ready, 1)
                dve.wait_ge(square_ready, 1)
                tt(square[:], square[:], rstd[:], mult).then_inc(square_ready, 1)
                dve.wait_ge(square_ready, 2)
                dve.tensor_scalar(spread[:], square[:], EPS, None, add).then_inc(spread_ready, 1)
                dve.wait_ge(rstd_ready, 5)
                dve.wait_ge(late_in, 16)
                for t in range(TILES):
                    dve.wait_ge(y_ready, t + 1)
                    dve.scalar_tensor_tensor(out=n[:, t, :], in0=y[:, t, :], scalar=rstd[:, t:t + 1],
                                             in1=cut(cl, LATE_AT, "scale"), op0=mult, op1=mult).then_inc(n_ready, 1)

            def feature_lo(stage):
                for k, (bank, lo, hi) in enumerate(TURNED):
                    dve.wait_ge(x_hi_ready, 4 * stage + k + 1)
                    m = REST if k % 2 else P
                    hi_part = (x_rest if k % 2 else x_hi)[0:m, lo:hi]
                    dst = x_rest[REST:P, lo:hi] if k % 2 else x_lo[:, lo:hi]
                    tt(dst, ps[0:m, bank, 0:hi - lo], hi_part.bitcast(F32), sub).then_inc(x_lo_ready, 1)

            def diagonal(qz, b, groups, each):
                whole = qz[:, b:b + groups * each, :]
                steps = [list(p) for p in whole.ap]
                return bass.AP(whole.tensor, whole.offset,
                               [steps[0], [each * STACK, groups], [STACK + SEQ, each], [1, SEQ]])

            def place(ap, b, groups, each):
                return ap[:, b * SEQ:(b + groups * each) * SEQ].rearrange("p (g j k) -> p g j k", g=groups, k=SEQ)

            def attention(layer):
                s = A[layer]
                dve.wait_ge(x_lo_ready, 8 * layer + 4)
                dve.tensor_copy(x3_lo[:].rearrange("p b (r k) -> p b r k", r=TRIO), thrice(x_lo[:])).then_inc(s["x3_dve"], 1)

                def keys_left():
                    n_act = KEYS_ACT[layer]
                    if n_act < HEADS_A:
                        dve.wait_ge(s["k_ready"], 1)
                        left = HEADS_A - n_act
                        for b in range(0, IMAGES, HALF_IMAGES):
                            kk = k_a[:, b * SEQ:(b + HALF_IMAGES) * SEQ].rearrange("p (b k) -> p b k", k=SEQ)
                            shape = [P, HALF_IMAGES, left, SEQ]
                            tt(kb_a[:, b:b + HALF_IMAGES, n_act:, :], kk.unsqueeze(2).broadcast_to(shape),
                               cut(ce, EARLY_AT, "head")[:, n_act:].unsqueeze(1).unsqueeze(3).broadcast_to(shape), mult
                               ).then_inc(s["keys_dve"], 1)

                def keep_values():
                    trio = cut(ce, EARLY_AT, "trio")[0:STACK]
                    for i in range(HALF_IMAGES):
                        dve.wait_ge(s["v_done"], i + 1)
                        tt(vb[:, 2 * i:2 * i + 2, :, 0:TRIO * HEAD].rearrange("p b g c -> p (b g) c"),
                           ps[0:STACK, 7 * (1 - i % 2), 0:2 * EMBED].rearrange("p (g c) -> p g c", c=TRIO * HEAD),
                           trio.unsqueeze(1).broadcast_to([STACK, 2 * TRIOS, TRIO * HEAD]), mult).then_inc(s["v_ready"], 1)

                if layer == 0:
                    cos = cut(ce, EARLY_AT, "cos").unsqueeze(1).broadcast_to([P, 2, HALF])
                    sin = cut(ce, EARLY_AT, "sin").unsqueeze(1).broadcast_to([P, 2, HALF])

                    def rotate(p):
                        if p == 1:
                            dve.wait_ge(s["k_ready"], 1)
                        if p == 2:
                            dve.wait_ge(s["q_ready"], 4)
                        for k, (dst, table) in enumerate(((turn1, cos), (turn2, sin))):
                            u = 2 * p + k
                            dve.wait_ge(s["qk_done"], u + 1)
                            dve.scalar_tensor_tensor(
                                out=halves(dst[:]), in0=ps[:, 3 + 2 * k:5 + 2 * k, 0:HALF],
                                scalar=ce[:, EARLY_AT["bqk"][0] + u:EARLY_AT["bqk"][0] + u + 1], in1=table,
                                op0=add, op1=mult).then_inc(s["qk_read"], 1)
                        dve.wait_ge(s["qk_read"], 2 * p + 2)

                    dve.wait_ge(blank_ready, 9)
                    rotate(0)
                    tt(k_a[:], turn1[:], turn2[:], add).then_inc(s["k_ready"], 1)
                    keep_values()
                    rotate(1)
                    for hf in range(2):
                        for b, g, e in ((hf * 8, 2, 3), (hf * 8 + 6, 1, 2)):
                            tt(diagonal(qz_a, b, g, e), place(turn1[:], b, g, e), place(turn2[:], b, g, e), add
                               ).then_inc(s["q_ready"], 1)
                    rotate(2)
                    tt(k_b[:], turn1[REST:P, :], turn2[REST:P, :], add).then_inc(s["k_ready"], 1)
                    for hf in range(2):
                        for b, g, e in ((hf * 8, 2, 3), (hf * 8 + 6, 1, 2)):
                            tt(diagonal(qz_b, b, g, e), place(turn1[0:REST, :], b, g, e), place(turn2[0:REST, :], b, g, e), add
                               ).then_inc(s["q_ready"], 1)
                else:
                    dve.wait_ge(s["qk_done"], 1)
                    dve.tensor_copy(halves(k_a[:]), ps[:, 3:5, 0:HALF]).then_inc(s["k_ready"], 1)
                    dve.wait_ge(s["qk_done"], 2)
                    for hf in range(2):
                        for b, g, e in ((0, 2, 3), (6, 1, 2)):
                            dve.tensor_copy(diagonal(qz_a, hf * 8 + b, g, e), place(ps[:, 5 + hf, 0:HALF], b, g, e)
                                            ).then_inc(s["q_ready"], 1)
                    keep_values()
                    dve.wait_ge(s["qk_done"], 3)
                    dve.tensor_copy(halves(k_b[:]), ps[REST:P, 3:5, 0:HALF]).then_inc(s["k_ready"], 1)
                    for hf in range(2):
                        for b, g, e in ((0, 2, 3), (6, 1, 2)):
                            dve.tensor_copy(diagonal(qz_b, hf * 8 + b, g, e), place(ps[0:REST, 3 + hf, 0:HALF], b, g, e)
                                            ).then_inc(s["q_ready"], 1)
                keys_left()

                def center(g):
                    m = SEQ * len(GROUPS[g])
                    sc = ps[0:m, 3 + g % 2, 0:HEADS * SEQ].rearrange("p (h k) -> p h k", k=SEQ)
                    dve.wait_ge(s["s_done"], g + 1)
                    dve.tensor_reduce(o_max[0:m, g % 2, :], sc, AX_X, ALU.max).then_inc(s["max_ready"], 1)
                    dve.wait_ge(s["max_ready"], g + 1)
                    if g >= 2:
                        dve.wait_ge(s["pt_done"], g - 1)
                    tt(probs[0:m, g % 2], sc, o_max[0:m, g % 2, :].unsqueeze(2).broadcast_to([m, HEADS, SEQ]), sub
                       ).then_inc(s["s_read"], 1)

                def divide(g):
                    dve.wait_ge(s["o_done"], g + 1)
                    if g:
                        dve.wait_ge(s["o_ready"], g)
                    group = GROUPS[g]
                    parts = [(0, 2)] + [(2, 1)] * (len(group) == 3)
                    for k, (j, cnt) in enumerate(parts):
                        o = ps[0:SEQ, OUT_BANKS[g % 2][k], 0:cnt * TRIOS * VCOLS].rearrange("p (r c) -> p r c", c=VCOLS)
                        ins = dve.reciprocal(o_div[:, j:j + cnt].rearrange("p b r t -> p (b r) t"), o[:, :, TRIO * HEAD:])
                    ins.then_inc(s["div_ready"], 1)
                    dve.wait_ge(s["div_ready"], g + 1)
                    for k, (j, cnt) in enumerate(parts):
                        o = ps[0:SEQ, OUT_BANKS[g % 2][k], 0:cnt * TRIOS * VCOLS].rearrange("p (r c) -> p r c", c=VCOLS)
                        b = group[0] + j
                        ins = tt(o_sb[:, b:b + cnt, :].rearrange("p b (r t d) -> p (b r) t d", t=TRIO, d=HEAD),
                                 o[:, :, 0:TRIO * HEAD].rearrange("p r (t d) -> p r t d", d=HEAD),
                                 o_div[:, j:j + cnt].rearrange("p b r t -> p (b r) t").unsqueeze(3)
                                 .broadcast_to([SEQ, cnt * TRIOS, TRIO, HEAD]), mult)
                    ins.then_inc(s["o_ready"], 1)

                for g in range(len(GROUPS) + 2):
                    if g < len(GROUPS):
                        center(g)
                    if g >= 2:
                        divide(g - 2)
                for k in range(4):
                    hf, rest = divmod(k, 2)
                    dve.wait_ge(s["ot_hi"], k + 1)
                    m = REST if rest else P
                    cols = slice(hf * HALF, (hf + 1) * HALF)
                    src = ps[0:m, 3 + 2 * rest + hf, 0:HALF]
                    hi_part = (x_rest if rest else x_hi)[0:m, cols].bitcast(F32)
                    dst = x_rest[REST:P, cols] if rest else x_lo[:, cols]
                    if layer:
                        tt(dst, src, hi_part, sub).then_inc(s["ot_lo"], 1)
                    else:
                        at = EARLY_AT["bv"][0] + rest
                        dve.scalar_tensor_tensor(out=dst, in0=src, scalar=ce[0:m, at:at + 1], in1=hi_part, op0=add, op1=sub
                                                 ).then_inc(s["ot_lo"], 1)
                dve.wait_ge(h_biased, layer + 1)
                dve.wait_ge(s["proj_done"], 1)
                tt(full_tiles(h), full_out, full_tiles(h), add).then_inc(h_ready, 1)
                dve.wait_ge(s["proj_done"], 2)
                tt(h[0:LAST, TILES - 1, :], last_out, h[0:LAST, TILES - 1, :], add).then_inc(h_ready, 1)

            dve.memset(h[:, TILES - 1, :], 0.0).then_inc(h_blank, 1)
            dve.wait_ge(px_hi_ready, 1)
            tt(w_split[:, 1], w_raw[:], w_split[:, 0].bitcast(F32), sub).then_inc(px_lo_ready, 1)
            for c in range(PATCH_CHUNKS):
                dve.wait_ge(px_hi_ready, c + 2)
                tt(px_lo[:, c, :], px_raw[:, c, :], px_hi[:, c, :].bitcast(F32), sub).then_inc(px_lo_ready, 1)
            dve.wait_ge(early_in, 16)
            dve.wait_ge(start_in, 16)
            dve.wait_ge(embed_done, 1)
            dve.wait_ge(h_blank, 1)
            tt(full_tiles(h), full_out, full_tiles(start_rows), add).then_inc(h_ready, 1)
            tt(h[0:LAST, TILES - 1, :], last_out, start_rows[0:LAST, TILES - 1, :], add).then_inc(h_ready, 1)

            norm(0)
            feature_lo(0)
            attention(0)

            norm(1)
            feature_lo(1)
            dve.wait_ge(gate0_done, 1)
            dve.wait_ge(late_in, 16)

            def shifted(raw, experts, dst, bias, sem_):
                for lo, hi, m in ((0, 4, P), (4, 5, LAST)):
                    tt(dst[0:m, lo:hi, 0:experts], raw[0:m, lo * experts:hi * experts].rearrange("p (t e) -> p t e", e=experts),
                       bias[0:m].unsqueeze(1).broadcast_to([m, hi - lo, experts]), add).then_inc(sem_, 1)

            shifted(ps[:, 7, :], EXPERTS0, s0, cut(cl, LATE_AT, "gate_b"), s0_raw)
            dve.wait_ge(s0_raw, 2)
            tt(s0[:, :, 0:EXPERTS0], s0[:, :, 0:EXPERTS0],
               cut(cl, LATE_AT, "center").unsqueeze(1).broadcast_to([P, TILES, EXPERTS0]), sub).then_inc(s0_ready, 1)

            def first_ones(scores, picks, left, count, ready, ready_at, tops, picked, lefts):
                dve.wait_ge(ready, ready_at)
                for t in range(TILES):
                    dve.max(top8[:, t, :], scores[:, t, :]).then_inc(tops, 1)
                dve.wait_ge(tops, TILES)
                dve.tensor_copy(picks[:, :, 0:count], top8[:, :, 0:count]).then_inc(picked, 1)
                dve.wait_ge(picked, 1)
                for t in range(TILES):
                    dve.match_replace(left[:, t, :], picks[:, t, :], scores[:, t, :], TAKEN).then_inc(lefts, 1)
                dve.wait_ge(lefts, TILES)

            first_ones(s0, pick0, s0_left, 1, s0_ready, 1, top0_ready, pick0_ready, left0_ready)
            tt(chosen[:], s0_left[:, :, 0:EXPERTS0], s0[:, :, 0:EXPERTS0], ALU.not_equal).then_inc(chosen_ready, 1)
            dve.wait_ge(chosen_ready, 1)

            def split_hidden0(u):
                dve.wait_ge(hid0_ready, u + 1)
                if u >= 4:
                    dve.wait_ge(down0_done, u - 3)
                dve.tensor_copy(hid0_hi[:, u % 4, :], hid0[:, u % 2, :]).then_inc(hid0_hi_ready, 1)
                dve.wait_ge(hid0_hi_ready, u + 1)
                tt(hid0_lo[:, u % 4, :], hid0[:, u % 2, :], hid0_hi[:, u % 4, :].bitcast(F32), sub).then_inc(hid0_lo_ready, 1)

            def add_expert(e):
                dve.wait_ge(down0_done, CHUNKS0 * (e + 1))
                for t in range(TILES):
                    m = rows_of(t)
                    if e:
                        dve.wait_ge(b2_added, TILES * (e - 1) + t + 1)
                    dve.scalar_tensor_tensor(out=h[0:m, t, :], in0=token_out(t), scalar=chosen[0:m, t, e:e + 1],
                                             in1=h[0:m, t, :], op0=mult, op1=add).then_inc(y0_added, 1)
                b2 = cut(cl, LATE_AT, "b2").rearrange("p (e c) -> p e c", c=EMBED)
                for t in range(TILES):
                    m = rows_of(t)
                    dve.wait_ge(y0_added, TILES * e + t + 1)
                    last = e == EXPERTS0 - 1 and t >= TILES - 2
                    dve.scalar_tensor_tensor(out=h[0:m, t, :], in0=b2[0:m, e, :], scalar=chosen[0:m, t, e:e + 1],
                                             in1=h[0:m, t, :], op0=mult, op1=add).then_inc(h_ready if last else b2_added, 1)

            for u in range(EXPERTS0 * CHUNKS0):
                if u % CHUNKS0 == 1 and u > CHUNKS0:
                    add_expert(u // CHUNKS0 - 1)
                split_hidden0(u)
            add_expert(EXPERTS0 - 1)

            norm(2)
            feature_lo(2)
            attention(1)

            norm(3)
            feature_lo(3)
            b1 = cut(cl, LATE_AT, "pair_b1")
            dve.tensor_scalar(lin_b1[:], b1, 1.0, None, add).then_inc(lin_b1_ready, 1)
            dve.wait_ge(gate1_done, 1)
            shifted(ps[:, 7, :], EXPERTS1, s1, cut(cl, LATE_AT, "gate1_b"), s1_ready)
            first_ones(s1, pick1, s1_left, TOP, s1_ready, 2, top1_ready, pick1_ready, left1_ready)
            tt(among[:], s1_left[:, :, 0:EXPERTS1], s1[:, :, 0:EXPERTS1], ALU.not_equal).then_inc(among_ready, 1)
            tt(gate[:], s1[:, :, 0:EXPERTS1], top8[:, :, 0:1].broadcast_to([P, TILES, EXPERTS1]), sub).then_inc(gap_ready, 1)
            dve.wait_ge(exp_ready, 1)
            dve.wait_ge(among_ready, 1)
            tt(gate[:], gate[:], among[:], mult).then_inc(weigh_ready, 1)
            dve.wait_ge(weigh_ready, 1)
            dve.tensor_reduce(gate_sum[:], gate[:], AX_X, add).then_inc(gsum_ready, 1)
            dve.wait_ge(gsum_ready, 1)
            dve.reciprocal(gate_sum[:], gate_sum[:]).then_inc(grec_ready, 1)
            dve.wait_ge(grec_ready, 1)
            tt(gate[:], gate[:], gate_sum[:].unsqueeze(2).broadcast_to([P, TILES, EXPERTS1]), mult).then_inc(gate_ready, 1)

            def gates_lo():
                dve.wait_ge(gt_hi, 1)
                tt(gate_t[32:32 + EXPERTS1, 0:4 * P], ps[0:EXPERTS1, 0, 0:4 * P], gate_t[0:EXPERTS1, 0:4 * P].bitcast(F32), sub
                   ).then_inc(gt_lo, 1)
                dve.wait_ge(gt_hi, 2)
                tt(gate_t[32:32 + EXPERTS1, 4 * P:], ps[0:EXPERTS1, 1, 0:LAST], gate_t[0:EXPERTS1, 4 * P:].bitcast(F32), sub
                   ).then_inc(gt_lo, 1)

            def hidden(slot, count):
                dve.wait_ge(lin_read, count)
                part = lin[:, slot % 2, :]
                dve.tensor_scalar(part, part, LIMIT + 1.0, 1.0 - LIMIT, ALU.min, ALU.max).then_inc(lin_ready, 1)
                dve.wait_ge(act1_ready, count)
                dve.wait_ge(lin_ready, count)
                tt(prod[:], part, act1[:, slot % 2, :], mult).then_inc(prod_ready, 1)
                dve.wait_ge(prod_ready, count)

            def weigh(slot, pair):
                q, u = divmod(slot, UNITS)
                dve.wait_ge(bc_ready, pair * 4 + (2 if u == 0 else 4))
                tt(hid1[:, slot % 2, :], prod[:], gate_bc[:, (0, 1, 2 + q)[u], :], mult).then_inc(hid1_ready, 1)

            def hidden_lo(slot, count):
                dve.wait_ge(hid1_hi_ready, count)
                tt(hid1_lo[:, slot, :], hid1[:, slot % 2, :], hid1_hi[:, slot, :].bitcast(F32), sub).then_inc(hid1_lo_ready, 1)

            def two_pairs(i):
                first = isinstance(i, int)
                for slot in range(2 * UNITS):
                    q, u = divmod(slot, UNITS)
                    unit = i * (2 * UNITS) + slot
                    at = q * 2 * UNITS + u
                    if not (first and slot < 2):
                        dve.wait_ge(act1_ready, unit - 1)
                    dve.wait_ge(glu_done, unit + 1)
                    column = b1[:, at:at + 1] if first else cl[:, bass.ds(i * (4 * UNITS) + (LATE_AT["pair_b1"][0] + at), 1)]
                    dve.tensor_scalar(halves(glu[:, slot % 2, :]), ps[:, 3:5, 0:HALF], column, LIMIT, add, ALU.min
                                      ).then_inc(glu_ready, 1)
                    if first and slot == 0:
                        gates_lo()
                    if not (first and slot < 2):
                        hidden_lo((slot - 2) % (2 * UNITS), unit - 1)
                    if not (first and slot == 0):
                        earlier = (slot - 1) % (2 * UNITS)
                        hidden(earlier, unit)
                        weigh(earlier, i * 2 + (slot - 1) // UNITS)

            two_pairs(0)
            with dve.Fori(1, PAIRS // 2) as i:
                two_pairs(i)
            hidden_lo(2 * UNITS - 2, UNITS * PAIRS - 1)
            hidden(2 * UNITS - 1, UNITS * PAIRS)
            weigh(2 * UNITS - 1, PAIRS - 1)
            hidden_lo(2 * UNITS - 1, UNITS * PAIRS)
            dve.wait_ge(h_biased, 3)
            dve.wait_ge(down1_done, UNITS * PAIRS)
            tt(full_tiles(n), full_out, full_tiles(h), add).then_inc(result_ready, 1)
            tt(n[0:LAST, TILES - 1, :], last_out, h[0:LAST, TILES - 1, :], add).then_inc(result_ready, 1)


TURNED = [(3, 0, 3 * P), (5, 0, 3 * P), (4, 3 * P, TOKENS), (6, 3 * P, TOKENS)]
OUT_BANKS = [(7, 0), (1, 2)]
KEYS_ACT = [HEADS_A, 5]
GATE_ROWS = 32 + EXPERTS1


def kernel(x, cls_tok, L0_tok_W_proj, L0_tok_b_proj, L0_attn_w_qkv, L0_attn_b_qkv, L0_attn_w_proj,
           L0_attn_b_proj, L0_ffn_gate_w, L0_ffn_gate_b, L0_ffn_gate_center, L0_ffn_w1, L0_ffn_b1,
           L0_ffn_w2, L0_ffn_b2, L1_attn_w_qkv, L1_attn_w_proj, L1_attn_b_proj, L1_ffn_scale,
           L1_ffn_gate_w, L1_ffn_gate_b, L1_ffn_w1, L1_ffn_b1, L1_ffn_w2, L1_ffn_b2):
    import numpy as np
    import concourse.bacc as bacc
    from concourse.bass_utils import run_bass_kernel_spmd

    f32 = np.float32
    arr = {k: np.asarray(v) for k, v in locals().items() if k.startswith("L")}

    def chunked(w):
        return np.stack([w[:P], np.concatenate([w[P:], w[P:]])], axis=1)

    def rows(v):
        return np.broadcast_to(v.reshape(1, -1), (P, v.size))

    px = np.asarray(x).reshape(IMAGES, CHANNELS, SIDE, PATCH, SIDE, PATCH).transpose(1, 3, 5, 0, 2, 4)
    px = px.reshape(PATCH_CHUNKS * P, IMAGES, SEQ - 1)
    px = np.concatenate([np.zeros((PATCH_CHUNKS * P, IMAGES, 1), f32), px], axis=2)
    px = px.reshape(PATCH_CHUNKS, P, TOKENS)
    w_embed = arr["L0_tok_W_proj"].T.reshape(PATCH_CHUNKS, P, EMBED).transpose(1, 0, 2)
    start = np.concatenate([np.asarray(cls_tok).reshape(1, EMBED),
                            np.broadcast_to(arr["L0_tok_b_proj"], (SEQ - 1, EMBED))])
    start = np.concatenate([np.tile(start, (IMAGES, 1)), np.zeros((TILES * P - TOKENS, EMBED), f32)])
    start = start.reshape(TILES, P, EMBED).transpose(1, 0, 2)

    inv = f32(1.0) / f32(10000.0) ** (np.arange(0, HEAD, 2, dtype=f32) / f32(HEAD))
    angle = (np.arange(SEQ, dtype=f32)[:, None] * inv[None, :]).astype(f32)
    cos, sin = np.cos(angle), np.sin(angle)
    cos = np.concatenate([cos, cos], axis=1).T.astype(f32)
    sin = np.concatenate([-sin, sin], axis=1).T.astype(f32)
    cos, sin = (np.tile(t, (P // HEAD, HALF_IMAGES)) for t in (cos, sin))

    part = np.arange(P)
    head = (part[:, None] // HEAD == np.arange(HEADS_A)[None, :]).astype(f32)
    trio = (part[:, None] // SEQ == np.arange(TRIO * HEAD)[None, :] // HEAD).astype(f32)

    turn = np.arange(EMBED).reshape(HEADS, 2, HEAD // 2)[:, ::-1].reshape(-1)
    w_qkv, b_qkv = arr["L0_attn_w_qkv"], arr["L0_attn_b_qkv"]
    q0, k0 = np.arange(P), EMBED + np.arange(P)
    rest = np.concatenate([np.arange(P, EMBED), EMBED + np.arange(P, EMBED)])
    t2 = np.concatenate([turn, EMBED + turn])
    units0 = [k0, t2[k0], q0, t2[q0], rest, t2[rest]]
    cols0 = np.concatenate(units0 + [2 * EMBED + np.arange(EMBED)])
    bqk = np.stack([b_qkv[u] for u in units0], axis=1)
    bv = b_qkv[2 * EMBED:]
    bv = np.stack([bv[:P], np.concatenate([bv[P:], bv[P:]])], axis=1)
    att0 = np.concatenate([chunked(w_qkv.T[:, cols0]).reshape(P, -1),
                           chunked(arr["L0_attn_w_proj"].T).reshape(P, -1)], axis=1)
    cols1 = np.concatenate([k0, q0, rest, 2 * EMBED + np.arange(EMBED)])
    att1 = np.concatenate([chunked(arr["L1_attn_w_qkv"][:, cols1]).reshape(P, -1),
                           chunked(arr["L1_attn_w_proj"]).reshape(P, -1)], axis=1)

    early = np.concatenate([np.eye(P, dtype=f32), cos, sin, head, trio, bqk, bv,
                            rows(arr["L0_attn_b_proj"])], axis=1)

    ffn0 = np.stack([
        np.concatenate([chunked(arr["L0_ffn_w1"][e]).reshape(P, -1),
                        arr["L0_ffn_w2"][e].reshape(CHUNKS0, P, EMBED).transpose(1, 0, 2).reshape(P, -1)], axis=1)
        for e in range(EXPERTS0)])
    b1 = arr["L0_ffn_b1"].reshape(EXPERTS0 * CHUNKS0, P).T

    def paired(a, b):
        out_ = []
        for lo in (0, EMBED):
            out_ += [a[..., lo:lo + P], b[..., lo:lo + P], a[..., lo + P:lo + EMBED], b[..., lo + P:lo + EMBED]]
        return np.concatenate(out_, axis=-1)

    up, b1_1, w2_1 = arr["L1_ffn_w1"], arr["L1_ffn_b1"], arr["L1_ffn_w2"]
    ffn1, pair_b1 = [], []
    for q in range(PAIRS):
        a, b = 2 * q, 2 * q + 1
        pick = np.stack([(part % 32 == e) & (part < GATE_ROWS) for e in (a, b)], axis=1).astype(f32)
        down = np.concatenate([w2_1[a][:P], w2_1[b][:P], np.concatenate([w2_1[a][P:], w2_1[b][P:]])], axis=1)
        ffn1.append(np.concatenate([chunked(paired(up[a], up[b])).reshape(P, -1), pick, down], axis=1))
        pair_b1.append(paired(b1_1[a], b1_1[b]).reshape(2 * UNITS, P).T)
    ffn1 = np.stack(ffn1)

    late = np.concatenate([b1] + pair_b1 + [rows(arr[s]) for s in (
        "L0_ffn_gate_b", "L0_ffn_gate_center", "L1_ffn_gate_b", "L1_attn_b_proj", "L1_ffn_scale", "L0_ffn_b2")], axis=1)

    twice = np.zeros((P, EMBED), f32)
    twice[0:EXPERTS1] = arr["L1_ffn_b2"]
    twice[32:32 + EXPERTS1] = arr["L1_ffn_b2"]
    pos = np.arange(SEQ)
    far = np.zeros((P, HEADS * SEQ), f32)
    far[0:SEQ] = np.tile(np.where(np.abs(pos[:, None] - pos[None, :]) > WINDOW, f32(FAR), f32(0)), (1, HEADS))
    same = np.zeros((P, STACK), f32)
    same[0:SEQ] = np.tile(np.eye(SEQ, dtype=f32), (1, TRIO))
    mult = np.concatenate([chunked(arr["L0_ffn_gate_w"]).reshape(P, -1), chunked(arr["L1_ffn_gate_w"].T).reshape(P, -1),
                           twice, far, same, np.zeros((P, 1), f32)], axis=1)

    given = dict(x=px, w_embed=w_embed, start=start, early=early, late=late, mult=mult, att0=att0, att1=att1, ffn0=ffn0, ffn1=ffn1)
    given = {k: np.ascontiguousarray(v) for k, v in given.items()}
    nc = bacc.Bacc("TRN2", target_bir_lowering=False, num_devices=1)
    args = {k: nc.dram_tensor(f"in_{k}", v.shape, F32, kind="ExternalInput").ap() for k, v in given.items()}
    out = nc.dram_tensor("out_0", (TOKENS, EMBED), F32, kind="ExternalOutput").ap()
    vit_tower(nc, out=out, **args)
    r = run_bass_kernel_spmd(nc, [{f"in_{k}": v for k, v in given.items()}], core_ids=[0])
    return r.results[0]["out_0"].reshape(IMAGES, SEQ, EMBED)
```

```python
from contextlib import ExitStack

import concourse.bass as bass
from concourse import mybir

F32 = mybir.dt.float32
F32R = mybir.dt.float32r
ALU = mybir.AluOpType
ACT = mybir.ActivationFunctionType
AX_X = mybir.AxisListType.X

P = 128
IMAGES = 16
PATCH = 16
SIDE = 6
CHANNELS = 3
EMBED = 192
REST = EMBED - P
SEQ = SIDE * SIDE + 1
TOKENS = IMAGES * SEQ
HALF = TOKENS // 2
HALF_IMAGES = IMAGES // 2
TILES = (TOKENS + P - 1) // P
LAST = TOKENS - (TILES - 1) * P
PATCH_CHUNKS = CHANNELS * PATCH * PATCH // P
HEADS = 12
HEAD = EMBED // HEADS
HEADS_A = P // HEAD
HEADS_B = HEADS - HEADS_A
TRIO = 3
TRIOS = HEADS // TRIO
VCOLS = TRIO * HEAD + TRIO
STACK = TRIO * SEQ
SCALE = float(HEAD) ** -0.5
HIDDEN0 = 768
EXPERTS0 = 4
CHUNKS0 = HIDDEN0 // P
EXPERTS1 = 16
TOP = 4
PAIRS = EXPERTS1 // 2
UNITS = 3
LIMIT = 7.0
EPS = 1e-5
WINDOW = 6
FAR = -1e30
EMPTY = -3e38
TAKEN = 3e38
GROUPS = [[0, 1, 2], [3, 4, 5], [6, 7], [8, 9, 10], [11, 12, 13], [14, 15]]

EARLY = dict(ident=P, cos=HALF, sin=HALF, head=HEADS_A, trio=TRIO * HEAD, bqk=6, bv=2, bproj=EMBED)
LATE = dict(b1=EXPERTS0 * CHUNKS0, pair_b1=PAIRS * 2 * UNITS, gate_b=EXPERTS0, center=EXPERTS0,
            gate1_b=EXPERTS1, bproj1=EMBED, scale=EMBED, b2=EXPERTS0 * EMBED)
MULT = dict(gate=2 * EXPERTS0, gate1=2 * EXPERTS1, b2=EMBED, far=HEADS * SEQ, same=STACK, pad=1)
MULT_SPLIT = 2 * EXPERTS0 + 2 * EXPERTS1 + EMBED


def places(widths):
    at, out = 0, {}
    for name, width in widths.items():
        out[name] = (at, at + width)
        at += width
    return out, at


EARLY_AT, EARLY_N = places(EARLY)
LATE_AT, LATE_N = places(LATE)
MULT_AT, MULT_N = places(MULT)

QK0 = ["k", "k_turned", "rest", "rest_turned", "q", "q_turned"]
QK1 = ["k", "rest", "q"]
ATT0_CHUNK = len(QK0) * P + EMBED
ATT1_CHUNK = len(QK1) * P + EMBED
ATT0_N = 2 * ATT0_CHUNK + 2 * EMBED
ATT1_N = 2 * ATT1_CHUNK + 2 * EMBED
FFN0_N = 2 * HIDDEN0 + CHUNKS0 * EMBED
UP1_N = 2 * 2 * UNITS * P + 2
DOWN1_N = UNITS * EMBED
FFN1_N = UP1_N + DOWN1_N


def vit_tower(nc, x, w_embed, start, early, late, mult, att0, att1, ffn0, ffn1, out):
    ctx = ExitStack()
    with ctx:
        base = -(-nc.sbuf_base // 64) * 64
        top = [base]
        peak = [base]

        def here(name, shape, dtype, at):
            size = 4
            for s in shape[1:]:
                size *= s
            peak[0] = max(peak[0], at + size)
            return nc.alloc_sbuf_tensor_at(name, shape, dtype, offset=at), at + -(-size // 32) * 32

        def keep(name, shape, dtype=F32):
            t, top[0] = here(name, shape, dtype, top[0])
            return t

        def region(size):
            at = top[0]
            top[0] += -(-size // 32) * 32
            return at

        def placed(at, *tensors):
            out_ = []
            for name, shape, dtype in tensors:
                t, at = here(name, shape, dtype, at)
                out_.append(t)
            return out_

        def sem(name):
            return ctx.enter_context(nc.semaphore(name))

        h = keep("h", [P, TILES, EMBED])
        n = keep("n", [P, TILES, EMBED])
        x_hi = keep("x_hi", [P, TOKENS], F32R)
        x_lo = keep("x_lo", [P, TOKENS], F32R)
        x_rest = keep("x_rest", [P, TOKENS], F32R)
        ce = keep("ce", [P, EARLY_N])
        cl = keep("cl", [P, LATE_N])
        cm_hi = keep("cm_hi", [P, MULT_N], F32R)
        cm_lo = keep("cm_lo", [P, MULT_SPLIT], F32R)
        cm_raw = keep("cm_raw", [P, MULT_N])
        stats = keep("stats", [P, TILES, 6])
        moments = keep("moments", [P, TILES, 2])
        spread = keep("spread", [P, TILES])
        square = keep("square", [P, TILES])
        rms = keep("rms", [P, TILES])
        score_rows = keep("score_rows", [EXPERTS1, TOKENS])
        rstd = keep("rstd", [P, TILES])
        minus_half = keep("minus_half", [P, TILES])
        one = keep("one", [P, 1])
        top8 = keep("top8", [P, TILES, 8])
        s0 = keep("s0", [P, TILES, 12])
        s0_left = keep("s0_left", [P, TILES, 12])
        pick0 = keep("pick0", [P, TILES, 8])
        chosen = keep("chosen", [P, TILES, EXPERTS0])
        s1 = keep("s1", [P, TILES, EXPERTS1 + TOP])
        s1_left = keep("s1_left", [P, TILES, EXPERTS1 + TOP])
        pick1 = keep("pick1", [P, TILES, 8])
        gate = keep("gate", [P, TILES, EXPERTS1])
        among = keep("among", [P, TILES, EXPERTS1])
        gate_sum = keep("gate_sum", [P, TILES])
        gate_t = keep("gate_t", [64, TOKENS], F32R)
        lin_b1 = keep("lin_b1", [P, PAIRS * 2 * UNITS])

        r_split = region(2 * 2 * FFN0_N * 4)
        r_att_w = region(2 * ATT0_N * 4)
        r_att_raw = region(ATT0_N * 4)
        r_raw = region(2 * FFN0_N * 4)
        qz_a = keep("qz_a", [P, IMAGES, STACK])
        qz_b = keep("qz_b", [REST, IMAGES, STACK])
        vb = keep("vb", [STACK, IMAGES, TRIOS, VCOLS])
        r_work = top[0]

        w_raw, px_raw = placed(r_raw, ("w_raw", [P, PATCH_CHUNKS, EMBED], F32),
                               ("px_raw", [P, PATCH_CHUNKS, TOKENS], F32))
        w_split, px_hi, px_lo = placed(r_split, ("w_split", [P, 2, PATCH_CHUNKS, EMBED], F32R),
                                       ("px_hi", [P, PATCH_CHUNKS, TOKENS], F32R),
                                       ("px_lo", [P, PATCH_CHUNKS, TOKENS], F32R))
        (start_rows,) = placed(r_work, ("start_rows", [P, TILES, EMBED], F32))
        (a0_raw,) = placed(r_att_raw, ("a0_raw", [P, ATT0_N], F32))
        (a1_raw,) = placed(r_att_raw, ("a1_raw", [P, ATT1_N], F32))
        (y,) = placed(r_att_raw, ("y", [P, TILES, EMBED], F32))
        (a0,) = placed(r_att_w, ("a0", [P, 2, ATT0_N], F32R))
        (a1,) = placed(r_att_w, ("a1", [P, 2, ATT1_N], F32R))
        (f0_raw,) = placed(r_raw, ("f0_raw", [P, 2, FFN0_N], F32))
        (f1_raw,) = placed(r_raw, ("f1_raw", [P, 2, FFN1_N], F32))
        (f0,) = placed(r_split, ("f0", [P, 2, 2, FFN0_N], F32R))
        (f1,) = placed(r_split, ("f1", [P, 2, 2, FFN1_N], F32R))
        up1, down1 = f1[:, :, :, 0:UP1_N], f1[:, :, :, UP1_N:]

        turn1, turn2 = placed(r_work, ("turn1", [P, TOKENS], F32), ("turn2", [P, TOKENS], F32))
        o_sb, k_a, k_b, kb_a, kb_b, probs, probs_t, o_div, o_max = placed(
            r_work, ("o_sb", [SEQ, IMAGES, EMBED], F32), ("k_a", [P, TOKENS], F32), ("k_b", [REST, TOKENS], F32),
            ("kb_a", [P, IMAGES, HEADS_A, SEQ], F32), ("kb_b", [REST, IMAGES, HEADS_B, SEQ], F32),
            ("probs", [STACK, 2, HEADS, SEQ], F32), ("probs_t", [STACK, 2, TRIOS, STACK], F32),
            ("o_div", [SEQ, 3, TRIOS, TRIO], F32),
            ("o_max", [STACK, 2, HEADS], F32))
        x3_hi, x3_rest, x3_lo = placed(r_split + 2 * FFN0_N * 4, ("x3_hi", [P, IMAGES, STACK], F32R),
                                       ("x3_rest", [P, IMAGES, STACK], F32R), ("x3_lo", [P, IMAGES, STACK], F32R))
        hid0, hid0_hi, hid0_lo = placed(r_work, ("hid0", [P, 2, TOKENS], F32),
                                        ("hid0_hi", [P, 4, TOKENS], F32R), ("hid0_lo", [P, 4, TOKENS], F32R))
        glu, act1, lin, prod, hid1, hid1_hi, hid1_lo = placed(
            r_work, ("glu", [P, 2, TOKENS], F32), ("act1", [P, 2, TOKENS], F32),
            ("lin", [P, 2, TOKENS], F32), ("prod", [P, TOKENS], F32), ("hid1", [P, 2, TOKENS], F32),
            ("hid1_hi", [P, 2 * UNITS, TOKENS], F32R), ("hid1_lo", [P, 2 * UNITS, TOKENS], F32R))
        (gate_bc,) = placed(r_att_w, ("gate_bc", [P, 4, TOKENS], F32))
        assert peak[0] <= nc.sbuf_usable_end, peak[0] - nc.sbuf_usable_end

        ps = ctx.enter_context(nc.psum_tensor("ps", [P, 8, 512], F32))

        def cut(tensor, at, name):
            return tensor[:, at[name][0]:at[name][1]]

        ident = cut(ce, EARLY_AT, "ident")

        def rows_of(t):
            return P if t < TILES - 1 else LAST

        def halves(ap):
            return ap.rearrange("p (a c) -> p a c", a=2)

        def token_out(t):
            return ps[0:rows_of(t), t // 2, (t % 2) * EMBED:(t % 2 + 1) * EMBED]

        last_out = ps[0:LAST, 2, 0:EMBED]

        def features(lo, size):
            s = slice(lo, lo + size)
            return [(x_hi[:, s], 0, 0), (x_hi[:, s], 0, 1), (x_rest[:, s], 1, 0),
                    (x_rest[:, s], 1, 1), (x_lo[:, s], 0, 0)]

        def thrice(ap):
            return ap.rearrange("p (b k) -> p b k", k=SEQ).unsqueeze(2).broadcast_to([P, IMAGES, TRIO, SEQ])

        wraw_in, early_in, late_in, mult_in, att0_in, att1_in = (
            sem(s) for s in ("wraw_in", "early_in", "late_in", "mult_in", "att0_in", "att1_in"))
        px_in = [sem(f"px_in{c}") for c in range(PATCH_CHUNKS)]
        f0_in = [sem(f"f0_in{i}") for i in range(2)]
        f1_in = [sem(f"f1_in{i}") for i in range(2)]
        start_in, out_done = sem("start_in"), sem("out_done")
        px_hi_ready, px_lo_ready, embed_done = sem("px_hi_ready"), sem("px_lo_ready"), sem("embed_done")
        blank_ready, h_blank = sem("blank_ready"), sem("h_blank")
        mult_hi_ready, mult_lo_ready = sem("mult_hi_ready"), sem("mult_lo_ready")
        att_hi_ready, att_lo_ready, att1_hi_ready = sem("att_hi_ready"), sem("att_lo_ready"), sem("att1_hi_ready")
        ones_ready = sem("ones_ready")
        h_ready, h_biased = sem("h_ready"), sem("h_biased")
        stats_ready, moments_ready, spread_ready, rstd_ready, n_ready = (
            sem(s) for s in ("stats_ready", "moments_ready", "spread_ready", "rstd_ready", "n_ready"))
        y_ready, square_ready = sem("y_ready"), sem("square_ready")
        rms_spread, rms_ready, sums_done = sem("rms_spread"), sem("rms_ready"), sem("sums_done")
        turned, x_hi_ready, x_lo_ready = sem("turned"), sem("x_hi_ready"), sem("x_lo_ready")
        A = []
        for layer in range(2):
            A.append({s: sem(f"{s}{layer}") for s in (
                "qk_done", "qk_read", "x3_act", "x3_dve", "k_ready", "q_ready", "keys_act", "keys_pool",
                "v_done", "v_ready", "s_done", "max_ready", "s_read", "p_ready", "pt_done", "pt_ready",
                "o_done", "div_ready", "o_ready", "ot_done", "ot_hi", "ot_lo", "proj_done")})
        last_added = sem("last_added")
        rows_done, rows_ready = sem("rows_done"), sem("rows_ready")
        gate0_done, s0_raw, s0_ready, top0_ready, pick0_ready, left0_ready, chosen_ready = (
            sem(s) for s in ("gate0_done", "s0_raw", "s0_ready", "top0_ready", "pick0_ready", "left0_ready", "chosen_ready"))
        f0_hi_ready, f0_lo_ready, up0_done, hid0_ready, hid0_hi_ready, hid0_lo_ready, down0_done, y0_added, b2_added = (
            sem(s) for s in ("f0_hi_ready", "f0_lo_ready", "up0_done", "hid0_ready", "hid0_hi_ready",
                             "hid0_lo_ready", "down0_done", "y0_added", "b2_added"))
        gate1_done, s1_ready, top1_ready, pick1_ready, left1_ready, among_ready, gap_ready, exp_ready, weigh_ready, gsum_ready, grec_ready, gate_ready = (
            sem(s) for s in ("gate1_done", "s1_ready", "top1_ready", "pick1_ready", "left1_ready", "among_ready",
                             "gap_ready", "exp_ready", "weigh_ready", "gsum_ready", "grec_ready", "gate_ready"))
        gt_done, gt_hi, gt_lo, lin_b1_ready = sem("gt_done"), sem("gt_hi"), sem("gt_lo"), sem("lin_b1_ready")
        up1_hi, up1_lo, down1_hi, down1_lo = sem("up1_hi"), sem("up1_lo"), sem("down1_hi"), sem("down1_lo")
        glu_done, lin_done, bc_done, bc_ready, glu_ready, lin_read, lin_ready, act1_ready, prod_ready, hid1_ready, hid1_hi_ready, hid1_lo_ready, down1_done = (
            sem(s) for s in ("glu_done", "lin_done", "bc_done", "bc_ready", "glu_ready", "lin_read", "lin_ready", "act1_ready",
                             "prod_ready", "hid1_ready", "hid1_hi_ready", "hid1_lo_ready", "down1_done"))
        result_ready = sem("result_ready")

        block = ctx.enter_context(nc.Block())

        @block.sync
        def _(sp):
            sp.dma_start(w_raw[:], w_embed).then_inc(wraw_in, 16)
            for c in range(PATCH_CHUNKS):
                sp.dma_start(px_raw[:, c, :], x[c]).then_inc(px_in[c], 16)
            sp.dma_start(ce[:], early).then_inc(early_in, 16)
            sp.dma_start(start_rows[:], start).then_inc(start_in, 16)
            sp.dma_start(a0_raw[:], att0).then_inc(att0_in, 16)
            sp.dma_start(cm_raw[:], mult).then_inc(mult_in, 16)
            sp.dma_start(cl[:], late).then_inc(late_in, 16)
            for e in range(EXPERTS0):
                if e == 0:
                    sp.wait_ge(px_lo_ready, PATCH_CHUNKS + 1)
                if e >= 2:
                    sp.wait_ge(f0_lo_ready, e - 1)
                sp.dma_start(f0_raw[:, e % 2, :], ffn0[e]).then_inc(f0_in[e % 2], 16)
                if e == 1:
                    sp.wait_ge(att_lo_ready, 1)
                    sp.dma_start(a1_raw[:], att1).then_inc(att1_in, 16)
            sp.wait_ge(f0_lo_ready, EXPERTS0)
            for q in range(2):
                sp.dma_start(f1_raw[:, q, :], ffn1[q]).then_inc(f1_in[q], 16)
            with sp.Fori(1, PAIRS // 2) as i:
                for q in range(2):
                    sp.wait_ge(down1_lo, i * 2 + (q - 1))
                    sp.dma_start(f1_raw[:, q, :], ffn1[bass.ds(i * 2 + q, 1)].rearrange("a p c -> (a p) c")
                                 ).then_inc(f1_in[q], 16)
            for k in range(2):
                sp.wait_ge(result_ready, k + 1)
                sp.dma_start(out[k * 2 * P:(k + 1) * 2 * P, :].rearrange("(t p) c -> p t c", p=P), n[:, 2 * k:2 * k + 2, :]
                             ).then_inc(out_done, 16)
            sp.wait_ge(result_ready, 3)
            sp.dma_start(out[4 * P:TOKENS, :], n[0:LAST, 4, :]).then_inc(out_done, 16)
            sp.wait_ge(out_done, 48)

        @block.gpsimd
        def _(pool):
            def power(wait, count, source, dst, signal):
                for k, (lo, hi) in enumerate(PARTS):
                    pool.wait_ge(wait, count + k)
                    pool.tensor_tensor(dst[:, lo:hi], source[:, lo:hi], minus_half[:, lo:hi], ALU.pow).then_inc(signal, 1)

            def norm_power(stage):
                power(spread_ready, 2 * stage + 1, spread, rstd, rstd_ready)

            def bias_rows(stage, bias):
                pool.wait_ge(n_ready, TILES * (stage + 1))
                pool.tensor_tensor(h[:], h[:], bias.unsqueeze(1).broadcast_to([P, TILES, EMBED]),
                                   ALU.add).then_inc(h_biased, 1)

            def keys_rest(layer):
                s = A[layer]
                pool.wait_ge(s["k_ready"], 2)
                for b in range(0, IMAGES, HALF_IMAGES):
                    kk = k_b[:, b * SEQ:(b + HALF_IMAGES) * SEQ].rearrange("p (b k) -> p b k", k=SEQ)
                    pool.tensor_tensor(
                        kb_b[:, b:b + HALF_IMAGES, :, :],
                        kk.unsqueeze(2).broadcast_to([REST, HALF_IMAGES, HEADS_B, SEQ]),
                        cut(ce, EARLY_AT, "head")[0:REST, 0:HEADS_B].unsqueeze(1).unsqueeze(3)
                        .broadcast_to([REST, HALF_IMAGES, HEADS_B, SEQ]),
                        ALU.mult).then_inc(s["keys_pool"], 1)

            def split(raw, hi, lo, hi_sem, hi_count, lo_sem):
                pool.tensor_tensor(hi, raw, one[:, 0:1].broadcast_to(list(raw.shape)), ALU.mult).then_inc(hi_sem, 1)
                pool.wait_ge(hi_sem, hi_count)
                pool.tensor_tensor(lo, raw, hi.bitcast(F32), ALU.subtract).then_inc(lo_sem, 1)

            pool.memset(minus_half[:], -0.5).then_inc(blank_ready, 1)
            pool.memset(one[:], 1.0).then_inc(blank_ready, 1)
            for t in (qz_a, qz_b):
                pool.memset(t[:], 0.0).then_inc(blank_ready, 1)
            for t in (s0, s1, pick0, pick1):
                pool.memset(t[:], EMPTY).then_inc(blank_ready, 1)
            pool.memset(gate_t[:].bitcast(F32), 0.0).then_inc(blank_ready, 1)
            pool.wait_ge(early_in, 16)
            trio = cut(ce, EARLY_AT, "trio")[0:STACK].rearrange("p (j d) -> p j d", d=HEAD)[:, :, 0:1]
            pool.tensor_copy(vb[:, :, :, TRIO * HEAD:].rearrange("p b g j -> p (b g) j"),
                             trio.rearrange("p j d -> p d j").broadcast_to([STACK, IMAGES * TRIOS, TRIO])
                             ).then_inc(ones_ready, 1)
            pool.wait_ge(blank_ready, 9)
            pool.wait_ge(att_hi_ready, 1)
            pool.tensor_tensor(a0[:, 1, :], a0_raw[:], a0[:, 0, :].bitcast(F32), ALU.subtract).then_inc(att_lo_ready, 1)
            norm_power(0)
            bias_rows(0, cut(ce, EARLY_AT, "bproj"))
            keys_rest(0)
            pool.wait_ge(mult_hi_ready, 1)
            pool.tensor_tensor(cm_lo[:], cm_raw[:, 0:MULT_SPLIT], cm_hi[:, 0:MULT_SPLIT].bitcast(F32),
                               ALU.subtract).then_inc(mult_lo_ready, 1)
            for e in range(EXPERTS0):
                pool.wait_ge(f0_in[e % 2], 16 * (e // 2 + 1))
                if e == 0:
                    pool.wait_ge(embed_done, 3)
                if e == 1:
                    pool.wait_ge(A[0]["v_done"], HALF_IMAGES)
                if e >= 2:
                    pool.wait_ge(down0_done, CHUNKS0 * (e - 1))
                split(f0_raw[:, e % 2, :], f0[:, e % 2, 0, :], f0[:, e % 2, 1, :], f0_hi_ready, e + 1, f0_lo_ready)
                if e == 1:
                    norm_power(1)
            pool.wait_ge(att1_in, 16)
            pool.wait_ge(A[0]["proj_done"], 3)
            split(a1_raw[:], a1[:, 0, :], a1[:, 1, :], att1_hi_ready, 1, att_lo_ready)
            norm_power(2)
            bias_rows(2, cut(cl, LATE_AT, "bproj1"))
            keys_rest(1)
            pool.wait_ge(down0_done, EXPERTS0 * CHUNKS0)

            def split_pair(q, i):
                first = isinstance(i, int)
                pool.wait_ge(f1_in[q], 16 if first else i * 16 + 16)
                if not first:
                    pool.wait_ge(lin_done, i * (2 * UNITS) + UNITS * (q - 1))
                split(f1_raw[:, q, 0:UP1_N], up1[:, q, 0, :], up1[:, q, 1, :], up1_hi,
                      q + 1 if first else i * 2 + (q + 1), up1_lo)
                if not first:
                    pool.wait_ge(down1_done, i * (2 * UNITS) + UNITS * (q - 1))
                split(f1_raw[:, q, UP1_N:], down1[:, q, 0, :], down1[:, q, 1, :], down1_hi,
                      q + 1 if first else i * 2 + (q + 1), down1_lo)

            split_pair(0, 0)
            pool.wait_ge(A[1]["v_done"], HALF_IMAGES)
            split_pair(1, 0)
            norm_power(3)
            power(rms_spread, 1, square, rms, rms_ready)
            pool.wait_ge(y_ready, TILES)
            pool.tensor_tensor(h[:], h[:], y[:], ALU.add).then_inc(h_biased, 1)
            with pool.Fori(1, PAIRS // 2) as i:
                split_pair(0, i)
                split_pair(1, i)

        @block.tensor
        def _(pe):
            def mm(o, lhs, rhs, start, stop):
                return pe.matmul(o, lhs, rhs, start=start, stop=stop, skip_group_check=True)

            def turn_rows(stage):
                if stage == 0:
                    pe.wait_ge(early_in, 16)
                for lo, hi, bank in ((0, 3, 3), (3, TILES, 4)):
                    pe.wait_ge(n_ready, TILES * stage + hi)
                    for t in range(lo, hi):
                        m, at = rows_of(t), (t - lo) * P
                        last = pe.transpose(ps[:, bank, at:at + m], n[0:m, t, 0:P], ident[0:m, 0:m])
                    last.then_inc(turned, 1)
                    for t in range(lo, hi):
                        m, at = rows_of(t), (t - lo) * P
                        last = pe.transpose(ps[0:REST, bank + 2, at:at + m], n[0:m, t, P:EMBED], ident[0:m, 0:m])
                    last.then_inc(turned, 1)

            def rows_product(w, chunk_at, ready, signal):
                for t in range(TILES):
                    if t in (0, 2):
                        pe.wait_ge(ready, 2 + t)
                    passes = features(t * P, rows_of(t))
                    for k, (stat, c, part) in enumerate(passes):
                        at = chunk_at[c]
                        last = mm(token_out(t), stat, w[:, part, at:at + EMBED], k == 0, k == len(passes) - 1)
                    if t % 2 or t == TILES - 1:
                        last.then_inc(signal, 1)

            def attention(layer, w, chunk, units):
                s = A[layer]
                stage = 2 * layer
                pe.wait_ge(att_lo_ready, layer + 1)

                def queries_keys(u):
                    if u >= 2:
                        pe.wait_ge(s["k_ready"] if layer else s["qk_read"], u - 1)
                    for hf in range(2):
                        if u == 0:
                            pe.wait_ge(x_lo_ready, 4 * stage + 2 + 2 * hf)
                        for k, (mov, c, part) in enumerate(features(hf * HALF, HALF)):
                            at = c * chunk + u * P
                            last = mm(ps[:, 3 + 2 * (u % 2) + hf, 0:HALF], w[:, part, at:at + P], mov, k == 0, k == 4)
                    last.then_inc(s["qk_done"], 1)

                def image_values(i):
                    if i >= 2:
                        pe.wait_ge(s["v_ready"], i - 1)
                    for j in range(2):
                        b = 2 * i + j
                        for k, (stat, c, part) in enumerate(((x3_hi, 0, 0), (x3_hi, 0, 1), (x3_rest, 1, 0),
                                                             (x3_rest, 1, 1), (x3_lo, 0, 0))):
                            at = c * chunk + units * P
                            last = mm(ps[0:STACK, 7 * (1 - i % 2), j * EMBED:(j + 1) * EMBED],
                                      stat[:, b, :], w[:, part, at:at + EMBED], k == 0, k == 4)
                    last.then_inc(s["v_done"], 1)

                for u in range(units):
                    queries_keys(u)
                pe.wait_ge(s["x3_act"], 2)
                pe.wait_ge(s["x3_dve"], 1)
                for i in range(HALF_IMAGES):
                    image_values(i)

                def scores(g):
                    group = GROUPS[g]
                    m = SEQ * len(group)
                    bank = 3 + g % 2
                    if g == 0:
                        pe.wait_ge(s["q_ready"], 8)
                        pe.wait_ge(s["keys_act"], HEADS_A)
                        pe.wait_ge(s["keys_pool"], 2)
                    if g >= 2:
                        pe.wait_ge(s["s_read"], g - 1)
                    if layer:
                        far, same = cut(cm_hi, MULT_AT, "far"), cut(cm_hi, MULT_AT, "same")
                        mm(ps[0:m, bank, 0:HEADS * SEQ], same[0:SEQ, 0:m], far[0:SEQ, :], True, False)
                    for j, b in enumerate(group):
                        last = j == len(group) - 1
                        mm(ps[0:m, bank, 0:HEADS_A * SEQ], qz_a[:, b, 0:m],
                           kb_a[:, b, :, :].rearrange("p h k -> p (h k)"), not layer and j == 0, last)
                        done = mm(ps[0:m, bank, HEADS_A * SEQ:HEADS * SEQ], qz_b[:, b, 0:m],
                                  kb_b[:, b, :, :].rearrange("p h k -> p (h k)"), False, last)
                    done.then_inc(s["s_done"], 1)

                def turn_probs(g):
                    m = SEQ * len(GROUPS[g])
                    pe.wait_ge(s["p_ready"], g + 1)
                    if g >= 2:
                        pe.wait_ge(s["pt_ready"], g - 1)
                    for r in range(TRIOS):
                        last = pe.transpose(ps[0:STACK, 5 + g % 2, r * STACK:r * STACK + m],
                                            probs[0:m, g % 2, r * TRIO:(r + 1) * TRIO, :].rearrange("p h k -> p (h k)"),
                                            ident[0:m, 0:m])
                    last.then_inc(s["pt_done"], 1)

                def values(g):
                    if g == 0:
                        pe.wait_ge(s["v_ready"], HALF_IMAGES)
                        pe.wait_ge(ones_ready, 1)
                    pe.wait_ge(s["pt_ready"], g + 1)
                    if g >= 2:
                        pe.wait_ge(s["o_ready"], g - 1)
                    for j, b in enumerate(GROUPS[g]):
                        bank, at = OUT_BANKS[g % 2][j // 2], (j % 2) * TRIOS * VCOLS
                        for r in range(TRIOS):
                            last = mm(ps[0:SEQ, bank, at + r * VCOLS:at + (r + 1) * VCOLS],
                                      probs_t[:, g % 2, r, j * SEQ:(j + 1) * SEQ], vb[:, b, r, :], True, True)
                    last.then_inc(s["o_done"], 1)

                def turn_outputs(k):
                    hf, rest = divmod(k, 2)
                    m, cols = (REST, slice(P, EMBED)) if rest else (P, slice(0, P))
                    if k == 0:
                        pe.wait_ge(s["o_ready"], len(GROUPS) // 2)
                    if k == 2:
                        pe.wait_ge(s["o_ready"], len(GROUPS))
                    pe.wait_ge(s["pt_ready"] if rest else s["s_read"], len(GROUPS) - 1 + hf)
                    for i in range(HALF_IMAGES):
                        last = pe.transpose(ps[0:m, 3 + 2 * rest + hf, i * SEQ:(i + 1) * SEQ],
                                            o_sb[:, hf * HALF_IMAGES + i, cols], ident[0:SEQ, 0:SEQ])
                    last.then_inc(s["ot_done"], 1)

                groups = len(GROUPS)
                for g in range(groups + 2):
                    if g < groups:
                        scores(g)
                    if g == groups:
                        turn_outputs(0)
                    if 1 <= g <= groups:
                        turn_probs(g - 1)
                    if g == groups + 1:
                        turn_outputs(1)
                    if g >= 2:
                        values(g - 2)
                turn_outputs(2)
                turn_outputs(3)
                rows_product(w, (2 * chunk, 2 * chunk + EMBED), s["ot_lo"], s["proj_done"])

            def gates(stage, name, experts):
                pe.wait_ge(mult_lo_ready, 1)
                for hf in range(2):
                    pe.wait_ge(x_lo_ready, 4 * stage + 2 + 2 * hf)
                    for k, (mov, c, part) in enumerate(features(hf * HALF, HALF)):
                        at = MULT_AT[name][0] + c * experts
                        last = mm(ps[0:experts, hf, 0:HALF], (cm_hi, cm_lo)[part][:, at:at + experts], mov, k == 0, k == 4)
                    last.then_inc(rows_done, 1)

            def turn_scores(layer, experts, signal):
                pe.wait_ge(rows_ready, 2 * (layer + 1))
                for t in range(TILES):
                    m = rows_of(t)
                    last = pe.transpose(ps[0:m, 7, t * experts:(t + 1) * experts], score_rows[0:experts, t * P:t * P + m],
                                        ident[0:experts, 0:experts])
                last.then_inc(signal, 1)

            def down(hi, lo, w_hi, w_lo, first, stop, before=None, signal=None):
                passes = list(enumerate(((hi, w_hi), (hi, w_lo), (lo, w_hi))))
                order = [(t, p) for t in range(TILES) for p in passes] if signal else [(t, p) for p in passes for t in range(TILES)]
                for t, (k, (stat, w)) in order:
                    if before and k == 0 and t % 2 == 0:
                        before(t)
                    last = mm(token_out(t), stat[:, t * P:t * P + rows_of(t)], w,
                              first and k == 0 and t % 2 == 0, stop and k == 2)
                    if signal and k == 2 and t % 2:
                        last.then_inc(signal, 1)
                return last

            for c in range(PATCH_CHUNKS):
                pe.wait_ge(px_lo_ready, c + 2)
                last = down(px_hi[:, c, :], px_lo[:, c, :], w_split[:, 0, c, :], w_split[:, 1, c, :], c == 0, c == PATCH_CHUNKS - 1,
                            signal=embed_done if c == PATCH_CHUNKS - 1 else None)
            last.then_inc(embed_done, 1)

            turn_rows(0)
            attention(0, a0, ATT0_CHUNK, len(QK0))
            turn_rows(1)
            gates(1, "gate", EXPERTS0)

            def up0(u):
                e, c = divmod(u, CHUNKS0)
                if c == 0:
                    pe.wait_ge(f0_lo_ready, e + 1)
                if u >= 2:
                    pe.wait_ge(hid0_ready, u - 1)
                for hf in range(2):
                    for k, (mov, ch, part) in enumerate(features(hf * HALF, HALF)):
                        at = ch * HIDDEN0 + c * P
                        last = mm(ps[:, 3 + 2 * (u % 2) + hf, 0:HALF], f0[:, e % 2, part, at:at + P], mov, k == 0, k == 4)
                last.then_inc(up0_done, 1)

            def down0(u):
                e, c = divmod(u, CHUNKS0)
                pe.wait_ge(hid0_lo_ready, u + 1)

                def free(t):
                    pe.wait_ge(y0_added, TILES * (e - 1) + min(t + 2, TILES))

                at = 2 * HIDDEN0 + c * EMBED
                down(hid0_hi[:, u % 4, :], hid0_lo[:, u % 4, :], f0[:, e % 2, 0, at:at + EMBED],
                     f0[:, e % 2, 1, at:at + EMBED], c == 0, c == CHUNKS0 - 1, before=free if c == 0 and e else None,
                     signal=sums_done if u == units0 - 1 else None).then_inc(down0_done, 1)

            units0 = EXPERTS0 * CHUNKS0
            for u in range(units0 + 2):
                if u < units0:
                    up0(u)
                if u == 0:
                    turn_scores(0, EXPERTS0, gate0_done)
                if u >= 2:
                    down0(u - 2)

            turn_rows(2)
            attention(1, a1, ATT1_CHUNK, len(QK1))
            turn_rows(3)
            gates(3, "gate1", EXPERTS1)
            def turn_gates():
                pe.wait_ge(gate_ready, 1)
                for t in range(TILES):
                    m = rows_of(t)
                    last = pe.transpose(ps[0:EXPERTS1, t // 4, (t % 4) * P:(t % 4) * P + m], gate[0:m, t, :], ident[0:m, 0:m])
                last.then_inc(gt_done, 1)

            def open_sums(part):
                b2 = (cm_hi, cm_lo)[part][0:GATE_ROWS, MULT_AT["b2"][0]:MULT_AT["b2"][1]]
                for t in range(TILES):
                    mm(token_out(t), gate_t[0:GATE_ROWS, t * P:t * P + rows_of(t)], b2, part == 0 and t % 2 == 0, False)

            def broadcast_gate(q, expert, hf, pair):
                count = pair * 4 + (2 * expert + hf)
                if not isinstance(count, int) or count > 0:
                    pe.wait_ge(bc_ready, count)
                at = UP1_N - 2 + expert
                pick = up1[0:GATE_ROWS, q, 0, at:at + 1].broadcast_to([GATE_ROWS, P])
                mm(ps[:, 7, 0:HALF], pick, gate_t[0:GATE_ROWS, hf * HALF:(hf + 1) * HALF], True, True).then_inc(bc_done, 1)

            def up1_unit(q, col, bank, signal):
                for hf in range(2):
                    for k, (mov, ch, part) in enumerate(features(hf * HALF, HALF)):
                        at = ch * 2 * UNITS * P + col * P
                        last = mm(ps[:, bank + hf, 0:HALF], up1[:, q, part, at:at + P], mov, k == 0, k == 4)
                last.then_inc(signal, 1)

            def down1_unit(slot, count, stop):
                pe.wait_ge(hid1_lo_ready, count)
                q, u = divmod(slot, UNITS)
                at = u * EMBED
                down(hid1_hi[:, slot, :], hid1_lo[:, slot, :], down1[:, q, 0, at:at + EMBED],
                     down1[:, q, 1, at:at + EMBED], False, stop,
                     signal=sums_done if stop else None).then_inc(down1_done, 1)

            def two_pairs(i):
                first = isinstance(i, int)
                for slot in range(2 * UNITS):
                    q, u = divmod(slot, UNITS)
                    unit = i * (2 * UNITS) + slot
                    pair = i * 2 + q
                    if u == 0:
                        pe.wait_ge(up1_lo, pair + 1)
                    if not (first and slot == 0):
                        pe.wait_ge(glu_ready, unit)
                    up1_unit(q, u, 3, glu_done)
                    if first and slot == 0:
                        turn_scores(1, EXPERTS1, gate1_done)
                    elif first and slot == 1:
                        turn_gates()
                    elif first and slot == 2:
                        broadcast_gate(q, 1, 1, pair)
                    elif not (first and slot == 0) and u < 2:
                        broadcast_gate(q, u, 0, pair)
                    if not (first and slot == 0):
                        pe.wait_ge(lin_read, unit)
                    up1_unit(q, UNITS + u, 5, lin_done)
                    if first and slot == 1:
                        pe.wait_ge(gt_lo, 2)
                        broadcast_gate(q, 0, 0, pair)
                        open_sums(0)
                        broadcast_gate(q, 0, 1, pair)
                        open_sums(1)
                        broadcast_gate(q, 1, 0, pair)
                    elif u < 2 and not (first and slot == 0):
                        broadcast_gate(q, u, 1, pair)
                    if not (first and slot < UNITS):
                        if u == 0:
                            pe.wait_ge(down1_lo, pair)
                        down1_unit((slot + UNITS) % (2 * UNITS), unit - (UNITS - 1), False)

            two_pairs(0)
            with pe.Fori(1, PAIRS // 2) as i:
                two_pairs(i)
            pe.wait_ge(down1_lo, PAIRS)
            for u in range(UNITS):
                down1_unit(UNITS + u, UNITS * (PAIRS - 1) + u + 1, u == UNITS - 1)

        @block.scalar
        def _(act):
            def copy(o, i):
                return act.activation(o, i, ACT.Copy)

            def feature_hi(stage):
                for k, (bank, lo, hi) in enumerate(TURNED):
                    act.wait_ge(turned, 4 * stage + k + 1)
                    m, dst = (REST, x_rest) if k % 2 else (P, x_hi)
                    copy(dst[0:m, lo:hi], ps[0:m, bank, 0:hi - lo]).then_inc(x_hi_ready, 1)

            def attention(layer):
                s = A[layer]
                act.wait_ge(x_lo_ready, 8 * layer + 4)
                for dst, src in ((x3_hi, x_hi), (x3_rest, x_rest)):
                    copy(dst[:].rearrange("p b (r k) -> p b r k", r=TRIO), thrice(src[:])).then_inc(s["x3_act"], 1)
                act.wait_ge(s["k_ready"], 1)
                for hd in range(HEADS_A):
                    act.activation(kb_a[:, :, hd, :], k_a[:].rearrange("p (b k) -> p b k", k=SEQ), ACT.Copy,
                                   scale=ce[:, EARLY_AT["head"][0] + hd:EARLY_AT["head"][0] + hd + 1]).then_inc(s["keys_act"], 1)

                def soften(g):
                    m = SEQ * len(GROUPS[g])
                    act.wait_ge(s["s_read"], g + 1)
                    act.activation(probs[0:m, g % 2], probs[0:m, g % 2], ACT.Exp, scale=SCALE).then_inc(s["p_ready"], 1)

                def keep_turned(g):
                    m = SEQ * len(GROUPS[g])
                    act.wait_ge(s["pt_done"], g + 1)
                    if g >= 2:
                        act.wait_ge(s["o_done"], g - 1)
                    copy(probs_t[:, g % 2, :, 0:m],
                         ps[0:STACK, 5 + g % 2, 0:TRIOS * STACK].rearrange("p (r c) -> p r c", c=STACK)[:, :, 0:m]
                         ).then_inc(s["pt_ready"], 1)

                for g in range(len(GROUPS) + 1):
                    if g < len(GROUPS):
                        soften(g)
                    if g:
                        keep_turned(g - 1)
                for k in range(4):
                    hf, rest = divmod(k, 2)
                    act.wait_ge(s["ot_done"], k + 1)
                    m = REST if rest else P
                    dst = (x_rest if rest else x_hi)[0:m, hf * HALF:(hf + 1) * HALF]
                    src = ps[0:m, 3 + 2 * rest + hf, 0:HALF]
                    if layer:
                        copy(dst, src).then_inc(s["ot_hi"], 1)
                    else:
                        at = EARLY_AT["bv"][0] + rest
                        act.activation(dst, src, ACT.Identity, bias=ce[0:m, at:at + 1]).then_inc(s["ot_hi"], 1)

            def keep_rows(layer, experts):
                for hf in range(2):
                    act.wait_ge(rows_done, 2 * layer + hf + 1)
                    copy(score_rows[0:experts, hf * HALF:(hf + 1) * HALF], ps[0:experts, hf, 0:HALF]).then_inc(rows_ready, 1)

            act.wait_ge(wraw_in, 16)
            copy(w_split[:, 0], w_raw[:]).then_inc(px_hi_ready, 1)
            for c in range(PATCH_CHUNKS):
                act.wait_ge(px_in[c], 16)
                copy(px_hi[:, c, :], px_raw[:, c, :]).then_inc(px_hi_ready, 1)
            act.wait_ge(early_in, 16)
            act.wait_ge(att0_in, 16)
            copy(a0[:, 0, :], a0_raw[:]).then_inc(att_hi_ready, 1)
            act.wait_ge(mult_in, 16)
            copy(cm_hi[:], cm_raw[:]).then_inc(mult_hi_ready, 1)

            feature_hi(0)
            attention(0)
            feature_hi(1)
            keep_rows(0, EXPERTS0)
            act.wait_ge(late_in, 16)
            for u in range(EXPERTS0 * CHUNKS0):
                act.wait_ge(up0_done, u + 1)
                if u >= 2:
                    act.wait_ge(hid0_lo_ready, u - 1)
                act.activation(halves(hid0[:, u % 2, :]), ps[:, 3 + 2 * (u % 2):5 + 2 * (u % 2), 0:HALF], ACT.Gelu,
                               bias=cl[:, LATE_AT["b1"][0] + u:LATE_AT["b1"][0] + u + 1]).then_inc(hid0_ready, 1)
            feature_hi(2)
            attention(1)
            feature_hi(3)
            keep_rows(1, EXPERTS1)
            act.wait_ge(gap_ready, 1)
            act.activation(gate[:], gate[:], ACT.Exp).then_inc(exp_ready, 1)

            def turned_gates():
                act.wait_ge(blank_ready, 9)
                act.wait_ge(gt_done, 1)
                copy(gate_t[0:EXPERTS1, 0:4 * P], ps[0:EXPERTS1, 0, 0:4 * P]).then_inc(gt_hi, 1)
                copy(gate_t[0:EXPERTS1, 4 * P:], ps[0:EXPERTS1, 1, 0:LAST]).then_inc(gt_hi, 1)

            def two_pairs(i):
                first = isinstance(i, int)
                for slot in range(2 * UNITS):
                    q, u = divmod(slot, UNITS)
                    unit = i * (2 * UNITS) + slot
                    pair = i * 2 + q

                    def keep_gate(expert, hf):
                        act.wait_ge(bc_done, pair * 4 + (2 * expert + hf + 1))
                        cols, mix = slice(hf * HALF, (hf + 1) * HALF), slice(expert * REST, (expert + 1) * REST)
                        if hf == 0 and not (first and q == 0):
                            act.wait_ge(hid1_ready, pair * UNITS - (2 - expert))
                        copy(gate_bc[:, expert, cols], ps[:, 7, 0:HALF])
                        copy(gate_bc[mix, 2 + q, cols], ps[mix, 7, 0:HALF]).then_inc(bc_ready, 1)

                    late = first and q == 0
                    if u < 2 and not late:
                        keep_gate(u, 0)
                    if first and slot == 1:
                        turned_gates()
                    act.wait_ge(glu_ready, unit + 1)
                    if not (first and slot < 2):
                        act.wait_ge(prod_ready, unit - 1)
                    act.activation(act1[:, slot % 2, :], glu[:, slot % 2, :], ACT.Gelu_apprx_sigmoid).then_inc(act1_ready, 1)
                    if late and slot == 2:
                        keep_gate(1, 1)
                    act.wait_ge(lin_done, unit + 1)
                    at = UNITS + q * 2 * UNITS + u
                    column = lin_b1[:, at:at + 1] if first else lin_b1[:, bass.ds(i * (4 * UNITS) + at, 1)]
                    act.activation(halves(lin[:, slot % 2, :]), ps[:, 5:7, 0:HALF], ACT.Identity, bias=column).then_inc(lin_read, 1)
                    if late and slot == 1:
                        keep_gate(0, 0)
                        keep_gate(0, 1)
                        keep_gate(1, 0)
                    if u < 2 and not late:
                        keep_gate(u, 1)
                    if not (first and slot == 0):
                        hidden_hi((slot - 1) % (2 * UNITS), unit, first and slot <= 2 * UNITS)

            def hidden_hi(slot, count, free):
                act.wait_ge(hid1_ready, count)
                if not free:
                    act.wait_ge(down1_done, count - 2 * UNITS)
                copy(hid1_hi[:, slot, :], hid1[:, slot % 2, :]).then_inc(hid1_hi_ready, 1)

            act.wait_ge(lin_b1_ready, 1)
            two_pairs(0)
            with act.Fori(1, PAIRS // 2) as i:
                two_pairs(i)
            hidden_hi(2 * UNITS - 1, UNITS * PAIRS, False)

        @block.vector
        def _(dve):
            sub, add, mult = ALU.subtract, ALU.add, ALU.mult

            def tt(o, a, b, op):
                return dve.tensor_tensor(o, a, b, op)

            def norm(stage, add_bank):
                var = moments[:, :, 1]

                def tile_stats(t):
                    dve.wait_ge(h_ready, 3 * stage + t // 2 + 1)
                    dve.bn_stats(stats[:, t, :], h[:, t, :]).then_inc(stats_ready, 1)

                def tile_moments(t):
                    dve.wait_ge(stats_ready, TILES * stage + t + 1)
                    dve.bn_aggr(moments[:, t, :], stats[:, t, :]).then_inc(moments_ready, 1)

                def part_spread(k):
                    lo, hi = PARTS[k]
                    dve.wait_ge(moments_ready, TILES * stage + hi)
                    dve.tensor_scalar(spread[:, lo:hi], var[:, lo:hi], EPS, None, add).then_inc(spread_ready, 1)

                add_bank(0)
                tile_stats(0)
                tile_stats(1)
                add_bank(1)
                tile_moments(0)
                tile_moments(1)
                tile_stats(2)
                tile_stats(3)
                tile_moments(2)
                tile_moments(3)
                part_spread(0)
                add_bank(2)
                tile_stats(4)
                tile_moments(4)
                part_spread(1)
                for k, (lo, hi) in enumerate(PARTS):
                    dve.wait_ge(rstd_ready, 2 * stage + k + 1)
                    if stage == 3:
                        tt(square[:, lo:hi], var[:, lo:hi], rstd[:, lo:hi], mult).then_inc(square_ready, 1)
                        dve.wait_ge(square_ready, 2 * k + 1)
                        tt(square[:, lo:hi], square[:, lo:hi], rstd[:, lo:hi], mult).then_inc(square_ready, 1)
                        dve.wait_ge(square_ready, 2 * k + 2)
                        dve.tensor_scalar(square[:, lo:hi], square[:, lo:hi], EPS, None, add).then_inc(rms_spread, 1)
                    for t in range(lo, hi):
                        row = dve.tensor_scalar((y if stage == 3 else n)[:, t, :], h[:, t, :], moments[:, t, 0:1], rstd[:, t:t + 1], sub, mult)
                        row.then_inc(y_ready if stage == 3 else n_ready, 1)
                if stage < 3:
                    return
                dve.wait_ge(late_in, 16)
                for k, (lo, hi) in enumerate(PARTS):
                    dve.wait_ge(rms_ready, k + 1)
                    for t in range(lo, hi):
                        dve.wait_ge(y_ready, t + 1)
                        dve.scalar_tensor_tensor(out=n[:, t, :], in0=y[:, t, :], scalar=rms[:, t:t + 1],
                                                 in1=cut(cl, LATE_AT, "scale"), op0=mult, op1=mult).then_inc(n_ready, 1)

            def bank_rows(tensor, k):
                if k == 2:
                    return tensor[0:LAST, TILES - 1, :]
                return tensor[:, 2 * k:2 * k + 2, :].rearrange("p t c -> p (t c)")

            def bank_sums(k):
                return last_out if k == 2 else ps[:, k, 0:2 * EMBED]

            def feature_lo(stage):
                for k, (bank, lo, hi) in enumerate(TURNED):
                    dve.wait_ge(x_hi_ready, 4 * stage + k + 1)
                    m = REST if k % 2 else P
                    hi_part = (x_rest if k % 2 else x_hi)[0:m, lo:hi]
                    dst = x_rest[REST:P, lo:hi] if k % 2 else x_lo[:, lo:hi]
                    tt(dst, ps[0:m, bank, 0:hi - lo], hi_part.bitcast(F32), sub).then_inc(x_lo_ready, 1)

            def diagonal(qz, b, groups, each):
                whole = qz[:, b:b + groups * each, :]
                steps = [list(p) for p in whole.ap]
                return bass.AP(whole.tensor, whole.offset,
                               [steps[0], [each * STACK, groups], [STACK + SEQ, each], [1, SEQ]])

            def place(ap, b, groups, each):
                return ap[:, b * SEQ:(b + groups * each) * SEQ].rearrange("p (g j k) -> p g j k", g=groups, k=SEQ)

            def attention(layer):
                s = A[layer]
                dve.wait_ge(x_lo_ready, 8 * layer + 4)
                dve.tensor_copy(x3_lo[:].rearrange("p b (r k) -> p b r k", r=TRIO), thrice(x_lo[:])).then_inc(s["x3_dve"], 1)

                def keep_values():
                    trio = cut(ce, EARLY_AT, "trio")[0:STACK]
                    for i in range(HALF_IMAGES):
                        dve.wait_ge(s["v_done"], i + 1)
                        tt(vb[:, 2 * i:2 * i + 2, :, 0:TRIO * HEAD].rearrange("p b g c -> p (b g) c"),
                           ps[0:STACK, 7 * (1 - i % 2), 0:2 * EMBED].rearrange("p (g c) -> p g c", c=TRIO * HEAD),
                           trio.unsqueeze(1).broadcast_to([STACK, 2 * TRIOS, TRIO * HEAD]), mult).then_inc(s["v_ready"], 1)

                if layer == 0:
                    cos = cut(ce, EARLY_AT, "cos").unsqueeze(1).broadcast_to([P, 2, HALF])
                    sin = cut(ce, EARLY_AT, "sin").unsqueeze(1).broadcast_to([P, 2, HALF])

                    def rotate(p):
                        if p == 1:
                            dve.wait_ge(s["k_ready"], 1)
                        if p == 2:
                            dve.wait_ge(s["q_ready"], 4)
                        for k, (dst, table) in enumerate(((turn1, cos), (turn2, sin))):
                            u = 2 * p + k
                            dve.wait_ge(s["qk_done"], u + 1)
                            dve.scalar_tensor_tensor(
                                out=halves(dst[:]), in0=ps[:, 3 + 2 * k:5 + 2 * k, 0:HALF],
                                scalar=ce[:, EARLY_AT["bqk"][0] + u:EARLY_AT["bqk"][0] + u + 1], in1=table,
                                op0=add, op1=mult).then_inc(s["qk_read"], 1)
                        dve.wait_ge(s["qk_read"], 2 * p + 2)

                    dve.wait_ge(blank_ready, 9)
                    rotate(0)
                    tt(k_a[:], turn1[:], turn2[:], add).then_inc(s["k_ready"], 1)
                    rotate(1)
                    tt(k_b[:], turn1[REST:P, :], turn2[REST:P, :], add).then_inc(s["k_ready"], 1)
                    for hf in range(2):
                        for b, g, e in ((hf * 8, 2, 3), (hf * 8 + 6, 1, 2)):
                            tt(diagonal(qz_b, b, g, e), place(turn1[0:REST, :], b, g, e), place(turn2[0:REST, :], b, g, e), add
                               ).then_inc(s["q_ready"], 1)
                    rotate(2)
                    for hf in range(2):
                        for b, g, e in ((hf * 8, 2, 3), (hf * 8 + 6, 1, 2)):
                            tt(diagonal(qz_a, b, g, e), place(turn1[:], b, g, e), place(turn2[:], b, g, e), add
                               ).then_inc(s["q_ready"], 1)
                else:
                    dve.wait_ge(s["qk_done"], 1)
                    dve.tensor_copy(halves(k_a[:]), ps[:, 3:5, 0:HALF]).then_inc(s["k_ready"], 1)
                    dve.wait_ge(s["qk_done"], 2)
                    dve.tensor_copy(halves(k_b[:]), ps[REST:P, 5:7, 0:HALF]).then_inc(s["k_ready"], 1)
                    for hf in range(2):
                        for b, g, e in ((0, 2, 3), (6, 1, 2)):
                            dve.tensor_copy(diagonal(qz_b, hf * 8 + b, g, e), place(ps[0:REST, 5 + hf, 0:HALF], b, g, e)
                                            ).then_inc(s["q_ready"], 1)
                    dve.wait_ge(s["qk_done"], 3)
                    for hf in range(2):
                        for b, g, e in ((0, 2, 3), (6, 1, 2)):
                            dve.tensor_copy(diagonal(qz_a, hf * 8 + b, g, e), place(ps[:, 3 + hf, 0:HALF], b, g, e)
                                            ).then_inc(s["q_ready"], 1)
                keep_values()

                def center(g):
                    m = SEQ * len(GROUPS[g])
                    sc = ps[0:m, 3 + g % 2, 0:HEADS * SEQ].rearrange("p (h k) -> p h k", k=SEQ)
                    dve.wait_ge(s["s_done"], g + 1)
                    dve.tensor_reduce(o_max[0:m, g % 2, :], sc, AX_X, ALU.max).then_inc(s["max_ready"], 1)
                    dve.wait_ge(s["max_ready"], g + 1)
                    if g >= 2:
                        dve.wait_ge(s["pt_done"], g - 1)
                    tt(probs[0:m, g % 2], sc, o_max[0:m, g % 2, :].unsqueeze(2).broadcast_to([m, HEADS, SEQ]), sub
                       ).then_inc(s["s_read"], 1)

                def divide(g):
                    dve.wait_ge(s["o_done"], g + 1)
                    if g:
                        dve.wait_ge(s["o_ready"], g)
                    group = GROUPS[g]
                    parts = [(0, 2)] + [(2, 1)] * (len(group) == 3)
                    for k, (j, cnt) in enumerate(parts):
                        o = ps[0:SEQ, OUT_BANKS[g % 2][k], 0:cnt * TRIOS * VCOLS].rearrange("p (r c) -> p r c", c=VCOLS)
                        ins = dve.reciprocal(o_div[:, j:j + cnt].rearrange("p b r t -> p (b r) t"), o[:, :, TRIO * HEAD:])
                    ins.then_inc(s["div_ready"], 1)
                    dve.wait_ge(s["div_ready"], g + 1)
                    for k, (j, cnt) in enumerate(parts):
                        o = ps[0:SEQ, OUT_BANKS[g % 2][k], 0:cnt * TRIOS * VCOLS].rearrange("p (r c) -> p r c", c=VCOLS)
                        b = group[0] + j
                        ins = tt(o_sb[:, b:b + cnt, :].rearrange("p b (r t d) -> p (b r) t d", t=TRIO, d=HEAD),
                                 o[:, :, 0:TRIO * HEAD].rearrange("p r (t d) -> p r t d", d=HEAD),
                                 o_div[:, j:j + cnt].rearrange("p b r t -> p (b r) t").unsqueeze(3)
                                 .broadcast_to([SEQ, cnt * TRIOS, TRIO, HEAD]), mult)
                    ins.then_inc(s["o_ready"], 1)

                for g in range(len(GROUPS) + 2):
                    if g < len(GROUPS):
                        center(g)
                    if g >= 2:
                        divide(g - 2)
                for k in range(4):
                    hf, rest = divmod(k, 2)
                    dve.wait_ge(s["ot_hi"], k + 1)
                    m = REST if rest else P
                    cols = slice(hf * HALF, (hf + 1) * HALF)
                    src = ps[0:m, 3 + 2 * rest + hf, 0:HALF]
                    hi_part = (x_rest if rest else x_hi)[0:m, cols].bitcast(F32)
                    dst = x_rest[REST:P, cols] if rest else x_lo[:, cols]
                    if layer:
                        tt(dst, src, hi_part, sub).then_inc(s["ot_lo"], 1)
                    else:
                        at = EARLY_AT["bv"][0] + rest
                        dve.scalar_tensor_tensor(out=dst, in0=src, scalar=ce[0:m, at:at + 1], in1=hi_part, op0=add, op1=sub
                                                 ).then_inc(s["ot_lo"], 1)

            def add_output(layer):
                def add_bank(k):
                    if k == 0:
                        dve.wait_ge(h_biased, layer + 1)
                    dve.wait_ge(A[layer]["proj_done"], k + 1)
                    tt(bank_rows(h, k), bank_sums(k), bank_rows(h, k), add).then_inc(h_ready, 1)
                return add_bank

            dve.memset(h[:, TILES - 1, :], 0.0).then_inc(h_blank, 1)
            dve.wait_ge(px_hi_ready, 1)
            tt(w_split[:, 1], w_raw[:], w_split[:, 0].bitcast(F32), sub).then_inc(px_lo_ready, 1)
            for c in range(PATCH_CHUNKS):
                dve.wait_ge(px_hi_ready, c + 2)
                tt(px_lo[:, c, :], px_raw[:, c, :], px_hi[:, c, :].bitcast(F32), sub).then_inc(px_lo_ready, 1)
            dve.wait_ge(early_in, 16)
            dve.wait_ge(start_in, 16)
            dve.wait_ge(h_blank, 1)

            def add_start(k):
                dve.wait_ge(embed_done, k + 1)
                tt(bank_rows(h, k), bank_sums(k), bank_rows(start_rows, k), add).then_inc(h_ready, 1)

            norm(0, add_start)
            feature_lo(0)
            attention(0)

            norm(1, add_output(0))
            feature_lo(1)

            def shifted(raw, experts, dst, bias, sem_):
                for lo, hi, m in ((0, 4, P), (4, 5, LAST)):
                    tt(dst[0:m, lo:hi, 0:experts], raw[0:m, lo * experts:hi * experts].rearrange("p (t e) -> p t e", e=experts),
                       bias[0:m].unsqueeze(1).broadcast_to([m, hi - lo, experts]), add).then_inc(sem_, 1)

            def first_ones(scores, picks, left, count, ready, ready_at, tops, picked, lefts):
                dve.wait_ge(ready, ready_at)
                for t in range(TILES):
                    dve.max(top8[:, t, :], scores[:, t, :]).then_inc(tops, 1)
                dve.wait_ge(tops, TILES)
                dve.tensor_copy(picks[:, :, 0:count], top8[:, :, 0:count]).then_inc(picked, 1)
                dve.wait_ge(picked, 1)
                for t in range(TILES):
                    dve.match_replace(left[:, t, :], picks[:, t, :], scores[:, t, :], TAKEN).then_inc(lefts, 1)
                dve.wait_ge(lefts, TILES)

            def choose():
                dve.wait_ge(gate0_done, 1)
                dve.wait_ge(late_in, 16)
                shifted(ps[:, 7, :], EXPERTS0, s0, cut(cl, LATE_AT, "gate_b"), s0_raw)
                dve.wait_ge(s0_raw, 2)
                tt(s0[:, :, 0:EXPERTS0], s0[:, :, 0:EXPERTS0],
                   cut(cl, LATE_AT, "center").unsqueeze(1).broadcast_to([P, TILES, EXPERTS0]), sub).then_inc(s0_ready, 1)
                first_ones(s0, pick0, s0_left, 1, s0_ready, 1, top0_ready, pick0_ready, left0_ready)
                tt(chosen[:], s0_left[:, :, 0:EXPERTS0], s0[:, :, 0:EXPERTS0], ALU.not_equal).then_inc(chosen_ready, 1)

            def split_hidden0(u):
                dve.wait_ge(hid0_ready, u + 1)
                if u >= 4:
                    dve.wait_ge(down0_done, u - 3)
                dve.tensor_copy(hid0_hi[:, u % 4, :], hid0[:, u % 2, :]).then_inc(hid0_hi_ready, 1)
                dve.wait_ge(hid0_hi_ready, u + 1)
                tt(hid0_lo[:, u % 4, :], hid0[:, u % 2, :], hid0_hi[:, u % 4, :].bitcast(F32), sub).then_inc(hid0_lo_ready, 1)

            b2 = cut(cl, LATE_AT, "b2").rearrange("p (e c) -> p e c", c=EMBED)

            def add_bias(e):
                dve.wait_ge(chosen_ready, 1)
                dve.wait_ge(h_biased, 1)
                for t in range(TILES):
                    m = rows_of(t)
                    if e:
                        dve.wait_ge(y0_added, TILES * (e - 1) + t + 1)
                    dve.scalar_tensor_tensor(out=h[0:m, t, :], in0=b2[0:m, e, :], scalar=chosen[0:m, t, e:e + 1],
                                             in1=h[0:m, t, :], op0=mult, op1=add).then_inc(b2_added, 1)

            def add_expert(e, t, signal):
                m = rows_of(t)
                dve.wait_ge(b2_added, TILES * e + t + 1)
                dve.scalar_tensor_tensor(out=h[0:m, t, :], in0=token_out(t), scalar=chosen[0:m, t, e:e + 1],
                                         in1=h[0:m, t, :], op0=mult, op1=add).then_inc(signal, 1)

            for u in range(EXPERTS0 * CHUNKS0):
                e, c = divmod(u, CHUNKS0)
                split_hidden0(u)
                if u == 1:
                    choose()
                if c == 1 and e:
                    dve.wait_ge(down0_done, CHUNKS0 * e)
                    for t in range(TILES):
                        add_expert(e - 1, t, y0_added)
                if c == 3:
                    add_bias(e)

            def add_last_expert(k):
                if k < 2:
                    dve.wait_ge(sums_done, k + 1)
                    add_expert(EXPERTS0 - 1, 2 * k, last_added)
                    add_expert(EXPERTS0 - 1, 2 * k + 1, h_ready)
                else:
                    dve.wait_ge(down0_done, EXPERTS0 * CHUNKS0)
                    add_expert(EXPERTS0 - 1, TILES - 1, h_ready)

            norm(2, add_last_expert)
            feature_lo(2)
            attention(1)

            norm(3, add_output(1))
            feature_lo(3)
            b1 = cut(cl, LATE_AT, "pair_b1")
            dve.tensor_scalar(lin_b1[:], b1, 1.0, None, add).then_inc(lin_b1_ready, 1)
            dve.wait_ge(gate1_done, 1)
            shifted(ps[:, 7, :], EXPERTS1, s1, cut(cl, LATE_AT, "gate1_b"), s1_ready)
            first_ones(s1, pick1, s1_left, TOP, s1_ready, 2, top1_ready, pick1_ready, left1_ready)
            tt(among[:], s1_left[:, :, 0:EXPERTS1], s1[:, :, 0:EXPERTS1], ALU.not_equal).then_inc(among_ready, 1)
            tt(gate[:], s1[:, :, 0:EXPERTS1], top8[:, :, 0:1].broadcast_to([P, TILES, EXPERTS1]), sub).then_inc(gap_ready, 1)
            dve.wait_ge(exp_ready, 1)
            dve.wait_ge(among_ready, 1)
            tt(gate[:], gate[:], among[:], mult).then_inc(weigh_ready, 1)
            dve.wait_ge(weigh_ready, 1)
            dve.tensor_reduce(gate_sum[:], gate[:], AX_X, add).then_inc(gsum_ready, 1)
            dve.wait_ge(gsum_ready, 1)
            dve.reciprocal(gate_sum[:], gate_sum[:]).then_inc(grec_ready, 1)
            dve.wait_ge(grec_ready, 1)
            tt(gate[:], gate[:], gate_sum[:].unsqueeze(2).broadcast_to([P, TILES, EXPERTS1]), mult).then_inc(gate_ready, 1)

            def gates_lo():
                dve.wait_ge(gt_hi, 1)
                tt(gate_t[32:32 + EXPERTS1, 0:4 * P], ps[0:EXPERTS1, 0, 0:4 * P], gate_t[0:EXPERTS1, 0:4 * P].bitcast(F32), sub
                   ).then_inc(gt_lo, 1)
                dve.wait_ge(gt_hi, 2)
                tt(gate_t[32:32 + EXPERTS1, 4 * P:], ps[0:EXPERTS1, 1, 0:LAST], gate_t[0:EXPERTS1, 4 * P:].bitcast(F32), sub
                   ).then_inc(gt_lo, 1)

            def hidden(slot, count):
                dve.wait_ge(lin_read, count)
                part = lin[:, slot % 2, :]
                dve.tensor_scalar(part, part, LIMIT + 1.0, 1.0 - LIMIT, ALU.min, ALU.max).then_inc(lin_ready, 1)
                dve.wait_ge(act1_ready, count)
                dve.wait_ge(lin_ready, count)
                tt(prod[:], part, act1[:, slot % 2, :], mult).then_inc(prod_ready, 1)
                dve.wait_ge(prod_ready, count)

            def weigh(slot, pair):
                q, u = divmod(slot, UNITS)
                dve.wait_ge(bc_ready, pair * 4 + (2 if u == 0 else 4))
                tt(hid1[:, slot % 2, :], prod[:], gate_bc[:, (0, 1, 2 + q)[u], :], mult).then_inc(hid1_ready, 1)

            def hidden_lo(slot, count):
                dve.wait_ge(hid1_hi_ready, count)
                tt(hid1_lo[:, slot, :], hid1[:, slot % 2, :], hid1_hi[:, slot, :].bitcast(F32), sub).then_inc(hid1_lo_ready, 1)

            def two_pairs(i):
                first = isinstance(i, int)
                for slot in range(2 * UNITS):
                    q, u = divmod(slot, UNITS)
                    unit = i * (2 * UNITS) + slot
                    at = q * 2 * UNITS + u
                    if not (first and slot < 2):
                        dve.wait_ge(act1_ready, unit - 1)
                    dve.wait_ge(glu_done, unit + 1)
                    column = b1[:, at:at + 1] if first else cl[:, bass.ds(i * (4 * UNITS) + (LATE_AT["pair_b1"][0] + at), 1)]
                    dve.tensor_scalar(halves(glu[:, slot % 2, :]), ps[:, 3:5, 0:HALF], column, LIMIT, add, ALU.min
                                      ).then_inc(glu_ready, 1)
                    if first and slot == 1:
                        gates_lo()
                    if not (first and slot < 2):
                        hidden_lo((slot - 2) % (2 * UNITS), unit - 1)
                    if not (first and slot == 0):
                        earlier = (slot - 1) % (2 * UNITS)
                        hidden(earlier, unit)
                        weigh(earlier, i * 2 + (slot - 1) // UNITS)

            two_pairs(0)
            with dve.Fori(1, PAIRS // 2) as i:
                two_pairs(i)
            hidden(2 * UNITS - 1, UNITS * PAIRS)
            hidden_lo(2 * UNITS - 2, UNITS * PAIRS - 1)
            weigh(2 * UNITS - 1, PAIRS - 1)
            hidden_lo(2 * UNITS - 1, UNITS * PAIRS)
            dve.wait_ge(h_biased, 3)
            for k in range(3):
                if k < 2:
                    dve.wait_ge(sums_done, 2 + k + 1)
                else:
                    dve.wait_ge(down1_done, UNITS * PAIRS)
                tt(bank_rows(n, k), bank_sums(k), bank_rows(h, k), add).then_inc(result_ready, 1)


TURNED = [(3, 0, 3 * P), (5, 0, 3 * P), (4, 3 * P, TOKENS), (6, 3 * P, TOKENS)]
OUT_BANKS = [(7, 0), (1, 2)]
PARTS = [(0, TILES - 1), (TILES - 1, TILES)]
GATE_ROWS = 32 + EXPERTS1


def kernel(x, cls_tok, L0_tok_W_proj, L0_tok_b_proj, L0_attn_w_qkv, L0_attn_b_qkv, L0_attn_w_proj,
           L0_attn_b_proj, L0_ffn_gate_w, L0_ffn_gate_b, L0_ffn_gate_center, L0_ffn_w1, L0_ffn_b1,
           L0_ffn_w2, L0_ffn_b2, L1_attn_w_qkv, L1_attn_w_proj, L1_attn_b_proj, L1_ffn_scale,
           L1_ffn_gate_w, L1_ffn_gate_b, L1_ffn_w1, L1_ffn_b1, L1_ffn_w2, L1_ffn_b2):
    import numpy as np
    import concourse.bacc as bacc
    from concourse.bass_utils import run_bass_kernel_spmd

    f32 = np.float32
    arr = {k: np.asarray(v) for k, v in locals().items() if k.startswith("L")}

    def chunked(w):
        return np.stack([w[:P], np.concatenate([w[P:], w[P:]])], axis=1)

    def rows(v):
        return np.broadcast_to(v.reshape(1, -1), (P, v.size))

    px = np.asarray(x).reshape(IMAGES, CHANNELS, SIDE, PATCH, SIDE, PATCH).transpose(1, 3, 5, 0, 2, 4)
    px = px.reshape(PATCH_CHUNKS * P, IMAGES, SEQ - 1)
    px = np.concatenate([np.zeros((PATCH_CHUNKS * P, IMAGES, 1), f32), px], axis=2)
    px = px.reshape(PATCH_CHUNKS, P, TOKENS)
    w_embed = arr["L0_tok_W_proj"].T.reshape(PATCH_CHUNKS, P, EMBED).transpose(1, 0, 2)
    start = np.concatenate([np.asarray(cls_tok).reshape(1, EMBED),
                            np.broadcast_to(arr["L0_tok_b_proj"], (SEQ - 1, EMBED))])
    start = np.concatenate([np.tile(start, (IMAGES, 1)), np.zeros((TILES * P - TOKENS, EMBED), f32)])
    start = start.reshape(TILES, P, EMBED).transpose(1, 0, 2)

    inv = f32(1.0) / f32(10000.0) ** (np.arange(0, HEAD, 2, dtype=f32) / f32(HEAD))
    angle = (np.arange(SEQ, dtype=f32)[:, None] * inv[None, :]).astype(f32)
    cos, sin = np.cos(angle), np.sin(angle)
    cos = np.concatenate([cos, cos], axis=1).T.astype(f32)
    sin = np.concatenate([-sin, sin], axis=1).T.astype(f32)
    cos, sin = (np.tile(t, (P // HEAD, HALF_IMAGES)) for t in (cos, sin))

    part = np.arange(P)
    head = (part[:, None] // HEAD == np.arange(HEADS_A)[None, :]).astype(f32)
    trio = (part[:, None] // SEQ == np.arange(TRIO * HEAD)[None, :] // HEAD).astype(f32)

    turn = np.arange(EMBED).reshape(HEADS, 2, HEAD // 2)[:, ::-1].reshape(-1)
    w_qkv, b_qkv = arr["L0_attn_w_qkv"], arr["L0_attn_b_qkv"]
    q0, k0 = np.arange(P), EMBED + np.arange(P)
    rest = np.concatenate([np.arange(P, EMBED), EMBED + np.arange(P, EMBED)])
    t2 = np.concatenate([turn, EMBED + turn])
    units0 = [k0, t2[k0], rest, t2[rest], q0, t2[q0]]
    cols0 = np.concatenate(units0 + [2 * EMBED + np.arange(EMBED)])
    bqk = np.stack([b_qkv[u] for u in units0], axis=1)
    bv = b_qkv[2 * EMBED:]
    bv = np.stack([bv[:P], np.concatenate([bv[P:], bv[P:]])], axis=1)
    att0 = np.concatenate([chunked(w_qkv.T[:, cols0]).reshape(P, -1),
                           chunked(arr["L0_attn_w_proj"].T).reshape(P, -1)], axis=1)
    cols1 = np.concatenate([k0, rest, q0, 2 * EMBED + np.arange(EMBED)])
    att1 = np.concatenate([chunked(arr["L1_attn_w_qkv"][:, cols1]).reshape(P, -1),
                           chunked(arr["L1_attn_w_proj"]).reshape(P, -1)], axis=1)

    early = np.concatenate([np.eye(P, dtype=f32), cos, sin, head, trio, bqk, bv,
                            rows(arr["L0_attn_b_proj"])], axis=1)

    ffn0 = np.stack([
        np.concatenate([chunked(arr["L0_ffn_w1"][e]).reshape(P, -1),
                        arr["L0_ffn_w2"][e].reshape(CHUNKS0, P, EMBED).transpose(1, 0, 2).reshape(P, -1)], axis=1)
        for e in range(EXPERTS0)])
    b1 = arr["L0_ffn_b1"].reshape(EXPERTS0 * CHUNKS0, P).T

    def paired(a, b):
        out_ = []
        for lo in (0, EMBED):
            out_ += [a[..., lo:lo + P], b[..., lo:lo + P], a[..., lo + P:lo + EMBED], b[..., lo + P:lo + EMBED]]
        return np.concatenate(out_, axis=-1)

    up, b1_1, w2_1 = arr["L1_ffn_w1"], arr["L1_ffn_b1"], arr["L1_ffn_w2"]
    ffn1, pair_b1 = [], []
    for q in range(PAIRS):
        a, b = 2 * q, 2 * q + 1
        pick = np.stack([(part % 32 == e) & (part < GATE_ROWS) for e in (a, b)], axis=1).astype(f32)
        down = np.concatenate([w2_1[a][:P], w2_1[b][:P], np.concatenate([w2_1[a][P:], w2_1[b][P:]])], axis=1)
        ffn1.append(np.concatenate([chunked(paired(up[a], up[b])).reshape(P, -1), pick, down], axis=1))
        pair_b1.append(paired(b1_1[a], b1_1[b]).reshape(2 * UNITS, P).T)
    ffn1 = np.stack(ffn1)

    late = np.concatenate([b1] + pair_b1 + [rows(arr[s]) for s in (
        "L0_ffn_gate_b", "L0_ffn_gate_center", "L1_ffn_gate_b", "L1_attn_b_proj", "L1_ffn_scale", "L0_ffn_b2")], axis=1)

    twice = np.zeros((P, EMBED), f32)
    twice[0:EXPERTS1] = arr["L1_ffn_b2"]
    twice[32:32 + EXPERTS1] = arr["L1_ffn_b2"]
    pos = np.arange(SEQ)
    far = np.zeros((P, HEADS * SEQ), f32)
    far[0:SEQ] = np.tile(np.where(np.abs(pos[:, None] - pos[None, :]) > WINDOW, f32(FAR), f32(0)), (1, HEADS))
    same = np.zeros((P, STACK), f32)
    same[0:SEQ] = np.tile(np.eye(SEQ, dtype=f32), (1, TRIO))
    mult = np.concatenate([chunked(arr["L0_ffn_gate_w"]).reshape(P, -1), chunked(arr["L1_ffn_gate_w"].T).reshape(P, -1),
                           twice, far, same, np.zeros((P, 1), f32)], axis=1)

    given = dict(x=px, w_embed=w_embed, start=start, early=early, late=late, mult=mult, att0=att0, att1=att1, ffn0=ffn0, ffn1=ffn1)
    given = {k: np.ascontiguousarray(v) for k, v in given.items()}
    nc = bacc.Bacc("TRN2", target_bir_lowering=False, num_devices=1)
    args = {k: nc.dram_tensor(f"in_{k}", v.shape, F32, kind="ExternalInput").ap() for k, v in given.items()}
    out = nc.dram_tensor("out_0", (TOKENS, EMBED), F32, kind="ExternalOutput").ap()
    vit_tower(nc, out=out, **args)
    r = run_bass_kernel_spmd(nc, [{f"in_{k}": v for k, v in given.items()}], core_ids=[0])
    return r.results[0]["out_0"].reshape(IMAGES, SEQ, EMBED)
```

```python
from contextlib import ExitStack

import concourse.bass as bass
from concourse import mybir

F32 = mybir.dt.float32
F32R = mybir.dt.float32r
ALU = mybir.AluOpType
ACT = mybir.ActivationFunctionType
AX_X = mybir.AxisListType.X

P = 128
IMAGES = 16
PATCH = 16
SIDE = 6
CHANNELS = 3
EMBED = 192
REST = EMBED - P
SEQ = SIDE * SIDE + 1
TOKENS = IMAGES * SEQ
HALF = TOKENS // 2
HALF_IMAGES = IMAGES // 2
TILES = (TOKENS + P - 1) // P
LAST = TOKENS - (TILES - 1) * P
PATCH_CHUNKS = CHANNELS * PATCH * PATCH // P
HEADS = 12
HEAD = EMBED // HEADS
HEADS_A = P // HEAD
HEADS_B = HEADS - HEADS_A
TRIO = 3
TRIOS = HEADS // TRIO
VCOLS = TRIO * HEAD + TRIO
STACK = TRIO * SEQ
SCALE = float(HEAD) ** -0.5
HIDDEN0 = 768
EXPERTS0 = 4
CHUNKS0 = HIDDEN0 // P
EXPERTS1 = 16
TOP = 4
PAIRS = EXPERTS1 // 2
UNITS = 3
LIMIT = 7.0
EPS = 1e-5
WINDOW = 6
FAR = -1e30
EMPTY = -3e38
TAKEN = 3e38
GROUPS = [[0, 1, 2], [3, 4, 5], [6, 7], [8, 9, 10], [11, 12, 13], [14, 15]]

EARLY = dict(ident=P, cos=HALF, sin=HALF, head=HEADS_A, trio=TRIO * HEAD, bqk=6, bv=2, bproj=EMBED)
LATE = dict(b1=EXPERTS0 * CHUNKS0, pair_b1=PAIRS * 2 * UNITS, gate_b=EXPERTS0, center=EXPERTS0,
            gate1_b=EXPERTS1, bproj1=EMBED, scale=EMBED, b2=EXPERTS0 * EMBED)
MULT = dict(gate=2 * EXPERTS0, gate1=2 * EXPERTS1, b2=EMBED, far=HEADS * SEQ, same=STACK, pick=2, pad=1)
MULT_SPLIT = 2 * EXPERTS0 + 2 * EXPERTS1 + EMBED


def places(widths):
    at, out = 0, {}
    for name, width in widths.items():
        out[name] = (at, at + width)
        at += width
    return out, at


EARLY_AT, EARLY_N = places(EARLY)
LATE_AT, LATE_N = places(LATE)
MULT_AT, MULT_N = places(MULT)

QK0 = ["k", "k_turned", "rest", "rest_turned", "q", "q_turned"]
QK1 = ["k", "rest", "q"]
QK = [QK0, QK1]
ATT0_CHUNK = len(QK0) * P + EMBED
ATT1_CHUNK = len(QK1) * P + EMBED
ATT0_N = 2 * ATT0_CHUNK + 2 * EMBED
ATT1_N = 2 * ATT1_CHUNK + 2 * EMBED
FFN0_N = 2 * HIDDEN0 + CHUNKS0 * EMBED
UP1_N = 2 * 2 * UNITS * P + 2
DOWN1_N = UNITS * EMBED
FFN1_N = UP1_N + DOWN1_N


def vit_tower(nc, x, w_embed, start, early, late, mult, att0, att1, ffn0, ffn1, v_dram, out):
    ctx = ExitStack()
    with ctx:
        base = -(-nc.sbuf_base // 64) * 64
        top = [base]
        peak = [base]

        def here(name, shape, dtype, at):
            size = 4
            for s in shape[1:]:
                size *= s
            peak[0] = max(peak[0], at + size)
            return nc.alloc_sbuf_tensor_at(name, shape, dtype, offset=at), at + -(-size // 32) * 32

        def keep(name, shape, dtype=F32):
            t, top[0] = here(name, shape, dtype, top[0])
            return t

        def region(size):
            at = top[0]
            top[0] += -(-size // 32) * 32
            return at

        def placed(at, *tensors):
            out_ = []
            for name, shape, dtype in tensors:
                t, at = here(name, shape, dtype, at)
                out_.append(t)
            return out_

        def sem(name):
            return ctx.enter_context(nc.semaphore(name))

        h = keep("h", [P, TILES, EMBED])
        n = keep("n", [P, TILES, EMBED])
        x_hi = keep("x_hi", [P, TOKENS], F32R)
        x_lo = keep("x_lo", [P, TOKENS], F32R)
        x_rest = keep("x_rest", [P, TOKENS], F32R)
        ce = keep("ce", [P, EARLY_N])
        cl = keep("cl", [P, LATE_N])
        cm_hi = keep("cm_hi", [P, MULT_N], F32R)
        cm_lo = keep("cm_lo", [P, MULT_SPLIT], F32R)
        cm_raw = keep("cm_raw", [P, MULT_N])
        stats = keep("stats", [P, TILES, 6])
        moments = keep("moments", [P, TILES, 2])
        spread = keep("spread", [P, TILES])
        spread2 = keep("spread2", [P, TILES])
        factor = keep("factor", [P, TILES])
        shift = keep("shift", [P, TILES])
        score_rows = keep("score_rows", [EXPERTS1, TOKENS])
        rstd = keep("rstd", [P, TILES])
        minus_half = keep("minus_half", [P, TILES])
        one = keep("one", [P, 1])
        table_sink = keep("table_sink", [P, 1])
        top8 = keep("top8", [P, TILES, 8])
        s0 = keep("s0", [P, TILES, 12])
        s0_left = keep("s0_left", [P, TILES, 12])
        pick0 = keep("pick0", [P, TILES, 8])
        chosen = keep("chosen", [P, TILES, EXPERTS0])
        s1 = keep("s1", [P, TILES, EXPERTS1 + TOP])
        s1_left = keep("s1_left", [P, TILES, EXPERTS1 + TOP])
        pick1 = keep("pick1", [P, TILES, 8])
        gate = keep("gate", [P, TILES, EXPERTS1])
        among = keep("among", [P, TILES, EXPERTS1])
        gate_sum = keep("gate_sum", [P, TILES])
        gate_t = keep("gate_t", [64, TOKENS], F32R)
        lin_b1 = keep("lin_b1", [P, PAIRS * 2 * UNITS])

        r_split = region(2 * 2 * FFN0_N * 4)
        r_att_w = region(2 * ATT0_N * 4)
        r_att_raw = region(ATT0_N * 4)
        r_raw = region(2 * FFN0_N * 4)
        qz_a = keep("qz_a", [P, IMAGES, STACK])
        qz_b = keep("qz_b", [REST, IMAGES, STACK])
        vb = keep("vb", [STACK, IMAGES, TRIOS, VCOLS])
        r_work = top[0]

        w_raw, px_raw = placed(r_raw, ("w_raw", [P, PATCH_CHUNKS, EMBED], F32),
                               ("px_raw", [P, PATCH_CHUNKS, TOKENS], F32))
        w_split, px_hi, px_lo = placed(r_split, ("w_split", [P, 2, PATCH_CHUNKS, EMBED], F32R),
                                       ("px_hi", [P, PATCH_CHUNKS, TOKENS], F32R),
                                       ("px_lo", [P, PATCH_CHUNKS, TOKENS], F32R))
        (start_rows,) = placed(r_work, ("start_rows", [P, TILES, EMBED], F32))
        (a0_raw,) = placed(r_att_raw, ("a0_raw", [P, ATT0_N], F32))
        (a1_raw,) = placed(r_att_raw, ("a1_raw", [P, ATT1_N], F32))
        (y,) = placed(r_att_raw, ("y", [P, TILES, EMBED], F32))
        (a0,) = placed(r_att_w, ("a0", [P, 2, ATT0_N], F32R))
        (a1,) = placed(r_att_w, ("a1", [P, 2, ATT1_N], F32R))
        (f0_raw,) = placed(r_raw, ("f0_raw", [P, 2, FFN0_N], F32))
        (f1_raw,) = placed(r_raw, ("f1_raw", [P, 2, FFN1_N], F32))
        (f0,) = placed(r_split, ("f0", [P, 2, 2, FFN0_N], F32R))
        (f1,) = placed(r_split, ("f1", [P, 2, 2, FFN1_N], F32R))
        up1, down1 = f1[:, :, :, 0:UP1_N], f1[:, :, :, UP1_N:]

        turn1, turn2 = placed(r_work, ("turn1", [P, TOKENS], F32), ("turn2", [P, TOKENS], F32))
        o_sb, k_a, k_b, kb_a, kb_b, probs, probs_t, o_div, o_max = placed(
            r_work, ("o_sb", [SEQ, IMAGES, EMBED], F32), ("k_a", [P, TOKENS], F32), ("k_b", [REST, TOKENS], F32),
            ("kb_a", [P, IMAGES, HEADS_A, SEQ], F32), ("kb_b", [REST, IMAGES, HEADS_B, SEQ], F32),
            ("probs", [STACK, 2, HEADS, SEQ], F32), ("probs_t", [STACK, 2, TRIOS, STACK], F32),
            ("o_div", [SEQ, 3, TRIOS, TRIO], F32),
            ("o_max", [STACK, 2, HEADS], F32))
        v_rows, v3 = placed(r_att_raw, ("v_rows", [P, TILES, EMBED], F32), ("v3", [STACK, IMAGES, TRIOS * HEAD], F32))
        hid0, hid0_hi, hid0_lo = placed(r_work, ("hid0", [P, 2, TOKENS], F32),
                                        ("hid0_hi", [P, 4, TOKENS], F32R), ("hid0_lo", [P, 4, TOKENS], F32R))
        glu, act1, lin, prod, hid1, hid1_hi, hid1_lo = placed(
            r_work, ("glu", [P, 2, TOKENS], F32), ("act1", [P, 2, TOKENS], F32),
            ("lin", [P, 2, TOKENS], F32), ("prod", [P, TOKENS], F32), ("hid1", [P, 2, TOKENS], F32),
            ("hid1_hi", [P, 2 * UNITS, TOKENS], F32R), ("hid1_lo", [P, 2 * UNITS, TOKENS], F32R))
        (gate_bc,) = placed(r_att_w, ("gate_bc", [P, 4, TOKENS], F32))
        assert peak[0] <= nc.sbuf_usable_end, peak[0] - nc.sbuf_usable_end

        ps = ctx.enter_context(nc.psum_tensor("ps", [P, 8, 512], F32))

        def cut(tensor, at, name):
            return tensor[:, at[name][0]:at[name][1]]

        ident = cut(ce, EARLY_AT, "ident")

        def rows_of(t):
            return P if t < TILES - 1 else LAST

        def halves(ap):
            return ap.rearrange("p (a c) -> p a c", a=2)

        def token_out(t):
            return ps[0:rows_of(t), t // 2, (t % 2) * EMBED:(t % 2 + 1) * EMBED]

        last_out = ps[0:LAST, 2, 0:EMBED]

        def bank_of(tensor, k):
            if k == 2:
                return tensor[0:LAST, TILES - 1, :]
            return tensor[:, 2 * k:2 * k + 2, :].rearrange("p t c -> p (t c)")

        def bank_sums(k):
            return last_out if k == 2 else ps[:, k, 0:2 * EMBED]

        def features(lo, size):
            s = slice(lo, lo + size)
            return [(x_hi[:, s], 0, 0), (x_hi[:, s], 0, 1), (x_lo[:, s], 0, 0),
                    (x_rest[:, s], 1, 0), (x_rest[:, s], 1, 1)]

        wraw_in = [sem(f"wraw_in{c}") for c in range(2)]
        early_in, late_in, mult_in, att0_in, att1_in = (
            sem(s) for s in ("early_in", "late_in", "mult_in", "att0_in", "att1_in"))
        px_in = [sem(f"px_in{c}") for c in range(PATCH_CHUNKS)]
        f0_in = [sem(f"f0_in{i}") for i in range(2)]
        f1_in = [sem(f"f1_in{i}") for i in range(2)]
        start_in, out_done = sem("start_in"), sem("out_done")
        px_hi_ready, px_lo_ready, embed_done = sem("px_hi_ready"), sem("px_lo_ready"), sem("embed_done")
        blank_ready, h_blank = sem("blank_ready"), sem("h_blank")
        mult_hi_ready, mult_lo_ready = sem("mult_hi_ready"), sem("mult_lo_ready")
        att_hi_ready, att_lo_ready, att1_hi_ready = sem("att_hi_ready"), sem("att_lo_ready"), sem("att1_hi_ready")
        ones_ready = sem("ones_ready")
        h_ready, h_biased = sem("h_ready"), sem("h_biased")
        stats_ready, moments_ready, spread_ready, rstd_ready, n_ready = (
            sem(s) for s in ("stats_ready", "moments_ready", "spread_ready", "rstd_ready", "n_ready"))
        n_scaled = sem("n_scaled")
        y_ready, z_ready, shift_ready = sem("y_ready"), sem("z_ready"), sem("shift_ready")
        spread2_ready, factor_ready, sums_done = sem("spread2_ready"), sem("factor_ready"), sem("sums_done")
        turned, x_hi_ready, x_lo_ready = sem("turned"), sem("x_hi_ready"), sem("x_lo_ready")
        A = []
        for layer in range(2):
            A.append({s: sem(f"{s}{layer}") for s in (
                "qk_done", "qk_read", "q_done", "q_read", "k_ready", "q_ready", "keys_act", "keys_pool",
                "v_done", "v_kept", "v_stored", "v_back", "v_ready", "s_done", "max_ready", "s_read", "p_ready", "pt_done", "pt_ready",
                "o_done", "div_ready", "o_ready", "ot_done", "ot_hi", "ot_lo", "proj_done")})
        last_added = sem("last_added")
        rows_done, rows_ready = sem("rows_done"), sem("rows_ready")
        gate0_done, s0_raw, s0_ready, top0_ready, pick0_ready, left0_ready, chosen_ready = (
            sem(s) for s in ("gate0_done", "s0_raw", "s0_ready", "top0_ready", "pick0_ready", "left0_ready", "chosen_ready"))
        f0_hi_ready, f0_lo_ready, up0_done, hid0_ready, hid0_hi_ready, hid0_lo_ready, down0_done, y0_added, b2_added = (
            sem(s) for s in ("f0_hi_ready", "f0_lo_ready", "up0_done", "hid0_ready", "hid0_hi_ready",
                             "hid0_lo_ready", "down0_done", "y0_added", "b2_added"))
        gate1_done, s1_ready, top1_ready, pick1_ready, left1_ready, among_ready, gap_ready, exp_ready, weigh_ready, gsum_ready, grec_ready, gate_ready = (
            sem(s) for s in ("gate1_done", "s1_ready", "top1_ready", "pick1_ready", "left1_ready", "among_ready",
                             "gap_ready", "exp_ready", "weigh_ready", "gsum_ready", "grec_ready", "gate_ready"))
        gt_done, gt_hi, gt_lo, lin_b1_ready = sem("gt_done"), sem("gt_hi"), sem("gt_lo"), sem("lin_b1_ready")
        up1_hi, up1_lo, down1_hi, down1_lo = sem("up1_hi"), sem("up1_lo"), sem("down1_hi"), sem("down1_lo")
        glu_done, lin_done, bc_done, bc_ready, glu_ready, lin_read, lin_ready, act1_ready, prod_ready, hid1_ready, hid1_hi_ready, hid1_lo_ready, down1_done = (
            sem(s) for s in ("glu_done", "lin_done", "bc_done", "bc_ready", "glu_ready", "lin_read", "lin_ready", "act1_ready",
                             "prod_ready", "hid1_ready", "hid1_hi_ready", "hid1_lo_ready", "down1_done"))
        last_prod, last_hid, last_hi, last_lo = sem("last_prod"), sem("last_hid"), sem("last_hi"), sem("last_lo")
        result_ready = sem("result_ready")

        block = ctx.enter_context(nc.Block())

        @block.sync
        def _(sp):
            for c in range(PATCH_CHUNKS):
                if c < 2:
                    cols = W_PARTS[c]
                    sp.dma_start(w_raw[:, cols, :], w_embed[:, cols, :]).then_inc(wraw_in[c], 16)
                sp.dma_start(px_raw[:, c, :], x[c]).then_inc(px_in[c], 16)
            sp.dma_start(a0_raw[:], att0).then_inc(att0_in, 16)
            sp.dma_start(start_rows[:], start).then_inc(start_in, 16)
            sp.dma_start(ce[:], early).then_inc(early_in, 16)
            sp.dma_start(cm_raw[:], mult).then_inc(mult_in, 16)
            sp.dma_start(cl[:], late).then_inc(late_in, 16)

            def values_about(s):
                for k in range(3):
                    sp.wait_ge(s["v_kept"], k + 1)
                    if k < 2:
                        sp.dma_start(v_dram[2 * k * P:2 * (k + 1) * P, :].rearrange("(t p) c -> p t c", p=P),
                                     v_rows[:, 2 * k:2 * k + 2, :]).then_inc(s["v_stored"], 16)
                    else:
                        sp.dma_start(v_dram[4 * P:TOKENS, :], v_rows[0:LAST, 4, :]).then_inc(s["v_stored"], 16)
                sp.wait_ge(s["v_stored"], 48)
                for j in range(TRIO):
                    sp.dma_start(v3[j * SEQ:(j + 1) * SEQ], v_dram[:, j * TRIOS * HEAD:(j + 1) * TRIOS * HEAD]
                                 .rearrange("(b k) c -> k b c", k=SEQ)).then_inc(s["v_back"], 16)

            for e in range(EXPERTS0):
                if e == 0:
                    sp.wait_ge(px_lo_ready, PATCH_CHUNKS + 2)
                if e >= 2:
                    sp.wait_ge(f0_lo_ready, e - 1)
                sp.dma_start(f0_raw[:, e % 2, :], ffn0[e]).then_inc(f0_in[e % 2], 16)
                if e == 0:
                    values_about(A[0])
                if e == 2:
                    sp.wait_ge(A[0]["v_ready"], HALF_IMAGES)
                    sp.dma_start(a1_raw[:], att1).then_inc(att1_in, 16)
            sp.wait_ge(f0_lo_ready, EXPERTS0)
            for q in range(2):
                sp.dma_start(f1_raw[:, q, :], ffn1[q]).then_inc(f1_in[q], 16)
            values_about(A[1])
            with sp.Fori(1, PAIRS // 2) as i:
                for q in range(2):
                    sp.wait_ge(down1_lo, i * 2 + (q - 1))
                    sp.dma_start(f1_raw[:, q, :], ffn1[bass.ds(i * 2 + q, 1)].rearrange("a p c -> (a p) c")
                                 ).then_inc(f1_in[q], 16)
            for k in range(2):
                sp.wait_ge(result_ready, k + 1)
                sp.dma_start(out[k * 2 * P:(k + 1) * 2 * P, :].rearrange("(t p) c -> p t c", p=P), n[:, 2 * k:2 * k + 2, :]
                             ).then_inc(out_done, 16)
            sp.wait_ge(result_ready, 3)
            sp.dma_start(out[4 * P:TOKENS, :], n[0:LAST, 4, :]).then_inc(out_done, 16)
            sp.wait_ge(out_done, 48)

        @block.gpsimd
        def _(pool):
            def power(stage):
                for k, (lo, hi) in enumerate(PARTS):
                    if stage == 3:
                        pool.wait_ge(spread2_ready, k + 1)
                        pool.tensor_tensor(factor[:, lo:hi], spread2[:, lo:hi], minus_half[:, lo:hi], ALU.pow).then_inc(factor_ready, 1)
                    pool.wait_ge(spread_ready, len(PARTS) * stage + k + 1)
                    pool.tensor_tensor(rstd[:, lo:hi], spread[:, lo:hi], minus_half[:, lo:hi], ALU.pow).then_inc(rstd_ready, 1)

            def bias_rows(stage, bias):
                pool.wait_ge(n_ready, TILES * (stage + 1))
                pool.tensor_tensor(h[:], h[:], bias.unsqueeze(1).broadcast_to([P, TILES, EMBED]),
                                   ALU.add).then_inc(h_biased, 1)

            def keys_rest(layer):
                s = A[layer]
                pool.wait_ge(s["k_ready"], 2)
                for b in range(0, IMAGES, HALF_IMAGES):
                    kk = k_b[:, b * SEQ:(b + HALF_IMAGES) * SEQ].rearrange("p (b k) -> p b k", k=SEQ)
                    pool.tensor_tensor(
                        kb_b[:, b:b + HALF_IMAGES, :, :],
                        kk.unsqueeze(2).broadcast_to([REST, HALF_IMAGES, HEADS_B, SEQ]),
                        cut(ce, EARLY_AT, "head")[0:REST, 0:HEADS_B].unsqueeze(1).unsqueeze(3)
                        .broadcast_to([REST, HALF_IMAGES, HEADS_B, SEQ]),
                        ALU.mult).then_inc(s["keys_pool"], 1)

            def split(raw, hi, lo, hi_sem, hi_count, lo_sem):
                pool.tensor_tensor(hi, raw, one[:, 0:1].broadcast_to(list(raw.shape)), ALU.mult).then_inc(hi_sem, 1)
                pool.wait_ge(hi_sem, hi_count)
                pool.tensor_tensor(lo, raw, hi.bitcast(F32), ALU.subtract).then_inc(lo_sem, 1)

            pool.memset(minus_half[:], -0.5).then_inc(blank_ready, 1)
            pool.memset(one[:], 1.0).then_inc(blank_ready, 1)
            for t in (qz_a, qz_b):
                pool.memset(t[:], 0.0).then_inc(blank_ready, 1)
            for t in (s0, s1, pick0, pick1):
                pool.memset(t[:], EMPTY).then_inc(blank_ready, 1)
            pool.memset(gate_t[:].bitcast(F32), 0.0).then_inc(blank_ready, 1)
            pool.wait_ge(early_in, 16)
            trio = cut(ce, EARLY_AT, "trio")[0:STACK].rearrange("p (j d) -> p j d", d=HEAD)[:, :, 0:1]
            pool.tensor_copy(vb[:, :, :, TRIO * HEAD:].rearrange("p b g j -> p (b g) j"),
                             trio.rearrange("p j d -> p d j").broadcast_to([STACK, IMAGES * TRIOS, TRIO])
                             ).then_inc(ones_ready, 1)
            pool.wait_ge(blank_ready, 9)
            power(0)
            bias_rows(0, cut(ce, EARLY_AT, "bproj"))
            keys_rest(0)
            pool.wait_ge(mult_hi_ready, 1)
            pool.tensor_tensor(cm_lo[:], cm_raw[:, 0:MULT_SPLIT], cm_hi[:, 0:MULT_SPLIT].bitcast(F32),
                               ALU.subtract).then_inc(mult_lo_ready, 1)
            for e in range(EXPERTS0):
                pool.wait_ge(f0_in[e % 2], 16 * (e // 2 + 1))
                if e == 0:
                    pool.wait_ge(embed_done, 3)
                if e >= 2:
                    pool.wait_ge(down0_done, CHUNKS0 * (e - 1))
                split(f0_raw[:, e % 2, :], f0[:, e % 2, 0, :], f0[:, e % 2, 1, :], f0_hi_ready, e + 1, f0_lo_ready)
                if e == 1:
                    power(1)
            pool.wait_ge(att1_in, 16)
            pool.wait_ge(A[0]["proj_done"], 3)
            split(a1_raw[:], a1[:, 0, :], a1[:, 1, :], att1_hi_ready, 1, att_lo_ready)
            power(2)
            bias_rows(2, cut(cl, LATE_AT, "bproj1"))
            keys_rest(1)
            pool.wait_ge(down0_done, EXPERTS0 * CHUNKS0)

            def split_pair(q, i):
                first = isinstance(i, int)
                pool.wait_ge(f1_in[q], 16 if first else i * 16 + 16)
                if not first:
                    pool.wait_ge(lin_done, i * (2 * UNITS) + UNITS * (q - 1))
                split(f1_raw[:, q, 0:UP1_N], up1[:, q, 0, :], up1[:, q, 1, :], up1_hi,
                      q + 1 if first else i * 2 + (q + 1), up1_lo)
                if not first:
                    pool.wait_ge(down1_done, i * (2 * UNITS) + UNITS * (q - 1))
                split(f1_raw[:, q, UP1_N:], down1[:, q, 0, :], down1[:, q, 1, :], down1_hi,
                      q + 1 if first else i * 2 + (q + 1), down1_lo)

            split_pair(0, 0)
            split_pair(1, 0)
            power(3)
            pool.wait_ge(y_ready, TILES)
            pool.tensor_tensor(h[:], h[:], y[:], ALU.add).then_inc(h_biased, 1)
            with pool.Fori(1, PAIRS // 2) as i:
                split_pair(0, i)
                split_pair(1, i)

        @block.tensor
        def _(pe):
            def mm(o, lhs, rhs, start, stop):
                return pe.matmul(o, lhs, rhs, start=start, stop=stop, skip_group_check=True)

            def stay_busy(products, bank=7):
                for _ in range(products):
                    mm(ps[:, bank, 0:EMBED], one[:, 0:1].broadcast_to([P, P]), one[:, 0:1].broadcast_to([P, EMBED]), True, True)

            def turn_rows(stage):
                stay_busy(BUSY[stage])
                if stage == 0:
                    pe.wait_ge(early_in, 16)
                for lo, hi, bank in ((0, 3, 3), (3, TILES, 4)):
                    for t in range(lo, hi):
                        if stage == 3 and t < 2:
                            pe.wait_ge(n_scaled, t + 1)
                        elif stage == 3:
                            pe.wait_ge(n_ready, TILES * stage + t - 1)
                        else:
                            pe.wait_ge(n_ready, TILES * stage + t + 1)
                        m, at = rows_of(t), (t - lo) * P
                        first = pe.transpose(ps[:, bank, at:at + m], n[0:m, t, 0:P], ident[0:m, 0:m])
                        if t == hi - 1:
                            first.then_inc(turned, 1)
                        rest = pe.transpose(ps[0:REST, bank + 2, at:at + m], n[0:m, t, P:EMBED], ident[0:m, 0:m])
                    rest.then_inc(turned, 1)

            def features_ready(stage, hf, k):
                if k == 0:
                    pe.wait_ge(x_hi_ready, 4 * stage + 1 + 2 * hf)
                if k == 2:
                    pe.wait_ge(x_lo_ready, 4 * stage + 1 + 2 * hf)
                if k == 3:
                    pe.wait_ge(x_lo_ready, 4 * stage + 2 + 2 * hf)

            def rows_product(w, chunk_at, ready, signal):
                for t in range(TILES):
                    if t in (0, 2):
                        pe.wait_ge(ready, 2 + t)
                    passes = features(t * P, rows_of(t))
                    for k, (stat, c, part) in enumerate(passes):
                        at = chunk_at[c]
                        last = mm(token_out(t), stat, w[:, part, at:at + EMBED], k == 0, k == len(passes) - 1)
                    if t % 2 or t == TILES - 1:
                        last.then_inc(signal, 1)

            def attention(layer, w, chunk, units):
                s = A[layer]
                stage = 2 * layer
                pe.wait_ge(att_lo_ready, layer + 1)

                def queries_keys(u, hf):
                    if u >= 2 and hf == 0:
                        pe.wait_ge(s["k_ready"] if layer else s["qk_read"], u - 1)
                    for k, (mov, c, part) in enumerate(features(hf * HALF, HALF)):
                        if u == 0:
                            if k == 0:
                                pe.wait_ge(x_lo_ready, 4 * stage + 1 + 2 * hf)
                            features_ready(stage, hf, k)
                        at = c * chunk + u * P
                        last = mm(ps[:, 3 + 2 * (u % 2) + hf, 0:HALF], w[:, part, at:at + P], mov, k == 0, k == 4)
                    return last

                def make_values():
                    for t in range(TILES):
                        for k, (stat, c, part) in enumerate(features(t * P, rows_of(t))):
                            at = c * chunk + units * P
                            last = mm(token_out(t), stat, w[:, part, at:at + EMBED], k == 0, k == 4)
                        if t % 2 or t == TILES - 1:
                            last.then_inc(s["v_done"], 1)

                first_q = QK[layer].index("q")
                for u in range(first_q):
                    queries_keys(u, 0)
                    queries_keys(u, 1).then_inc(s["qk_done"], 1)
                make_values()
                for hf in range(2):
                    for u in range(first_q, units):
                        queries_keys(u, hf).then_inc(s["q_done"], 1)

                def scores(g):
                    group = GROUPS[g]
                    m = SEQ * len(group)
                    bank = 3 + g % 2
                    if g in (0, len(GROUPS) // 2):
                        hf = int(g > 0)
                        pe.wait_ge(s["q_ready"], 6 + 2 * hf)
                        pe.wait_ge(s["keys_act"], HEADS_A * (1 + hf))
                        pe.wait_ge(s["keys_pool"], 1 + hf)
                    if g == 1:
                        pe.wait_ge(s["q_ready"], 8)
                    if g >= 2:
                        pe.wait_ge(s["s_read"], g - 1)
                    if layer:
                        far, same = cut(cm_hi, MULT_AT, "far"), cut(cm_hi, MULT_AT, "same")
                        mm(ps[0:m, bank, 0:HEADS * SEQ], same[0:SEQ, 0:m], far[0:SEQ, :], True, False)
                    for j, b in enumerate(group):
                        last = j == len(group) - 1
                        mm(ps[0:m, bank, 0:HEADS_A * SEQ], qz_a[:, b, 0:m],
                           kb_a[:, b, :, :].rearrange("p h k -> p (h k)"), not layer and j == 0, last)
                        done = mm(ps[0:m, bank, HEADS_A * SEQ:HEADS * SEQ], qz_b[:, b, 0:m],
                                  kb_b[:, b, :, :].rearrange("p h k -> p (h k)"), False, last)
                    done.then_inc(s["s_done"], 1)

                def turn_probs(g):
                    m = SEQ * len(GROUPS[g])
                    pe.wait_ge(s["p_ready"], g + 1)
                    if g >= 2:
                        pe.wait_ge(s["pt_ready"], g - 1)
                    for r in range(TRIOS):
                        last = pe.transpose(ps[0:STACK, 5 + g % 2, r * STACK:r * STACK + m],
                                            probs[0:m, g % 2, r * TRIO:(r + 1) * TRIO, :].rearrange("p h k -> p (h k)"),
                                            ident[0:m, 0:m])
                    last.then_inc(s["pt_done"], 1)

                def values(g):
                    pe.wait_ge(s["v_ready"], GROUPS[g][-1] // 2 + 1)
                    if g == 0:
                        pe.wait_ge(ones_ready, 1)
                    pe.wait_ge(s["pt_ready"], g + 1)
                    if g >= 2:
                        pe.wait_ge(s["o_ready"], g - 1)
                    for j, b in enumerate(GROUPS[g]):
                        bank, at = OUT_BANKS[g % 2][j // 2], (j % 2) * TRIOS * VCOLS
                        for r in range(TRIOS):
                            last = mm(ps[0:SEQ, bank, at + r * VCOLS:at + (r + 1) * VCOLS],
                                      probs_t[:, g % 2, r, j * SEQ:(j + 1) * SEQ], vb[:, b, r, :], True, True)
                    last.then_inc(s["o_done"], 1)

                def turn_outputs(k):
                    hf, rest = divmod(k, 2)
                    m, cols = (REST, slice(P, EMBED)) if rest else (P, slice(0, P))
                    if k == 0:
                        pe.wait_ge(s["o_ready"], len(GROUPS) // 2)
                    if k == 2:
                        pe.wait_ge(s["o_ready"], len(GROUPS))
                    pe.wait_ge(s["pt_ready"] if rest else s["s_read"], len(GROUPS) - 1 + hf)
                    for i in range(HALF_IMAGES):
                        last = pe.transpose(ps[0:m, 3 + 2 * rest + hf, i * SEQ:(i + 1) * SEQ],
                                            o_sb[:, hf * HALF_IMAGES + i, cols], ident[0:SEQ, 0:SEQ])
                    last.then_inc(s["ot_done"], 1)

                groups = len(GROUPS)
                for g in range(groups + 2):
                    if g < groups:
                        scores(g)
                    if g == groups:
                        turn_outputs(0)
                    if 1 <= g <= groups:
                        turn_probs(g - 1)
                    if g == groups + 1:
                        turn_outputs(1)
                    if g >= 2:
                        values(g - 2)
                stay_busy(BUSY_BEFORE_OUTPUTS, 6)
                turn_outputs(2)
                turn_outputs(3)
                rows_product(w, (2 * chunk, 2 * chunk + EMBED), s["ot_lo"], s["proj_done"])

            def gates(stage, name, experts):
                pe.wait_ge(mult_lo_ready, 1)
                for hf in range(2):
                    for k, (mov, c, part) in enumerate(features(hf * HALF, HALF)):
                        features_ready(stage, hf, k)
                        at = MULT_AT[name][0] + c * experts
                        last = mm(ps[0:experts, hf, 0:HALF], (cm_hi, cm_lo)[part][:, at:at + experts], mov, k == 0, k == 4)
                    last.then_inc(rows_done, 1)

            def turn_scores(layer, experts, signal):
                pe.wait_ge(rows_ready, 2 * (layer + 1))
                for t in range(TILES):
                    m = rows_of(t)
                    last = pe.transpose(ps[0:m, 7, t * experts:(t + 1) * experts], score_rows[0:experts, t * P:t * P + m],
                                        ident[0:experts, 0:experts])
                last.then_inc(signal, 1)

            def free_bank(e):
                def before(t, k):
                    if t % 2 == 0 and k == 0:
                        pe.wait_ge(y0_added, TILES * (e - 1) + min(t + 2, TILES))
                return before

            def down(hi, lo, w_hi, w_lo, first, stop, before=None, signal=None, tile_by_tile=False):
                passes = list(enumerate(((hi, w_hi), (hi, w_lo), (lo, w_hi))))
                order = [(t, p) for t in range(TILES) for p in passes] if signal or tile_by_tile else [(t, p) for p in passes for t in range(TILES)]
                for t, (k, (stat, w)) in order:
                    if before:
                        before(t, k)
                    last = mm(token_out(t), stat[:, t * P:t * P + rows_of(t)], w,
                              first and k == 0 and t % 2 == 0, stop and k == 2)
                    if signal and k == 2 and t % 2:
                        last.then_inc(signal, 1)
                return last

            pe.wait_ge(blank_ready, 2)
            stay_busy(BUSY_AT_START)
            for c in range(PATCH_CHUNKS):
                done = c + min(c, 1)

                def chunk_ready(t, k):
                    if t == 0 and k == 0:
                        pe.wait_ge(px_hi_ready, done + 2)
                    if t == 0 and k == 1:
                        pe.wait_ge(px_lo_ready, min(done + 1, 3))
                    if t == 0 and k == 2:
                        pe.wait_ge(px_lo_ready, done + 2)

                last = down(px_hi[:, c, :], px_lo[:, c, :], w_split[:, 0, c, :], w_split[:, 1, c, :], c == 0, c == PATCH_CHUNKS - 1,
                            before=chunk_ready, signal=embed_done if c == PATCH_CHUNKS - 1 else None)
            last.then_inc(embed_done, 1)

            turn_rows(0)
            attention(0, a0, ATT0_CHUNK, len(QK0))
            turn_rows(1)
            gates(1, "gate", EXPERTS0)

            def up0(u):
                e, c = divmod(u, CHUNKS0)
                if c == 0:
                    pe.wait_ge(f0_lo_ready, e + 1)
                if u >= 2:
                    pe.wait_ge(hid0_ready, u - 1)
                for hf in range(2):
                    for k, (mov, ch, part) in enumerate(features(hf * HALF, HALF)):
                        at = ch * HIDDEN0 + c * P
                        last = mm(ps[:, 3 + 2 * (u % 2) + hf, 0:HALF], f0[:, e % 2, part, at:at + P], mov, k == 0, k == 4)
                last.then_inc(up0_done, 1)

            def down0(u):
                e, c = divmod(u, CHUNKS0)
                pe.wait_ge(hid0_lo_ready, u + 1)

                at = 2 * HIDDEN0 + c * EMBED
                down(hid0_hi[:, u % 4, :], hid0_lo[:, u % 4, :], f0[:, e % 2, 0, at:at + EMBED],
                     f0[:, e % 2, 1, at:at + EMBED], c == 0, c == CHUNKS0 - 1, before=free_bank(e) if c == 0 and e else None, tile_by_tile=c == 0 and e,
                     signal=sums_done if u == units0 - 1 else None).then_inc(down0_done, 1)

            units0 = EXPERTS0 * CHUNKS0
            for u in range(units0 + 2):
                if u < units0:
                    up0(u)
                if u == 0:
                    turn_scores(0, EXPERTS0, gate0_done)
                if u >= 2:
                    down0(u - 2)

            turn_rows(2)
            attention(1, a1, ATT1_CHUNK, len(QK1))
            turn_rows(3)
            gates(3, "gate1", EXPERTS1)

            def turn_gates():
                pe.wait_ge(gate_ready, 1)
                for t in range(TILES):
                    m = rows_of(t)
                    last = pe.transpose(ps[0:EXPERTS1, t // 4, (t % 4) * P:(t % 4) * P + m], gate[0:m, t, :], ident[0:m, 0:m])
                last.then_inc(gt_done, 1)

            def open_sums(part):
                b2 = (cm_hi, cm_lo)[part][0:GATE_ROWS, MULT_AT["b2"][0]:MULT_AT["b2"][1]]
                for t in range(TILES):
                    mm(token_out(t), gate_t[0:GATE_ROWS, t * P:t * P + rows_of(t)], b2, part == 0 and t % 2 == 0, False)

            def broadcast_gate(q, expert, hf, pair):
                count = pair * 4 + (2 * expert + hf)
                if not isinstance(count, int) or count > 0:
                    pe.wait_ge(bc_ready, count)
                source, at = (cm_hi, MULT_AT["pick"][0]) if isinstance(pair, int) and pair == 0 else (up1[:, q, 0, :], UP1_N - 2)
                pick = source[0:GATE_ROWS, at + expert:at + expert + 1].broadcast_to([GATE_ROWS, P])
                mm(ps[:, 7, 0:HALF], pick, gate_t[0:GATE_ROWS, hf * HALF:(hf + 1) * HALF], True, True).then_inc(bc_done, 1)

            def up1_unit(q, col, bank, signal, between=None):
                for hf in range(2):
                    if hf and between:
                        between()
                    for k, (mov, ch, part) in enumerate(features(hf * HALF, HALF)):
                        at = ch * 2 * UNITS * P + col * P
                        last = mm(ps[:, bank + hf, 0:HALF], up1[:, q, part, at:at + P], mov, k == 0, k == 4)
                last.then_inc(signal, 1)

            def down1_unit(slot, count):
                pe.wait_ge(hid1_lo_ready, count)
                q, u = divmod(slot, UNITS)
                at = u * EMBED
                down(hid1_hi[:, slot, :], hid1_lo[:, slot, :], down1[:, q, 0, at:at + EMBED],
                     down1[:, q, 1, at:at + EMBED], False, False).then_inc(down1_done, 1)

            def two_pairs(i):
                first = isinstance(i, int)
                for slot in range(2 * UNITS):
                    q, u = divmod(slot, UNITS)
                    unit = i * (2 * UNITS) + slot
                    pair = i * 2 + q
                    if u == 0:
                        pe.wait_ge(up1_lo, pair + 1)
                    if not (first and slot == 0):
                        pe.wait_ge(glu_ready, unit)
                    up1_unit(q, u, 3, glu_done)
                    if first and slot == 0:
                        turn_scores(1, EXPERTS1, gate1_done)
                    elif first and slot == 2:
                        pe.wait_ge(gt_lo, 2)
                        broadcast_gate(q, 0, 0, pair)
                    elif u < 2 and not (first and slot < 2):
                        broadcast_gate(q, u, 0, pair)
                    if not (first and slot == 0):
                        pe.wait_ge(lin_read, unit)
                    between = (lambda: broadcast_gate(0, 0, 1, 0)) if first and slot == 2 else None
                    up1_unit(q, UNITS + u, 5, lin_done, between)
                    if first and slot == 1:
                        turn_gates()
                    elif first and slot == 2:
                        broadcast_gate(q, 1, 0, pair)
                        open_sums(0)
                        open_sums(1)
                        broadcast_gate(q, 1, 1, pair)
                    elif u < 2 and not (first and slot == 0):
                        broadcast_gate(q, u, 1, pair)
                    if not (first and slot < UNITS):
                        if u == 0:
                            pe.wait_ge(down1_lo, pair)
                        down1_unit((slot + UNITS) % (2 * UNITS), unit - (UNITS - 1))

            two_pairs(0)
            with pe.Fori(1, PAIRS // 2) as i:
                two_pairs(i)
            pe.wait_ge(down1_lo, PAIRS)
            down1_unit(UNITS, UNITS * (PAIRS - 1) + 1)
            for u in range(1, UNITS):
                hi, at = hid1_hi[:, UNITS + u, :], u * EMBED
                if u == 1:
                    pe.wait_ge(hid1_hi_ready, UNITS * PAIRS - 1)
                for t in range(TILES):
                    if u == 2 and t in (0, 2):
                        pe.wait_ge(last_hi, t // 2 + 1)
                    for part in range(2):
                        mm(token_out(t), hi[:, t * P:t * P + rows_of(t)], down1[:, 1, part, at:at + EMBED], False, False)
            for u in range(1, UNITS):
                lo, at, stop = hid1_lo[:, UNITS + u, :], u * EMBED, u == UNITS - 1
                if u == 1:
                    pe.wait_ge(hid1_lo_ready, UNITS * PAIRS - 1)
                for t in range(TILES):
                    if stop and t in (0, 2):
                        pe.wait_ge(last_lo, t // 2 + 1)
                    last = mm(token_out(t), lo[:, t * P:t * P + rows_of(t)], down1[:, 1, 0, at:at + EMBED], False, stop)
                    if stop and t % 2:
                        last.then_inc(sums_done, 1)
                last.then_inc(down1_done, 1)

        @block.scalar
        def _(act):
            def copy(o, i):
                return act.activation(o, i, ACT.Copy)

            def load_table(function):
                act.activation(table_sink[:], one[:], function)

            def feature_hi(stage):
                for k, (bank, lo, hi) in enumerate(TURNED):
                    act.wait_ge(turned, 4 * stage + k + 1)
                    m, dst = (REST, x_rest) if k % 2 else (P, x_hi)
                    copy(dst[0:m, lo:hi], ps[0:m, bank, 0:hi - lo]).then_inc(x_hi_ready, 1)

            def attention(layer):
                s = A[layer]
                if layer == 0:
                    act.wait_ge(att_lo_ready, 1)
                load_table(ACT.Exp)
                act.wait_ge(s["k_ready"], 1)
                for k in range(2 * HEADS_A):
                    if k == KEYS_FIRST[layer]:
                        for bank in range(3):
                            act.wait_ge(s["v_done"], bank + 1)
                            copy(bank_of(v_rows, bank), bank_sums(bank)).then_inc(s["v_kept"], 1)
                    hf, hd = divmod(k, HEADS_A)
                    images = slice(hf * HALF_IMAGES, (hf + 1) * HALF_IMAGES)
                    act.activation(kb_a[:, images, hd, :], k_a[:, hf * HALF:(hf + 1) * HALF].rearrange("p (b k) -> p b k", k=SEQ),
                                   ACT.Copy, scale=ce[:, EARLY_AT["head"][0] + hd:EARLY_AT["head"][0] + hd + 1]).then_inc(s["keys_act"], 1)

                def soften(g):
                    m = SEQ * len(GROUPS[g])
                    act.wait_ge(s["s_read"], g + 1)
                    act.activation(probs[0:m, g % 2], probs[0:m, g % 2], ACT.Exp, scale=SCALE).then_inc(s["p_ready"], 1)

                def keep_turned(g):
                    m = SEQ * len(GROUPS[g])
                    act.wait_ge(s["pt_done"], g + 1)
                    if g >= 2:
                        act.wait_ge(s["o_done"], g - 1)
                    copy(probs_t[:, g % 2, :, 0:m],
                         ps[0:STACK, 5 + g % 2, 0:TRIOS * STACK].rearrange("p (r c) -> p r c", c=STACK)[:, :, 0:m]
                         ).then_inc(s["pt_ready"], 1)

                for g in range(len(GROUPS) + 1):
                    if g < len(GROUPS):
                        soften(g)
                    if g:
                        keep_turned(g - 1)
                for k in range(4):
                    hf, rest = divmod(k, 2)
                    act.wait_ge(s["ot_done"], k + 1)
                    m = REST if rest else P
                    dst = (x_rest if rest else x_hi)[0:m, hf * HALF:(hf + 1) * HALF]
                    src = ps[0:m, 3 + 2 * rest + hf, 0:HALF]
                    if layer:
                        copy(dst, src).then_inc(s["ot_hi"], 1)
                    else:
                        at = EARLY_AT["bv"][0] + rest
                        act.activation(dst, src, ACT.Identity, bias=ce[0:m, at:at + 1]).then_inc(s["ot_hi"], 1)

            def keep_rows(layer, experts):
                for hf in range(2):
                    act.wait_ge(rows_done, 2 * layer + hf + 1)
                    copy(score_rows[0:experts, hf * HALF:(hf + 1) * HALF], ps[0:experts, hf, 0:HALF]).then_inc(rows_ready, 1)

            for c in range(PATCH_CHUNKS):
                if c < 2:
                    act.wait_ge(wraw_in[c], 16)
                    copy(w_split[:, 0, W_PARTS[c]], w_raw[:, W_PARTS[c]]).then_inc(px_hi_ready, 1)
                act.wait_ge(px_in[c], 16)
                copy(px_hi[:, c, :], px_raw[:, c, :]).then_inc(px_hi_ready, 1)
            act.wait_ge(att0_in, 16)
            copy(a0[:, 0, :], a0_raw[:]).then_inc(att_hi_ready, 1)
            act.wait_ge(mult_in, 16)
            copy(cm_hi[:], cm_raw[:]).then_inc(mult_hi_ready, 1)

            act.wait_ge(blank_ready, 9)
            act.wait_ge(early_in, 16)
            feature_hi(0)
            attention(0)
            feature_hi(1)
            load_table(ACT.Gelu)
            keep_rows(0, EXPERTS0)
            act.wait_ge(late_in, 16)
            for u in range(EXPERTS0 * CHUNKS0):
                act.wait_ge(up0_done, u + 1)
                if u >= 2:
                    act.wait_ge(hid0_lo_ready, u - 1)
                act.activation(halves(hid0[:, u % 2, :]), ps[:, 3 + 2 * (u % 2):5 + 2 * (u % 2), 0:HALF], ACT.Gelu,
                               bias=cl[:, LATE_AT["b1"][0] + u:LATE_AT["b1"][0] + u + 1]).then_inc(hid0_ready, 1)
            feature_hi(2)
            attention(1)
            act.wait_ge(factor_ready, 1)
            for t in range(2):
                act.wait_ge(z_ready, t + 1)
                act.activation(n[:, t, :], n[:, t, :], ACT.Copy, scale=factor[:, t:t + 1]).then_inc(n_scaled, 1)
            feature_hi(3)
            keep_rows(1, EXPERTS1)
            act.wait_ge(shift_ready, 1)
            for t in range(TILES):
                act.activation(y[:, t, :], h[:, t, :], ACT.Identity, bias=shift[:, t:t + 1], scale=rstd[:, t:t + 1]).then_inc(y_ready, 1)
            act.wait_ge(lin_b1_ready, 1)
            act.wait_ge(lin_done, 1)
            act.activation(halves(lin[:, 0, :]), ps[:, 5:7, 0:HALF], ACT.Identity, bias=lin_b1[:, UNITS:UNITS + 1]).then_inc(lin_read, 1)
            act.wait_ge(gap_ready, 1)
            act.activation(gate[:], gate[:], ACT.Exp).then_inc(exp_ready, 1)
            load_table(ACT.Gelu_apprx_sigmoid)

            def turned_gates():
                act.wait_ge(blank_ready, 9)
                act.wait_ge(gt_done, 1)
                copy(gate_t[0:EXPERTS1, 0:4 * P], ps[0:EXPERTS1, 0, 0:4 * P]).then_inc(gt_hi, 1)
                copy(gate_t[0:EXPERTS1, 4 * P:], ps[0:EXPERTS1, 1, 0:LAST]).then_inc(gt_hi, 1)

            def two_pairs(i):
                first = isinstance(i, int)
                for slot in range(2 * UNITS):
                    q, u = divmod(slot, UNITS)
                    unit = i * (2 * UNITS) + slot
                    pair = i * 2 + q

                    def keep_gate(expert, hf):
                        act.wait_ge(bc_done, pair * 4 + (2 * expert + hf + 1))
                        cols, mix = slice(hf * HALF, (hf + 1) * HALF), slice(expert * REST, (expert + 1) * REST)
                        if hf == 0 and not (first and q == 0):
                            act.wait_ge(hid1_ready, pair * UNITS - (2 - expert))
                        copy(gate_bc[:, expert, cols], ps[:, 7, 0:HALF])
                        copy(gate_bc[mix, 2 + q, cols], ps[mix, 7, 0:HALF]).then_inc(bc_ready, 1)

                    def swish():
                        act.wait_ge(glu_ready, unit + 1)
                        if not (first and slot < 2):
                            act.wait_ge(prod_ready, unit - 1)
                        act.activation(act1[:, slot % 2, :], glu[:, slot % 2, :], ACT.Gelu_apprx_sigmoid).then_inc(act1_ready, 1)

                    def linear():
                        act.wait_ge(lin_done, unit + 1)
                        if not (first and slot < 2):
                            act.wait_ge(prod_ready, unit - 1)
                        at = UNITS + q * 2 * UNITS + u
                        column = lin_b1[:, at:at + 1] if first else lin_b1[:, bass.ds(i * (4 * UNITS) + at, 1)]
                        act.activation(halves(lin[:, slot % 2, :]), ps[:, 5:7, 0:HALF], ACT.Identity, bias=column).then_inc(lin_read, 1)

                    if first and slot == 0:
                        swish()
                    elif first and slot == 1:
                        turned_gates()
                        linear()
                        swish()
                    elif first and slot == 2:
                        keep_gate(0, 0)
                        keep_gate(0, 1)
                        keep_gate(1, 0)
                        linear()
                        keep_gate(1, 1)
                        swish()
                        hidden_hi(0, 1, True)
                    else:
                        if u < 2:
                            keep_gate(u, 0)
                        hidden_hi((slot - 2) % (2 * UNITS), unit - 1, first)
                        swish()
                        linear()
                        if u < 2:
                            keep_gate(u, 1)

            def hidden_hi(slot, count, unused):
                act.wait_ge(hid1_ready, count)
                if not unused:
                    act.wait_ge(down1_done, count - 2 * UNITS + (1 if slot == 2 * UNITS - 2 else 0))
                copy(hid1_hi[:, slot, :], hid1[:, slot % 2, :]).then_inc(hid1_hi_ready, 1)

            two_pairs(0)
            with act.Fori(1, PAIRS // 2) as i:
                two_pairs(i)
            hidden_hi(2 * UNITS - 2, UNITS * PAIRS - 1, False)
            for hf in range(2):
                cols = slice(hf * HALF, (hf + 1) * HALF)
                act.wait_ge(last_hid, hf + 1)
                if hf == 0:
                    act.wait_ge(down1_done, UNITS * (PAIRS - 2))
                copy(hid1_hi[:, 2 * UNITS - 1, cols], hid1[:, 1, cols]).then_inc(last_hi, 1)

        @block.vector
        def _(dve):
            sub, add, mult = ALU.subtract, ALU.add, ALU.mult

            def tt(o, a, b, op):
                return dve.tensor_tensor(o, a, b, op)

            def norm(stage, add_bank):
                mean, var = moments[:, :, 0], moments[:, :, 1]

                def tile_stats(t):
                    dve.wait_ge(h_ready, 3 * stage + t // 2 + 1)
                    dve.bn_stats(stats[:, t, :], h[:, t, :]).then_inc(stats_ready, 1)

                def tile_moments(t):
                    dve.wait_ge(stats_ready, TILES * stage + t + 1)
                    dve.bn_aggr(moments[:, t, :], stats[:, t, :]).then_inc(moments_ready, 1)

                def part_spread(k):
                    lo, hi = PARTS[k]
                    dve.wait_ge(moments_ready, TILES * stage + hi)
                    if stage == 3:
                        dve.tensor_scalar(spread2[:, lo:hi], var[:, lo:hi], 1.0 + EPS, EPS * EPS, mult, add).then_inc(spread2_ready, 1)
                    dve.tensor_scalar(spread[:, lo:hi], var[:, lo:hi], EPS, None, add).then_inc(spread_ready, 1)

                def scaled(t):
                    if stage == 3:
                        dve.wait_ge(late_in, 16)
                        dve.scalar_tensor_tensor(out=n[:, t, :], in0=h[:, t, :], scalar=moments[:, t, 0:1],
                                                 in1=cut(cl, LATE_AT, "scale"), op0=sub, op1=mult).then_inc(z_ready, 1)

                def row(t):
                    k = t // 2
                    if stage == 3:
                        if t < 2:
                            return
                        dve.wait_ge(factor_ready, k + 1)
                        dve.wait_ge(z_ready, t + 1)
                        dve.tensor_scalar(n[:, t, :], n[:, t, :], factor[:, t:t + 1], None, mult).then_inc(n_ready, 1)
                    else:
                        dve.wait_ge(rstd_ready, len(PARTS) * stage + k + 1)
                        dve.tensor_scalar(n[:, t, :], h[:, t, :], moments[:, t, 0:1], rstd[:, t:t + 1], sub, mult).then_inc(n_ready, 1)

                add_bank(0)
                tile_stats(0)
                tile_stats(1)
                add_bank(1)
                tile_moments(0)
                tile_moments(1)
                tile_stats(2)
                tile_stats(3)
                part_spread(0)
                scaled(0)
                scaled(1)
                tile_moments(2)
                tile_moments(3)
                add_bank(2)
                part_spread(1)
                scaled(2)
                tile_stats(4)
                row(0)
                row(1)
                tile_moments(4)
                row(2)
                part_spread(2)
                scaled(3)
                scaled(4)
                row(3)
                row(4)
                if stage == 3:
                    dve.wait_ge(rstd_ready, len(PARTS) * (stage + 1))
                    dve.scalar_tensor_tensor(out=shift[:], in0=mean, scalar=-1.0, in1=rstd[:], op0=mult, op1=mult).then_inc(shift_ready, 1)

            def feature_lo(stage):
                for k, (bank, lo, hi) in enumerate(TURNED):
                    dve.wait_ge(x_hi_ready, 4 * stage + k + 1)
                    m = REST if k % 2 else P
                    hi_part = (x_rest if k % 2 else x_hi)[0:m, lo:hi]
                    dst = x_rest[REST:P, lo:hi] if k % 2 else x_lo[:, lo:hi]
                    tt(dst, ps[0:m, bank, 0:hi - lo], hi_part.bitcast(F32), sub).then_inc(x_lo_ready, 1)

            def diagonal(qz, b, groups, each):
                whole = qz[:, b:b + groups * each, :]
                steps = [list(p) for p in whole.ap]
                return bass.AP(whole.tensor, whole.offset,
                               [steps[0], [each * STACK, groups], [STACK + SEQ, each], [1, SEQ]])

            def place(ap, b, groups, each):
                return ap[:, b * SEQ:(b + groups * each) * SEQ].rearrange("p (g j k) -> p g j k", g=groups, k=SEQ)

            def attention(layer):
                s = A[layer]

                def spread_values(i):
                    trio = cut(ce, EARLY_AT, "trio")[0:STACK].rearrange("p (j d) -> p j d", d=HEAD)
                    shape = [STACK, 2 * TRIOS, TRIO, HEAD]
                    dve.wait_ge(s["v_back"], 48)
                    tt(vb[:, 2 * i:2 * i + 2, :, 0:TRIO * HEAD].rearrange("p b g (j d) -> p (b g) j d", d=HEAD),
                       v3[:, 2 * i:2 * i + 2, :].rearrange("p b (g d) -> p (b g) d", d=HEAD).unsqueeze(2).broadcast_to(shape),
                       trio.unsqueeze(1).broadcast_to(shape), mult).then_inc(s["v_ready"], 1)

                if layer == 0:
                    cos = cut(ce, EARLY_AT, "cos").unsqueeze(1).broadcast_to([P, 2, HALF])
                    sin = cut(ce, EARLY_AT, "sin").unsqueeze(1).broadcast_to([P, 2, HALF])

                    def rotate(p):
                        if p == 1:
                            dve.wait_ge(s["k_ready"], 1)
                        for k, (dst, table) in enumerate(((turn1, cos), (turn2, sin))):
                            u = 2 * p + k
                            dve.wait_ge(s["qk_done"], u + 1)
                            dve.scalar_tensor_tensor(
                                out=halves(dst[:]), in0=ps[:, 3 + 2 * k:5 + 2 * k, 0:HALF],
                                scalar=ce[:, EARLY_AT["bqk"][0] + u:EARLY_AT["bqk"][0] + u + 1], in1=table,
                                op0=add, op1=mult).then_inc(s["qk_read"], 1)
                        dve.wait_ge(s["qk_read"], 2 * p + 2)

                    dve.wait_ge(blank_ready, 9)
                    rotate(0)
                    tt(k_a[:], turn1[:], turn2[:], add).then_inc(s["k_ready"], 1)
                    rotate(1)
                    tt(k_b[:], turn1[REST:P, :], turn2[REST:P, :], add).then_inc(s["k_ready"], 1)
                    for hf in range(2):
                        for b, g, e in ((hf * 8, 2, 3), (hf * 8 + 6, 1, 2)):
                            tt(diagonal(qz_b, b, g, e), place(turn1[0:REST, :], b, g, e), place(turn2[0:REST, :], b, g, e), add
                               ).then_inc(s["q_ready"], 1)
                    dve.wait_ge(s["q_ready"], 4)
                    for hf in range(2):
                        part = slice(hf * HALF, (hf + 1) * HALF)
                        for k, (dst, table) in enumerate(((turn1, cos), (turn2, sin))):
                            at = EARLY_AT["bqk"][0] + 4 + k
                            dve.wait_ge(s["q_done"], 2 * hf + k + 1)
                            dve.scalar_tensor_tensor(out=dst[:, part], in0=ps[:, 3 + 2 * k + hf, 0:HALF], scalar=ce[:, at:at + 1],
                                                     in1=table[:, hf, :], op0=add, op1=mult).then_inc(s["q_read"], 1)
                        dve.wait_ge(s["q_read"], 2 * hf + 2)
                        for b, g, e in ((hf * 8, 2, 3), (hf * 8 + 6, 1, 2)):
                            tt(diagonal(qz_a, b, g, e), place(turn1[:], b, g, e), place(turn2[:], b, g, e), add
                               ).then_inc(s["q_ready"], 1)
                else:
                    dve.wait_ge(s["qk_done"], 1)
                    dve.tensor_copy(halves(k_a[:]), ps[:, 3:5, 0:HALF]).then_inc(s["k_ready"], 1)
                    dve.wait_ge(s["qk_done"], 2)
                    dve.tensor_copy(halves(k_b[:]), ps[REST:P, 5:7, 0:HALF]).then_inc(s["k_ready"], 1)
                    for hf in range(2):
                        for b, g, e in ((0, 2, 3), (6, 1, 2)):
                            dve.tensor_copy(diagonal(qz_b, hf * 8 + b, g, e), place(ps[0:REST, 5 + hf, 0:HALF], b, g, e)
                                            ).then_inc(s["q_ready"], 1)
                    for hf in range(2):
                        dve.wait_ge(s["q_done"], hf + 1)
                        for b, g, e in ((0, 2, 3), (6, 1, 2)):
                            dve.tensor_copy(diagonal(qz_a, hf * 8 + b, g, e), place(ps[:, 3 + hf, 0:HALF], b, g, e)
                                            ).then_inc(s["q_ready"], 1)

                def center(g):
                    m = SEQ * len(GROUPS[g])
                    sc = ps[0:m, 3 + g % 2, 0:HEADS * SEQ].rearrange("p (h k) -> p h k", k=SEQ)
                    dve.wait_ge(s["s_done"], g + 1)
                    dve.tensor_reduce(o_max[0:m, g % 2, :], sc, AX_X, ALU.max).then_inc(s["max_ready"], 1)
                    dve.wait_ge(s["max_ready"], g + 1)
                    if g >= 2:
                        dve.wait_ge(s["pt_done"], g - 1)
                    tt(probs[0:m, g % 2], sc, o_max[0:m, g % 2, :].unsqueeze(2).broadcast_to([m, HEADS, SEQ]), sub
                       ).then_inc(s["s_read"], 1)

                def divide(g):
                    dve.wait_ge(s["o_done"], g + 1)
                    if g:
                        dve.wait_ge(s["o_ready"], g)
                    group = GROUPS[g]
                    parts = [(0, 2)] + [(2, 1)] * (len(group) == 3)
                    for k, (j, cnt) in enumerate(parts):
                        o = ps[0:SEQ, OUT_BANKS[g % 2][k], 0:cnt * TRIOS * VCOLS].rearrange("p (r c) -> p r c", c=VCOLS)
                        ins = dve.reciprocal(o_div[:, j:j + cnt].rearrange("p b r t -> p (b r) t"), o[:, :, TRIO * HEAD:])
                    ins.then_inc(s["div_ready"], 1)
                    dve.wait_ge(s["div_ready"], g + 1)
                    for k, (j, cnt) in enumerate(parts):
                        o = ps[0:SEQ, OUT_BANKS[g % 2][k], 0:cnt * TRIOS * VCOLS].rearrange("p (r c) -> p r c", c=VCOLS)
                        b = group[0] + j
                        ins = tt(o_sb[:, b:b + cnt, :].rearrange("p b (r t d) -> p (b r) t d", t=TRIO, d=HEAD),
                                 o[:, :, 0:TRIO * HEAD].rearrange("p r (t d) -> p r t d", d=HEAD),
                                 o_div[:, j:j + cnt].rearrange("p b r t -> p (b r) t").unsqueeze(3)
                                 .broadcast_to([SEQ, cnt * TRIOS, TRIO, HEAD]), mult)
                    ins.then_inc(s["o_ready"], 1)

                for g in range(len(GROUPS) + 2):
                    if g < len(GROUPS):
                        center(g)
                    if 1 <= g <= HALF_IMAGES // 2:
                        spread_values(2 * g - 2)
                        spread_values(2 * g - 1)
                    if g >= 2:
                        divide(g - 2)
                for k in range(4):
                    hf, rest = divmod(k, 2)
                    dve.wait_ge(s["ot_hi"], k + 1)
                    m = REST if rest else P
                    cols = slice(hf * HALF, (hf + 1) * HALF)
                    src = ps[0:m, 3 + 2 * rest + hf, 0:HALF]
                    hi_part = (x_rest if rest else x_hi)[0:m, cols].bitcast(F32)
                    dst = x_rest[REST:P, cols] if rest else x_lo[:, cols]
                    if layer:
                        tt(dst, src, hi_part, sub).then_inc(s["ot_lo"], 1)
                    else:
                        at = EARLY_AT["bv"][0] + rest
                        dve.scalar_tensor_tensor(out=dst, in0=src, scalar=ce[0:m, at:at + 1], in1=hi_part, op0=add, op1=sub
                                                 ).then_inc(s["ot_lo"], 1)

            def add_output(layer):
                def add_bank(k):
                    if k == 0:
                        dve.wait_ge(h_biased, layer + 1)
                    dve.wait_ge(A[layer]["proj_done"], k + 1)
                    tt(bank_of(h, k), bank_sums(k), bank_of(h, k), add).then_inc(h_ready, 1)
                return add_bank

            dve.memset(h[:, TILES - 1, :], 0.0).then_inc(h_blank, 1)
            for c in range(PATCH_CHUNKS):
                if c < 2:
                    dve.wait_ge(px_hi_ready, 2 * c + 1)
                    tt(w_split[:, 1, W_PARTS[c]], w_raw[:, W_PARTS[c]], w_split[:, 0, W_PARTS[c]].bitcast(F32), sub).then_inc(px_lo_ready, 1)
                dve.wait_ge(px_hi_ready, c + min(c, 1) + 2)
                tt(px_lo[:, c, :], px_raw[:, c, :], px_hi[:, c, :].bitcast(F32), sub).then_inc(px_lo_ready, 1)
            dve.wait_ge(att_hi_ready, 1)
            tt(a0[:, 1, :], a0_raw[:], a0[:, 0, :].bitcast(F32), sub).then_inc(att_lo_ready, 1)
            dve.wait_ge(start_in, 16)
            dve.wait_ge(h_blank, 1)

            def add_start(k):
                dve.wait_ge(embed_done, k + 1)
                tt(bank_of(h, k), bank_sums(k), bank_of(start_rows, k), add).then_inc(h_ready, 1)

            norm(0, add_start)
            feature_lo(0)
            attention(0)

            norm(1, add_output(0))
            feature_lo(1)

            def shifted(raw, experts, dst, bias, sem_):
                for lo, hi, m in ((0, 4, P), (4, 5, LAST)):
                    tt(dst[0:m, lo:hi, 0:experts], raw[0:m, lo * experts:hi * experts].rearrange("p (t e) -> p t e", e=experts),
                       bias[0:m].unsqueeze(1).broadcast_to([m, hi - lo, experts]), add).then_inc(sem_, 1)

            def first_ones(scores, picks, left, count, ready, ready_at, tops, picked, lefts):
                dve.wait_ge(ready, ready_at)
                for t in range(TILES):
                    dve.max(top8[:, t, :], scores[:, t, :]).then_inc(tops, 1)
                dve.wait_ge(tops, TILES)
                dve.tensor_copy(picks[:, :, 0:count], top8[:, :, 0:count]).then_inc(picked, 1)
                dve.wait_ge(picked, 1)
                for t in range(TILES):
                    dve.match_replace(left[:, t, :], picks[:, t, :], scores[:, t, :], TAKEN).then_inc(lefts, 1)
                dve.wait_ge(lefts, TILES)

            def choose():
                dve.wait_ge(gate0_done, 1)
                dve.wait_ge(late_in, 16)
                shifted(ps[:, 7, :], EXPERTS0, s0, cut(cl, LATE_AT, "gate_b"), s0_raw)
                dve.wait_ge(s0_raw, 2)
                tt(s0[:, :, 0:EXPERTS0], s0[:, :, 0:EXPERTS0],
                   cut(cl, LATE_AT, "center").unsqueeze(1).broadcast_to([P, TILES, EXPERTS0]), sub).then_inc(s0_ready, 1)
                first_ones(s0, pick0, s0_left, 1, s0_ready, 1, top0_ready, pick0_ready, left0_ready)
                tt(chosen[:], s0_left[:, :, 0:EXPERTS0], s0[:, :, 0:EXPERTS0], ALU.not_equal).then_inc(chosen_ready, 1)

            def hidden0_hi(u):
                dve.wait_ge(hid0_ready, u + 1)
                if u >= 4:
                    dve.wait_ge(down0_done, u - 3)
                dve.tensor_copy(hid0_hi[:, u % 4, :], hid0[:, u % 2, :]).then_inc(hid0_hi_ready, 1)

            def hidden0_lo(u):
                dve.wait_ge(hid0_hi_ready, u + 1)
                tt(hid0_lo[:, u % 4, :], hid0[:, u % 2, :], hid0_hi[:, u % 4, :].bitcast(F32), sub).then_inc(hid0_lo_ready, 1)

            b2 = cut(cl, LATE_AT, "b2").rearrange("p (e c) -> p e c", c=EMBED)

            def add_bias(e):
                dve.wait_ge(chosen_ready, 1)
                dve.wait_ge(h_biased, 1)
                for t in range(TILES):
                    m = rows_of(t)
                    if e:
                        dve.wait_ge(y0_added, TILES * (e - 1) + t + 1)
                    dve.scalar_tensor_tensor(out=h[0:m, t, :], in0=b2[0:m, e, :], scalar=chosen[0:m, t, e:e + 1],
                                             in1=h[0:m, t, :], op0=mult, op1=add).then_inc(b2_added, 1)

            def add_expert(e, t, signal):
                m = rows_of(t)
                dve.wait_ge(b2_added, TILES * e + t + 1)
                dve.scalar_tensor_tensor(out=h[0:m, t, :], in0=token_out(t), scalar=chosen[0:m, t, e:e + 1],
                                         in1=h[0:m, t, :], op0=mult, op1=add).then_inc(signal, 1)

            for u in range(EXPERTS0 * CHUNKS0):
                e, c = divmod(u, CHUNKS0)
                hidden0_hi(u)
                if c == 1 and e:
                    dve.wait_ge(down0_done, CHUNKS0 * e)
                    for t in range(TILES):
                        add_expert(e - 1, t, y0_added)
                hidden0_lo(u)
                if u == 1:
                    choose()
                if c == 3:
                    add_bias(e)

            def add_last_expert(k):
                if k < 2:
                    dve.wait_ge(sums_done, k + 1)
                    add_expert(EXPERTS0 - 1, 2 * k, last_added)
                    add_expert(EXPERTS0 - 1, 2 * k + 1, h_ready)
                else:
                    dve.wait_ge(down0_done, EXPERTS0 * CHUNKS0)
                    add_expert(EXPERTS0 - 1, TILES - 1, h_ready)

            norm(2, add_last_expert)
            feature_lo(2)
            attention(1)

            norm(3, add_output(1))
            feature_lo(3)
            b1 = cut(cl, LATE_AT, "pair_b1")
            dve.tensor_scalar(lin_b1[:], b1, 1.0, None, add).then_inc(lin_b1_ready, 1)

            def find_gates():
                dve.wait_ge(gate1_done, 1)
                shifted(ps[:, 7, :], EXPERTS1, s1, cut(cl, LATE_AT, "gate1_b"), s1_ready)
                first_ones(s1, pick1, s1_left, TOP, s1_ready, 2, top1_ready, pick1_ready, left1_ready)
                tt(among[:], s1_left[:, :, 0:EXPERTS1], s1[:, :, 0:EXPERTS1], ALU.not_equal).then_inc(among_ready, 1)
                tt(gate[:], s1[:, :, 0:EXPERTS1], top8[:, :, 0:1].broadcast_to([P, TILES, EXPERTS1]), sub).then_inc(gap_ready, 1)
                dve.wait_ge(exp_ready, 1)
                dve.wait_ge(among_ready, 1)
                tt(gate[:], gate[:], among[:], mult).then_inc(weigh_ready, 1)
                dve.wait_ge(weigh_ready, 1)
                dve.tensor_reduce(gate_sum[:], gate[:], AX_X, add).then_inc(gsum_ready, 1)
                dve.wait_ge(gsum_ready, 1)
                dve.reciprocal(gate_sum[:], gate_sum[:]).then_inc(grec_ready, 1)
                dve.wait_ge(grec_ready, 1)
                tt(gate[:], gate[:], gate_sum[:].unsqueeze(2).broadcast_to([P, TILES, EXPERTS1]), mult).then_inc(gate_ready, 1)

            def gates_lo():
                dve.wait_ge(gt_hi, 1)
                tt(gate_t[32:32 + EXPERTS1, 0:4 * P], ps[0:EXPERTS1, 0, 0:4 * P], gate_t[0:EXPERTS1, 0:4 * P].bitcast(F32), sub
                   ).then_inc(gt_lo, 1)
                dve.wait_ge(gt_hi, 2)
                tt(gate_t[32:32 + EXPERTS1, 4 * P:], ps[0:EXPERTS1, 1, 0:LAST], gate_t[0:EXPERTS1, 4 * P:].bitcast(F32), sub
                   ).then_inc(gt_lo, 1)

            def clip(slot, count):
                dve.wait_ge(lin_read, count)
                part = lin[:, slot % 2, :]
                dve.tensor_scalar(part, part, LIMIT + 1.0, 1.0 - LIMIT, ALU.min, ALU.max).then_inc(lin_ready, 1)

            def hidden(slot, count):
                clip(slot, count)
                dve.wait_ge(act1_ready, count)
                dve.wait_ge(lin_ready, count)
                tt(prod[:], lin[:, slot % 2, :], act1[:, slot % 2, :], mult).then_inc(prod_ready, 1)
                dve.wait_ge(prod_ready, count)

            def weigh(slot, pair):
                q, u = divmod(slot, UNITS)
                dve.wait_ge(bc_ready, pair * 4 + (2 if u == 0 else 4))
                tt(hid1[:, slot % 2, :], prod[:], gate_bc[:, (0, 1, 2 + q)[u], :], mult).then_inc(hid1_ready, 1)

            def hidden_lo(slot, count):
                dve.wait_ge(hid1_hi_ready, count)
                tt(hid1_lo[:, slot, :], hid1[:, slot % 2, :], hid1_hi[:, slot, :].bitcast(F32), sub).then_inc(hid1_lo_ready, 1)

            def two_pairs(i):
                first = isinstance(i, int)
                for slot in range(2 * UNITS):
                    q, u = divmod(slot, UNITS)
                    unit = i * (2 * UNITS) + slot
                    at = q * 2 * UNITS + u
                    if not (first and slot < 2):
                        dve.wait_ge(act1_ready, unit - 1)
                    dve.wait_ge(glu_done, unit + 1)
                    column = b1[:, at:at + 1] if first else cl[:, bass.ds(i * (4 * UNITS) + (LATE_AT["pair_b1"][0] + at), 1)]
                    dve.tensor_scalar(halves(glu[:, slot % 2, :]), ps[:, 3:5, 0:HALF], column, LIMIT, add, ALU.min
                                      ).then_inc(glu_ready, 1)
                    earlier = (slot - 1) % (2 * UNITS)
                    if first and slot == 0:
                        find_gates()
                    elif first and slot == 1:
                        gates_lo()
                        hidden(0, 1)
                    elif first and slot == 2:
                        weigh(0, 0)
                        hidden(1, 2)
                        weigh(1, 0)
                        hidden_lo(0, 1)
                    else:
                        hidden_lo((slot - 2) % (2 * UNITS), unit - 1)
                        hidden(earlier, unit)
                        weigh(earlier, i * 2 + (slot - 1) // UNITS)

            two_pairs(0)
            with dve.Fori(1, PAIRS // 2) as i:
                two_pairs(i)
            units, slot = UNITS * PAIRS, 2 * UNITS - 1
            parts = [slice(0, HALF), slice(HALF, TOKENS)]
            clip(slot, units)
            dve.wait_ge(act1_ready, units)
            dve.wait_ge(lin_ready, units)
            for cols in parts:
                tt(prod[:, cols], lin[:, 1, cols], act1[:, 1, cols], mult).then_inc(last_prod, 1)
            dve.wait_ge(bc_ready, 4 * PAIRS)
            for hf, cols in enumerate(parts):
                dve.wait_ge(last_prod, hf + 1)
                tt(hid1[:, 1, cols], prod[:, cols], gate_bc[:, 3, cols], mult).then_inc(last_hid, 1)
            hidden_lo(slot - 1, units - 1)
            for hf, cols in enumerate(parts):
                dve.wait_ge(last_hi, hf + 1)
                tt(hid1_lo[:, slot, cols], hid1[:, 1, cols], hid1_hi[:, slot, cols].bitcast(F32), sub).then_inc(last_lo, 1)
            dve.wait_ge(h_biased, 3)
            for k in range(3):
                if k < 2:
                    dve.wait_ge(sums_done, 2 + k + 1)
                else:
                    dve.wait_ge(down1_done, UNITS * PAIRS)
                tt(bank_of(n, k), bank_sums(k), bank_of(h, k), add).then_inc(result_ready, 1)


TURNED = [(3, 0, 3 * P), (5, 0, 3 * P), (4, 3 * P, TOKENS), (6, 3 * P, TOKENS)]
OUT_BANKS = [(7, 0), (1, 2)]
BUSY_AT_START = 6
BUSY = [12, 5, 9, 8]
BUSY_BEFORE_OUTPUTS = 4
W_PARTS = [slice(0, 1), slice(1, PATCH_CHUNKS)]
PARTS = [(0, 2), (2, 4), (4, TILES)]
KEYS_FIRST = [HEADS_A - 2, HEADS_A - 2]
GATE_ROWS = 32 + EXPERTS1


def kernel(x, cls_tok, L0_tok_W_proj, L0_tok_b_proj, L0_attn_w_qkv, L0_attn_b_qkv, L0_attn_w_proj,
           L0_attn_b_proj, L0_ffn_gate_w, L0_ffn_gate_b, L0_ffn_gate_center, L0_ffn_w1, L0_ffn_b1,
           L0_ffn_w2, L0_ffn_b2, L1_attn_w_qkv, L1_attn_w_proj, L1_attn_b_proj, L1_ffn_scale,
           L1_ffn_gate_w, L1_ffn_gate_b, L1_ffn_w1, L1_ffn_b1, L1_ffn_w2, L1_ffn_b2):
    import numpy as np
    import concourse.bacc as bacc
    from concourse.bass_utils import run_bass_kernel_spmd

    f32 = np.float32
    arr = {k: np.asarray(v) for k, v in locals().items() if k.startswith("L")}

    def chunked(w):
        return np.stack([w[:P], np.concatenate([w[P:], w[P:]])], axis=1)

    def rows(v):
        return np.broadcast_to(v.reshape(1, -1), (P, v.size))

    px = np.asarray(x).reshape(IMAGES, CHANNELS, SIDE, PATCH, SIDE, PATCH).transpose(1, 3, 5, 0, 2, 4)
    px = px.reshape(PATCH_CHUNKS * P, IMAGES, SEQ - 1)
    px = np.concatenate([np.zeros((PATCH_CHUNKS * P, IMAGES, 1), f32), px], axis=2)
    px = px.reshape(PATCH_CHUNKS, P, TOKENS)
    w_embed = arr["L0_tok_W_proj"].T.reshape(PATCH_CHUNKS, P, EMBED).transpose(1, 0, 2)
    start = np.concatenate([np.asarray(cls_tok).reshape(1, EMBED),
                            np.broadcast_to(arr["L0_tok_b_proj"], (SEQ - 1, EMBED))])
    start = np.concatenate([np.tile(start, (IMAGES, 1)), np.zeros((TILES * P - TOKENS, EMBED), f32)])
    start = start.reshape(TILES, P, EMBED).transpose(1, 0, 2)

    inv = f32(1.0) / f32(10000.0) ** (np.arange(0, HEAD, 2, dtype=f32) / f32(HEAD))
    angle = (np.arange(SEQ, dtype=f32)[:, None] * inv[None, :]).astype(f32)
    cos, sin = np.cos(angle), np.sin(angle)
    cos = np.concatenate([cos, cos], axis=1).T.astype(f32)
    sin = np.concatenate([-sin, sin], axis=1).T.astype(f32)
    cos, sin = (np.tile(t, (P // HEAD, HALF_IMAGES)) for t in (cos, sin))

    part = np.arange(P)
    head = (part[:, None] // HEAD == np.arange(HEADS_A)[None, :]).astype(f32)
    trio = (part[:, None] // SEQ == np.arange(TRIO * HEAD)[None, :] // HEAD).astype(f32)

    turn = np.arange(EMBED).reshape(HEADS, 2, HEAD // 2)[:, ::-1].reshape(-1)
    w_qkv, b_qkv = arr["L0_attn_w_qkv"], arr["L0_attn_b_qkv"]
    q0, k0 = np.arange(P), EMBED + np.arange(P)
    rest = np.concatenate([np.arange(P, EMBED), EMBED + np.arange(P, EMBED)])
    t2 = np.concatenate([turn, EMBED + turn])
    units0 = [k0, t2[k0], rest, t2[rest], q0, t2[q0]]
    v_cols = 2 * EMBED + np.arange(EMBED).reshape(TRIOS, TRIO, HEAD).transpose(1, 0, 2).reshape(-1)
    cols0 = np.concatenate(units0 + [v_cols])
    bqk = np.stack([b_qkv[u] for u in units0], axis=1)
    bv = b_qkv[2 * EMBED:]
    bv = np.stack([bv[:P], np.concatenate([bv[P:], bv[P:]])], axis=1)
    att0 = np.concatenate([chunked(w_qkv.T[:, cols0]).reshape(P, -1),
                           chunked(arr["L0_attn_w_proj"].T).reshape(P, -1)], axis=1)
    cols1 = np.concatenate([k0, rest, q0, v_cols])
    att1 = np.concatenate([chunked(arr["L1_attn_w_qkv"][:, cols1]).reshape(P, -1),
                           chunked(arr["L1_attn_w_proj"]).reshape(P, -1)], axis=1)

    early = np.concatenate([np.eye(P, dtype=f32), cos, sin, head, trio, bqk, bv,
                            rows(arr["L0_attn_b_proj"])], axis=1)

    ffn0 = np.stack([
        np.concatenate([chunked(arr["L0_ffn_w1"][e]).reshape(P, -1),
                        arr["L0_ffn_w2"][e].reshape(CHUNKS0, P, EMBED).transpose(1, 0, 2).reshape(P, -1)], axis=1)
        for e in range(EXPERTS0)])
    b1 = arr["L0_ffn_b1"].reshape(EXPERTS0 * CHUNKS0, P).T

    def paired(a, b):
        out_ = []
        for lo in (0, EMBED):
            out_ += [a[..., lo:lo + P], b[..., lo:lo + P], a[..., lo + P:lo + EMBED], b[..., lo + P:lo + EMBED]]
        return np.concatenate(out_, axis=-1)

    up, b1_1, w2_1 = arr["L1_ffn_w1"], arr["L1_ffn_b1"], arr["L1_ffn_w2"]
    ffn1, pair_b1, picks = [], [], []
    for q in range(PAIRS):
        a, b = 2 * q, 2 * q + 1
        pick = np.stack([(part % 32 == e) & (part < GATE_ROWS) for e in (a, b)], axis=1).astype(f32)
        picks.append(pick)
        down = np.concatenate([w2_1[a][:P], w2_1[b][:P], np.concatenate([w2_1[a][P:], w2_1[b][P:]])], axis=1)
        ffn1.append(np.concatenate([chunked(paired(up[a], up[b])).reshape(P, -1), pick, down], axis=1))
        pair_b1.append(paired(b1_1[a], b1_1[b]).reshape(2 * UNITS, P).T)
    ffn1 = np.stack(ffn1)

    late = np.concatenate([b1] + pair_b1 + [rows(arr[s]) for s in (
        "L0_ffn_gate_b", "L0_ffn_gate_center", "L1_ffn_gate_b", "L1_attn_b_proj", "L1_ffn_scale", "L0_ffn_b2")], axis=1)

    twice = np.zeros((P, EMBED), f32)
    twice[0:EXPERTS1] = arr["L1_ffn_b2"]
    twice[32:32 + EXPERTS1] = arr["L1_ffn_b2"]
    pos = np.arange(SEQ)
    far = np.zeros((P, HEADS * SEQ), f32)
    far[0:SEQ] = np.tile(np.where(np.abs(pos[:, None] - pos[None, :]) > WINDOW, f32(FAR), f32(0)), (1, HEADS))
    same = np.zeros((P, STACK), f32)
    same[0:SEQ] = np.tile(np.eye(SEQ, dtype=f32), (1, TRIO))
    mult = np.concatenate([chunked(arr["L0_ffn_gate_w"]).reshape(P, -1), chunked(arr["L1_ffn_gate_w"].T).reshape(P, -1),
                           twice, far, same, picks[0], np.zeros((P, 1), f32)], axis=1)

    given = dict(x=px, w_embed=w_embed, start=start, early=early, late=late, mult=mult, att0=att0, att1=att1, ffn0=ffn0, ffn1=ffn1)
    given = {k: np.ascontiguousarray(v) for k, v in given.items()}
    nc = bacc.Bacc("TRN2", target_bir_lowering=False, num_devices=1)
    args = {k: nc.dram_tensor(f"in_{k}", v.shape, F32, kind="ExternalInput").ap() for k, v in given.items()}
    out = nc.dram_tensor("out_0", (TOKENS, EMBED), F32, kind="ExternalOutput").ap()
    v_dram = nc.dram_tensor("values_by_rows", (TOKENS, EMBED), F32, kind="Internal").ap()
    vit_tower(nc, v_dram=v_dram, out=out, **args)
    r = run_bass_kernel_spmd(nc, [{f"in_{k}": v for k, v in given.items()}], core_ids=[0])
    return r.results[0]["out_0"].reshape(IMAGES, SEQ, EMBED)
```
